# Optimizing a Trainium2 kernel written in Bass

```python
import numpy as np
import jax
import jax.numpy as jnp

def _softmax(x, axis=-1):
    return jax.nn.softmax(x, axis=axis)

def _gelu(x):
    return jax.nn.gelu(x, approximate=True)

def _silu(x):
    return jax.nn.silu(x)

def _sigmoid(x):
    return jax.nn.sigmoid(x)

def _layernorm(x, axis=-1, eps=1e-05):
    m = jnp.mean(x, axis=axis, keepdims=True)
    v = jnp.var(x, axis=axis, keepdims=True)
    return (x - m) / jnp.sqrt(v + eps)

def _scatter_add(tgt, idx, src, axis=0):
    return tgt.at[idx].add(src)

def _segment_sum(src, seg, n):
    return jax.ops.segment_sum(src, seg, n)
kernel_name = 'mk_flamingo_gated_d2_seqx_r4_80f387'

def setup_inputs(seed: int=0):
    np.random.seed(seed)
    _w = jnp.asarray

    def _rec_inputs():
        import jax
        import jax.numpy as jnp
        _rk = jax.random.key(seed)
        x = -0.000929 + 1 * jax.random.normal(jax.random.fold_in(_rk, 1), (8, 112, 512), jnp.float32)
        _lenS = 112 - jax.random.randint(jax.random.fold_in(_rk, 7), (8,), 0, max(1, 112 // 4) + 1, jnp.int32)
        _lenS2 = 375 - jax.random.randint(jax.random.fold_in(_rk, 8), (8,), 0, max(1, 375 // 4) + 1, jnp.int32)
        _ctx_2048P = jax.random.normal(jax.random.fold_in(_rk, 11), (8, 16, 512), jnp.float32)
        _ctx_2048c = jax.random.dirichlet(jax.random.fold_in(_rk, 511), 0.3 * jnp.ones((16,), jnp.float32), (8, 375))
        _ctx_2048t = jnp.einsum('bsk,bkd->bsd', _ctx_2048c, _ctx_2048P)
        _ctx_2048t = _ctx_2048t * jax.lax.rsqrt(jnp.mean(jnp.square(_ctx_2048t)) + 1e-12) * 0.953939
        ctx_2048 = 2.81802e-05 + 1.00001 * (_ctx_2048t + 0.3 * jax.random.normal(jax.random.fold_in(_rk, 611), (8, 375, 512), jnp.float32))
        _g = jax.random.normal(jax.random.fold_in(_rk, 9001), (2, 2), jnp.float32)
        _g = jnp.sign(_g) * jnp.maximum(jnp.abs(_g), 1.0) + (_g == 0) * 1.0
        g_xattn = _g[0]
        g_ffn = _g[1]
        return (x, ctx_2048, g_xattn, g_ffn)
    x, ctx_2048, g_xattn, g_ffn = _rec_inputs()

    def _L0_xattn_setup():
        import jax, jax.numpy as jnp
        import numpy as np
        from jax import lax
        LN_EPS = 1e-05
        key = jax.random.key(seed)
        ks = jax.random.split(key, 8)
        B, S, T, D = (4, 128, 512, 512)
        scale = 0.02
        return {'Z': jax.random.normal(ks[0], (B, S, D), dtype=jnp.float32), 'kv': jax.random.normal(ks[1], (B, T, D), dtype=jnp.float32), 'decay': jnp.float32(0.9), 'W_in': jax.random.normal(ks[2], (D, D), dtype=jnp.float32) * scale, 'b_in': jnp.zeros((D,), dtype=jnp.float32), 'W_out': jax.random.normal(ks[3], (D, D), dtype=jnp.float32) * scale, 'b_out': jnp.zeros((D,), dtype=jnp.float32), 'gamma': jnp.ones((D,), dtype=jnp.float32), 'beta': jnp.zeros((D,), dtype=jnp.float32)}
    _L0_xattn_all = _L0_xattn_setup()
    _L0_xattn_in = {k: v for k, v in _L0_xattn_all.items() if k in ('decay', 'W_in', 'b_in', 'W_out', 'b_out', 'gamma', 'beta')}
    del _L0_xattn_all

    def _L0_ffn_setup():
        import jax, jax.numpy as jnp
        import numpy as np
        TOP_K = 4
        key = jax.random.key(seed)
        ks = jax.random.split(key, 5)
        H, I, E = (512, 192, 32)
        s = 0.02
        return {'hidden_states': jax.random.normal(ks[0], (1, 256, H), jnp.float32), 'router_w': jax.random.normal(ks[1], (E, H), jnp.float32) * s, 'gate_w': jax.random.normal(ks[2], (E, I, H), jnp.float32) * s, 'up_w': jax.random.normal(ks[3], (E, I, H), jnp.float32) * s, 'down_w': jax.random.normal(ks[4], (E, H, I), jnp.float32) * s}
    _L0_ffn_all = _L0_ffn_setup()
    _L0_ffn_in = {k: v for k, v in _L0_ffn_all.items() if k in ('router_w', 'gate_w', 'up_w', 'down_w')}
    del _L0_ffn_all

    def _L1_xattn_setup():
        import jax, jax.numpy as jnp
        import numpy as np
        FEAT = 512
        G = 16
        DG = FEAT // G
        key = jax.random.key(seed)
        ks = jax.random.split(key, 8)
        bs, N1, N2 = (2, 1024, 128)
        s = 1.0 / np.sqrt(FEAT)
        return {'ref_feat': jax.random.normal(ks[0], (bs, N1, FEAT), jnp.float32), 'sup_feat': jax.random.normal(ks[1], (bs, N2, FEAT), jnp.float32), 'W_fc': jax.random.normal(ks[2], (FEAT, FEAT), jnp.float32) * s, 'b_fc': jnp.zeros((FEAT,), jnp.float32), 'W_q': jax.random.normal(ks[3], (FEAT, FEAT), jnp.float32) * s, 'b_q': jnp.zeros((FEAT,), jnp.float32), 'W_k': jax.random.normal(ks[4], (FEAT, FEAT), jnp.float32) * s, 'b_k': jnp.zeros((FEAT,), jnp.float32), 'W_v': jax.random.normal(ks[5], (FEAT, FEAT, 1, 1), jnp.float32) * 0.01, 'b_v': jnp.zeros((FEAT,), jnp.float32)}
    _L1_xattn_all = _L1_xattn_setup()
    _L1_xattn_in = {k: v for k, v in _L1_xattn_all.items() if k in ('W_fc', 'b_fc', 'W_q', 'b_q', 'W_k', 'b_k', 'W_v', 'b_v')}
    del _L1_xattn_all

    def _L1_ffn_setup():
        import jax, jax.numpy as jnp
        import numpy as np
        DIM = 512
        HIDDEN = 2048
        NUM_EXPERTS = 2
        BATCH, SEQ = (4, 256)
        key = jax.random.key(seed)
        k1, k2, k3, k4 = jax.random.split(key, 4)
        x = jax.random.normal(k1, (BATCH, SEQ, DIM), dtype=jnp.float32)
        w_router = jax.random.normal(k2, (NUM_EXPERTS, DIM), dtype=jnp.float32) * (1.0 / np.sqrt(DIM))
        w_fc = jax.random.normal(k3, (NUM_EXPERTS, HIDDEN, DIM), dtype=jnp.float32) * (1.0 / np.sqrt(DIM))
        w_proj = jax.random.normal(k4, (NUM_EXPERTS, DIM, HIDDEN), dtype=jnp.float32) * (1.0 / np.sqrt(HIDDEN))
        return {'x': x, 'w_router': w_router, 'w_fc': w_fc, 'w_proj': w_proj}
    _L1_ffn_all = _L1_ffn_setup()
    _L1_ffn_in = {k: v for k, v in _L1_ffn_all.items() if k in ('w_router', 'w_fc', 'w_proj')}
    del _L1_ffn_all
    return {'x': x, 'ctx_2048': ctx_2048, 'g_xattn': g_xattn, 'g_ffn': g_ffn, 'L0_xattn_decay': _L0_xattn_in['decay'], 'L0_xattn_W_in': _L0_xattn_in['W_in'], 'L0_xattn_b_in': _L0_xattn_in['b_in'], 'L0_xattn_W_out': _L0_xattn_in['W_out'], 'L0_xattn_b_out': _L0_xattn_in['b_out'], 'L0_xattn_gamma': _L0_xattn_in['gamma'], 'L0_xattn_beta': _L0_xattn_in['beta'], 'L0_ffn_router_w': _L0_ffn_in['router_w'], 'L0_ffn_gate_w': _L0_ffn_in['gate_w'], 'L0_ffn_up_w': _L0_ffn_in['up_w'], 'L0_ffn_down_w': _L0_ffn_in['down_w'], 'L1_xattn_W_fc': _L1_xattn_in['W_fc'], 'L1_xattn_b_fc': _L1_xattn_in['b_fc'], 'L1_xattn_W_q': _L1_xattn_in['W_q'], 'L1_xattn_b_q': _L1_xattn_in['b_q'], 'L1_xattn_W_k': _L1_xattn_in['W_k'], 'L1_xattn_b_k': _L1_xattn_in['b_k'], 'L1_xattn_W_v': _L1_xattn_in['W_v'], 'L1_xattn_b_v': _L1_xattn_in['b_v'], 'L1_ffn_w_router': _L1_ffn_in['w_router'], 'L1_ffn_w_fc': _L1_ffn_in['w_fc'], 'L1_ffn_w_proj': _L1_ffn_in['w_proj']}

def reference(x, ctx_2048, g_xattn, g_ffn, L0_xattn_decay, L0_xattn_W_in, L0_xattn_b_in, L0_xattn_W_out, L0_xattn_b_out, L0_xattn_gamma, L0_xattn_beta, L0_ffn_router_w, L0_ffn_gate_w, L0_ffn_up_w, L0_ffn_down_w, L1_xattn_W_fc, L1_xattn_b_fc, L1_xattn_W_q, L1_xattn_b_q, L1_xattn_W_k, L1_xattn_b_k, L1_xattn_W_v, L1_xattn_b_v, L1_ffn_w_router, L1_ffn_w_fc, L1_ffn_w_proj):
    import jax
    import jax.numpy as jnp

    def _L0_xattn_ref(Z, kv, decay, W_in, b_in, W_out, b_out, gamma, beta):
        import jax, jax.numpy as jnp
        import numpy as np
        from jax import lax
        LN_EPS = 1e-05
        B, T, D = kv.shape
        K = jax.nn.sigmoid(decay)
        x = jnp.einsum('btd,ed->bte', kv, W_in) + b_in

        def scan_fn(s, xt):
            s = K * s + xt
            return (s, s)
        s0 = jnp.zeros((B, D), dtype=kv.dtype)
        _, states = lax.scan(scan_fn, s0, jnp.swapaxes(x, 0, 1))
        states = jnp.swapaxes(states, 0, 1)
        proj = jnp.einsum('btd,ed->bte', states, W_out) + b_out
        summary = jnp.mean(proj, axis=1, keepdims=True)
        y = Z + summary
        mu = jnp.mean(y, axis=-1, keepdims=True)
        var = jnp.mean((y - mu) ** 2, axis=-1, keepdims=True)
        return (y - mu) / jnp.sqrt(var + LN_EPS) * gamma + beta

    def _L0_ffn_ref(hidden_states, router_w, gate_w, up_w, down_w):
        import jax, jax.numpy as jnp
        import numpy as np
        TOP_K = 4
        B, S, H = hidden_states.shape
        E = router_w.shape[0]
        x = hidden_states.reshape(-1, H)
        logits = x @ router_w.T
        probs = jax.nn.softmax(logits.astype(jnp.float32), axis=-1)
        rw, sel = jax.lax.top_k(probs, TOP_K)
        rw = rw / jnp.sum(rw, axis=-1, keepdims=True)
        rw = rw.astype(x.dtype)

        def body(acc, expert):
            gw, uw, dw, e = expert
            w_tok = jnp.sum(jnp.where(sel == e, rw, 0.0), axis=-1)
            h = jax.nn.silu(x @ gw.T) * (x @ uw.T)
            y = h @ dw.T
            return (acc + w_tok[:, None] * y, None)
        acc0 = jnp.zeros_like(x)
        out, _ = jax.lax.scan(body, acc0, (gate_w, up_w, down_w, jnp.arange(E)))
        return out.reshape(B, S, H)

    def _L1_xattn_ref(ref_feat, sup_feat, W_fc, b_fc, W_q, b_q, W_k, b_k, W_v, b_v):
        import jax, jax.numpy as jnp
        import numpy as np
        FEAT = 512
        G = 16
        DG = FEAT // G
        bs, N1, _ = ref_feat.shape
        sup = jax.nn.relu(sup_feat @ W_fc.T + b_fc)
        ref = jax.nn.relu(ref_feat @ W_fc.T + b_fc)
        q = (ref @ W_q.T + b_q).reshape(bs, N1, G, DG)
        k = (sup @ W_k.T + b_k).reshape(bs, -1, G, DG)
        aff = jnp.einsum('bqhd,bkhd->bhqk', q, k) * (1.0 / np.sqrt(DG))
        p = jax.nn.softmax(aff, axis=-1)
        out_h = jnp.einsum('bhqk,bkf->bhqf', p, sup)
        Wv = W_v.reshape(G, DG, FEAT)
        attn = jnp.einsum('bhqf,hjf->bqhj', out_h, Wv).reshape(bs, N1, FEAT) + b_v
        return ref + attn

    def _L1_ffn_ref(x, w_router, w_fc, w_proj):
        import jax, jax.numpy as jnp
        import numpy as np
        DIM = 512
        HIDDEN = 2048
        NUM_EXPERTS = 2
        BATCH, SEQ = (4, 256)
        bsz, seq, dim = x.shape
        num_experts = w_router.shape[0]
        x_flat = x.reshape(-1, dim)
        logits = x_flat @ w_router.T
        probs = jax.nn.softmax(logits, axis=-1)
        top_idx = jnp.argmax(probs, axis=-1)
        top_weight = jnp.take_along_axis(probs, top_idx[:, None], axis=1)[:, 0]
        h = jnp.einsum('nd,ehd->enh', x_flat, w_fc)
        a = jnp.square(jnp.where(h >= 0, h, 0.5 * h))
        expert_out = jnp.einsum('enh,edh->end', a, w_proj)
        mask = (top_idx[None, :] == jnp.arange(num_experts)[:, None]).astype(x.dtype)
        out = jnp.einsum('end,en->nd', expert_out, mask * top_weight[None, :])
        return out.reshape(bsz, seq, dim)
    x = x + jnp.tanh(g_xattn[0]) * _L0_xattn_ref(_layernorm(x, axis=-1), ctx_2048, L0_xattn_decay, L0_xattn_W_in, L0_xattn_b_in, L0_xattn_W_out, L0_xattn_b_out, L0_xattn_gamma, L0_xattn_beta)
    x = x + jnp.tanh(g_ffn[0]) * _L0_ffn_ref(_layernorm(x, axis=-1), L0_ffn_router_w, L0_ffn_gate_w, L0_ffn_up_w, L0_ffn_down_w)
    x = x + jnp.tanh(g_xattn[1]) * _L1_xattn_ref(_layernorm(x, axis=-1), ctx_2048, L1_xattn_W_fc, L1_xattn_b_fc, L1_xattn_W_q, L1_xattn_b_q, L1_xattn_W_k, L1_xattn_b_k, L1_xattn_W_v, L1_xattn_b_v)
    x = x + jnp.tanh(g_ffn[1]) * _L1_ffn_ref(_layernorm(x, axis=-1), L1_ffn_w_router, L1_ffn_w_fc, L1_ffn_w_proj)
    return x

_drawn_inputs = setup_inputs


def setup_inputs(seed=0):
    import zlib

    import numpy as np

    out = dict(_drawn_inputs(seed))
    spreads = {'g_ffn': (-1.0, 0.536),
     'L0_xattn_b_in': (0.0, 0.1),
     'L0_xattn_b_out': (0.0, 0.1),
     'L0_xattn_gamma': (1.0, 0.2),
     'L0_xattn_beta': (0.0, 0.1),
     'L1_xattn_b_fc': (0.0, 0.1),
     'L1_xattn_b_q': (0.0, 0.8),
     'L1_xattn_b_k': (0.0, 0.8),
     'L1_xattn_b_v': (0.0, 0.1)}
    factors = {'L0_ffn_router_w': 3.419,
     'L0_ffn_gate_w': 4.024,
     'L0_ffn_up_w': 3.985,
     'L0_ffn_down_w': 3.477,
     'L1_xattn_W_q': 5.987,
     'L1_xattn_W_k': 5.965}
    for name, (base, spread) in spreads.items():
        noise = np.random.default_rng([zlib.crc32(name.encode()), seed]).standard_normal(out[name].shape)
        drawn = base * np.exp(spread * noise) if base else spread * noise
        out[name] = jnp.asarray(drawn.astype(out[name].dtype))
    for name, factor in factors.items():
        out[name] = (out[name] * factor).astype(out[name].dtype)
    return out
```

```python
from contextlib import ExitStack

import numpy as np

import concourse.bass as bass
from concourse import mybir

F32 = mybir.dt.float32
BF16 = mybir.dt.bfloat16
I32 = mybir.dt.int32
U32 = mybir.dt.uint32
ACT = mybir.ActivationFunctionType
ALU = mybir.AluOpType
AX = mybir.AxisListType

B, S, T, D = 8, 112, 375, 512
N = B * S
P = 128
KD = D // P
E0, TOP, I0 = 32, 4, 192
E1, HID = 2, 2048
H, DG = 16, 32
TC = T // 3
EPS = 1e-5
SCALE = 1.0 / float(np.sqrt(DG))
NB0 = (N * TOP + E0 * (P - 1)) // P
NB0 += NB0 % 2
NB1 = (N + E1 * (P - 1)) // P
IH = I0 // 2
CH = 512
NCH = HID // CH
GU = KD * 2 * I0
RW0 = GU + 2 * D
NR0 = 4
RW1 = E1 * 2 * KD * CH

C_BIN, C_BFC, C_BQ, C_BK, C_GX, C_GF, C_DEC, C_PID = 0, 4, 8, 12, 16, 18, 20, 21
NCOL = 24

A_X = 0
A_K = A_X + B * D
A_V = A_K + B * KD * T
A_W = A_V + 3 * B * D
A_WFC, A_WQ, A_WK, A_WV = (A_W + i * KD * D for i in range(4))
A_SUP = A_WV + KD * D
A_C = A_SUP + KD * T
A_Z = A_C + 2 * KD * D
A_HT = A_Z + B * D
A_FREE = A_HT + KD * N
A_END = A_FREE + RW0
A_RING = [A_FREE, A_C, A_WK, A_WK + RW0]
A_CST = A_C + 3600
A_G0 = A_WK
A_REF = A_WK
A_QT = A_C
A_CH = [A_W, A_K]
A_XT1 = A_K + RW1
A_Y1 = A_XT1 + NB1 * D
A_L1 = A_Y1 + NB1 * D


def build(nc, x_in, ctx_in, wfc_in, wq_in, wk_in, wv_in, win_in, wout_in, cols_in, gamma_in, beta_in,
          bout_in, bv_in, rw0_in, rw1_in, gu_in, dn_in, ch_in, ident_in, sel_in, iota_in, tri_in, ones_in, out):
    h0_dram = nc.dram_tensor("h0_rows", [N, D], F32, kind="Internal").ap()
    y0_dram = nc.dram_tensor("y0_slots", [NB0 * P, D], F32, kind="Internal").ap()
    h1_dram = nc.dram_tensor("h1_rows", [N, D], F32, kind="Internal").ap()
    y1_dram = nc.dram_tensor("y1_slots", [NB1 * P, D], F32, kind="Internal").ap()
    out_rows = out.rearrange("b s d -> s b d")

    with ExitStack() as ctx:
        def sb(name, shape, dt=F32):
            return ctx.enter_context(nc.sbuf_tensor(name, shape, dt))

        def sem(name):
            return ctx.enter_context(nc.semaphore(name))

        arena = sb("arena", [P, A_END])

        def at(off, words, parts=P):
            return arena[0:parts, off:off + words]

        x = at(A_X, B * D, S).rearrange("p (b d) -> p b d", b=B)
        ctxk = at(A_K, B * KD * T).rearrange("p (b k t) -> p b k t", b=B, k=KD)
        vals = at(A_V, 3 * B * D, TC).rearrange("p (c d) -> p c d", d=D)
        wfc, wq, wk, wv = (at(a, KD * D).rearrange("p (k d) -> p k d", k=KD) for a in (A_WFC, A_WQ, A_WK, A_WV))
        sup = at(A_SUP, KD * T).rearrange("p (k t) -> p k t", k=KD)
        w_in = at(A_C, KD * D).rearrange("p (k d) -> p k d", k=KD)
        w_out = at(A_C + KD * D, KD * D).rearrange("p (k d) -> p k d", k=KD)
        z = at(A_Z, B * D, S).rearrange("p (b d) -> p b d", b=B)
        hT = at(A_HT, KD * N).rearrange("p (k n) -> p k n", k=KD)
        gamma = at(A_FREE, D, S)
        beta = at(A_FREE + D, D, S)
        bout = at(A_FREE + 2 * D, D, B)
        sel = at(A_FREE + 3 * D, B * S, B).rearrange("p (b s) -> p b s", b=B)
        bv = at(A_FREE, D, S)
        ones_row = at(A_HT, T)
        k_row = at(A_HT + T, T)
        r_row = at(A_HT + 2 * T, T)
        prod_rows = [at(A_HT + (3 + i) * T, T) for i in range(2)]
        summ = at(A_HT + 5 * T, D, B)
        lg0 = at(A_C + RW0, B * E0, S).rearrange("p (b e) -> p b e", b=B)
        lg1 = at(A_C + RW0, B * E1, S).rearrange("p (b e) -> p b e", b=B)
        iota = at(A_CST, P)
        tri = at(A_CST + P, S // 2, S).bitcast(BF16)
        ones_b = at(A_CST + P + S // 2, P // 2, S).bitcast(BF16)
        tile_no = at(A_CST + P + S // 2 + P // 2, B * TOP, S)

        ident = sb("ident", [P, P])
        cols = sb("cols", [P, NCOL])
        gates = sb("gates", [P, 8])
        rw0 = sb("rw0", [P, KD * E0])
        rw1 = sb("rw1", [P, KD * E1])
        stats = sb("stats", [S, B, 6])
        mv = sb("mv", [S, B, 2])
        veps = sb("veps", [S, B])
        mhalf = sb("mhalf", [S, B])
        rstd = sb("rstd", [S, B])
        uT = sb("uT", [P, KD, B])
        s1T = sb("s1T", [P, KD, B])
        bC = sb("bC", [P, KD])
        lidx = sb("lidx", [P, NB0], U32)
        slot_u = sb("slot_u", [S, B * TOP], U32)
        wt = sb("wt", [S, B * TOP])
        table = sb("table", [1, 96], I32)
        table2 = sb("table2", [1, 64], I32)
        idxb = sb("idxb", [P, 2], U32)
        nmx = sb("nmx", [S, 2, 4])
        psum_e = sb("psum_e", [S, 2, 4])
        rinv = sb("rinv", [S, 2, 4])
        ps = ctx.enter_context(nc.psum_tensor("ps", [P, 8, 512], F32))

        names = """ld_kv ld_ctx1 ld_ctx ld_x ld_sum ld_cst ld_small ld_bv gates_ready u_done kv_mm kv_ev
            ch_ready s1_mm s1_ready sum_mm sum_ready bc_mm y_added beta_ready bv_ready z_ready x_based veps_ready rstd_ready h_ready h_stored0
            h_stored1 tr_mm tr_ev lg_mm lg_ev ediff_ready eexp_ready ready_m rank_mm ready_r list_mm list_ready dve_done
            pool_done w_ready x0_landed x1_landed t_mm t_ev u_mm silu_done h_mul h_mm h_ev d_mm y_ev y0_stored y1_stored
            w0_landed w1_landed w2_landed w3_landed gath0 gath1 gath2 gath3 gath4 gath5 gath6 gath7 comb_done
            ref_mm ref_ev rt_mm rt_add qk0_landed qk1_landed s_mm mx_ready e_done pt_mm pt_ev pv_mm o_done
            c0_landed c1_landed t1_mm t1_ev u1_mm half_done l_done h1_mm h1_ev d1_mm y1_ev y1_done out_ready out_stored
            lidx_copied idx_seen""".split()
        sems = {n: sem(n) for n in names}
        q = type("Sems", (), sems)

        block = ctx.enter_context(nc.Block())

        def dispatch_views(E, C, NB):
            pairs = B * C
            off = [A_Z]

            def take(words, parts=S):
                a = off[0]
                off[0] += words
                assert off[0] <= A_FREE
                return at(a, words, parts)
            v = {}
            v["m8"] = take(B * 8).rearrange("p (b k) -> p b k", k=8)
            v["i8"] = take(B * 8).bitcast(U32).rearrange("p (b k) -> p b k", k=8)
            v["idf"] = take(pairs)
            v["oh"] = take(pairs * E // 2).bitcast(BF16)
            v["m"] = take(B * E // 2).bitcast(BF16)
            v["slot"] = take(B * E)
            v["pick"] = take(pairs * E)
            v["sk"] = take(pairs)
            v["ski"] = take(pairs).bitcast(I32)
            v["qi"] = take(pairs).bitcast(I32)
            v["ri"] = take(pairs).bitcast(I32)
            v["qf"] = take(pairs)
            v["rf"] = take(pairs)
            v["cnti"] = take(E, P).bitcast(I32)
            v["nb"] = take(E, P)
            v["cum"] = take(E, P)
            v["ones"] = take(E, P)
            v["base"] = take(E, P)
            v["eb"] = take(NB, P)
            v["la"] = take(NB, P)
            v["rm"] = take(pairs * P // 2).bitcast(BF16).rearrange("p (c r) -> p c r", r=P)
            v["qm"] = take(pairs * NB // 2).bitcast(BF16).rearrange("p (c j) -> p c j", j=NB)
            v["q2"] = take(pairs * NB).bitcast(BF16).rearrange("p (c a j) -> p c a j", a=2, j=NB)
            v["cmp"] = v["rm"].rearrange("p c r -> p (c r)")[0:1, 0:NB * E].rearrange("p (j e) -> p j e", e=E)
            v["cmp_ok"] = NB * E <= pairs * P
            return v

        disp0 = dispatch_views(E0, TOP, NB0)
        disp1 = dispatch_views(E1, 1, NB1)
        assert disp0["cmp_ok"] and disp1["cmp_ok"]

        def pair(off, words, parts=P):
            return [at(off + i * words, words, parts) for i in range(2)]
        xg = pair(A_Z, D)
        xT = [a.rearrange("p (k n) -> p k n", k=KD) for a in pair(A_Z + 2 * D, D)]
        sg = pair(A_Z + 4 * D, I0)
        hm = pair(A_Z + 4 * D + 2 * I0, I0)
        hmT = [a.rearrange("p (k n) -> p k n", k=2) for a in pair(A_Z + 4 * D + 4 * I0, 2 * P, IH)]
        yb = pair(A_Z + 4 * D + 4 * I0 + 4 * P, D)
        g0 = [at(A_G0 + i * D, D, S) for i in range(8)]
        ring = arena[:, :]

        A_AT = A_Z
        prob = [at(A_AT + i * 4 * T, 4 * T, S).rearrange("p (h t) -> p h t", h=4) for i in range(2)]
        pT = at(A_AT + 8 * T, 12 * S, TC).rearrange("p (c h s) -> p c h s", c=3, h=4)
        o_t = at(A_AT + 8 * T + 12 * S, 2 * P, S).rearrange("p (a n) -> p a n", a=2)
        A_KB = A_AT + 8 * T + 12 * S + 2 * P
        kb = [at(A_KB + i * KD * T, KD * T).rearrange("p (k t) -> p k t", k=KD) for i in range(2)]
        qb = [at(A_KB + 2 * KD * T + i * KD * S, KD * S).rearrange("p (k s) -> p k s", k=KD) for i in range(2)]
        assert A_KB + 2 * KD * T + 2 * KD * S <= A_END
        refT = at(A_REF, KD * N).rearrange("p (k n) -> p k n", k=KD)
        qT = at(A_QT, KD * N).rearrange("p (k n) -> p k n", k=KD)

        xT1 = at(A_XT1, NB1 * D).rearrange("p (j k n) -> p j k n", j=NB1, k=KD)
        y1 = at(A_Y1, NB1 * D).rearrange("p (j d) -> p j d", j=NB1)
        hf = pair(A_L1, CH)
        lk = pair(A_L1 + 2 * CH, CH)
        aT = [a.rearrange("p (k n) -> p k n", k=KD) for a in pair(A_L1 + 4 * CH, CH)]
        xg1 = [at(A_L1 + 6 * CH + i * D, D) for i in range(2)]
        g1 = [at(A_RING[0] - 8 * D + i * D, D, S) for i in range(8)]
        assert A_L1 + 6 * CH + 2 * D <= A_W

        gx0, gx1, gf0, gf1 = (gates[0:S, i:i + 1] for i in range(4))

        @block.sync
        def _(sp):
            def load(dst, src, s):
                sp.dma_start(dst, src).then_inc(s, 16)
            load(cols[:], cols_in, q.ld_kv)
            load(wfc, wfc_in.rearrange("p (k d) -> p k d", k=KD), q.ld_kv)
            load(ctxk[:, 0], ctx_in[0].rearrange("p (k t) -> p k t", k=KD), q.ld_kv)
            load(wk, wk_in.rearrange("p (k d) -> p k d", k=KD), q.ld_kv)
            load(wv, wv_in.rearrange("p (k d) -> p k d", k=KD), q.ld_kv)
            load(x, x_in.rearrange("p (b d) -> p b d", b=B), q.ld_x)
            load(ctxk[:, 1], ctx_in[1].rearrange("p (k t) -> p k t", k=KD), q.ld_ctx1)
            for b in range(2, B):
                load(ctxk[:, b], ctx_in[b].rearrange("p (k t) -> p k t", k=KD), q.ld_ctx)
            load(w_in, win_in.rearrange("p (k d) -> p k d", k=KD), q.ld_sum)
            load(w_out, wout_in.rearrange("p (k d) -> p k d", k=KD), q.ld_sum)
            load(gamma, gamma_in, q.ld_sum)
            load(beta, beta_in, q.ld_sum)
            load(bout, bout_in, q.ld_sum)
            load(sel, sel_in.rearrange("p (b s) -> p b s", b=B), q.ld_sum)
            load(ident[:], ident_in, q.ld_small)
            load(rw0[:], rw0_in, q.ld_small)
            load(rw1[:], rw1_in, q.ld_small)
            load(wq, wq_in.rearrange("p (k d) -> p k d", k=KD), q.ld_small)
            sp.wait_ge(q.sum_mm, 1)
            load(iota, iota_in[:, 0:P], q.ld_cst)
            load(tile_no, iota_in[0:S, P:P + B * TOP], q.ld_cst)
            load(tri, tri_in, q.ld_cst)
            load(ones_b, ones_in, q.ld_cst)
            for t in range(B):
                sp.wait_ge(q.h_ready, t + 1)
                sp.dma_start(h0_dram[t * S:(t + 1) * S, :], z[:, t]).then_inc(q.h_stored0, 16)

            landed = [q.w0_landed, q.w1_landed, q.w2_landed, q.w3_landed]

            def load_expert(e, slot):
                dst = at(A_RING[slot], GU)
                sp.dma_start(dst, gu_in[bass.ds(e, 1)].rearrange("e p n -> (e p) n")).then_inc(landed[slot], 16)
                dst = at(A_RING[slot] + GU, 2 * D, IH)
                sp.dma_start(dst, dn_in[bass.ds(e, 1)].rearrange("e p n -> (e p) n")).then_inc(landed[slot], 16)

            load_expert(0, 0)
            load_expert(1, 1)
            sp.wait_ge(q.kv_mm, 11 * B)
            load_expert(2, 2)
            load_expert(3, 3)
            sp.wait_ge(q.list_ready, 1)
            for e in range(NR0 - 1):
                sp.wait_ge(landed[e], 32)
                sp.sem_inc(q.w_ready, 1)
            with sp.Fori(0, E0 // NR0 - 1) as i:
                for slot in range(NR0):
                    ahead = (slot + NR0 - 1) % NR0
                    sp.wait_ge(landed[ahead], i * 32 + (32 if slot == 0 else 64))
                    sp.sem_inc(q.w_ready, 1)
                    done = sp.value_load(table[0:1, bass.ds(i * NR0 + (64 + slot), 1)], min_val=2, max_val=NB0 + 1)
                    sp.wait_ge(q.d_mm, done)
                    load_expert(i * NR0 + (NR0 + slot), slot)
            sp.wait_ge(landed[NR0 - 1], 32 * (E0 // NR0))
            sp.sem_inc(q.w_ready, 1)

            sp.wait_ge(q.d_mm, NB0 + 1)
            load(bv, bv_in, q.ld_bv)

            def load_chunk(c, slot, s):
                for a in range(4):
                    w = RW1 // 4
                    sp.dma_start(at(A_CH[slot] + a * w, w), ch_in[c, :, a * w:(a + 1) * w]).then_inc(s, 16)

            sp.wait_ge(q.ref_ev, 16)
            sp.wait_ge(q.rt_mm, B)
            sp.wait_ge(q.x_based, 2 * B)

            def stage_qk(b, par):
                s = (q.qk0_landed, q.qk1_landed)[par]
                sp.dma_start(kb[par], ctxk[:, bass.ds(b, 1)].rearrange("p b k t -> p (b k) t")).then_inc(s, 16)
                sp.dma_start(qb[par], qT[:, :, bass.ds(b * S, S)]).then_inc(s, 16)

            stage_qk(0, 0)
            stage_qk(1, 1)
            load_chunk(0, 0, q.c0_landed)
            with sp.Fori(1, B // 2) as i:
                for par in range(2):
                    sp.wait_ge(q.s_mm, i * 8 + (4 * par - 4))
                    stage_qk(i * 2 + par, par)
            sp.wait_ge(q.o_done, 4 * B)
            load_chunk(1, 1, q.c1_landed)
            for t in range(B):
                sp.wait_ge(q.h_ready, 2 * B + t + 1)
                sp.dma_start(h1_dram[t * S:(t + 1) * S, :], z[:, t]).then_inc(q.h_stored1, 16)
            chunk_landed = (q.c0_landed, q.c1_landed)
            for c in range(NCH):
                sp.wait_ge(chunk_landed[c % 2], 64 * (c // 2 + 1))
                sp.sem_inc(q.ch_ready, 1)
                if c >= 1 and c + 1 < NCH:
                    sp.wait_ge(q.d1_mm, NB1 * c)
                    load_chunk(c + 1, (c + 1) % 2, chunk_landed[(c + 1) % 2])
            for j in range(NB1):
                sp.wait_ge(q.y1_ev, NB1 * (NCH - 1) + j + 1)
                sp.dma_start(y1_dram[j * P:(j + 1) * P, :], y1[:, j]).then_inc(q.y1_done, 16)
            for t in range(B):
                sp.wait_ge(q.out_ready, t + 1)
                sp.dma_start(out_rows[:, t], x[:, t]).then_inc(q.out_stored, 16)
            sp.wait_ge(q.out_stored, 16 * B)

        @block.gpsimd
        def _(pool):
            pool.memset(mhalf[:], -0.5).then_inc(q.pool_done, 1)
            pool.wait_ge(q.pool_done, 1)

            def root(n):
                pool.wait_ge(q.veps_ready, n + 1)
                pool.tensor_tensor(rstd[:], veps[:], mhalf[:], ALU.pow).then_inc(q.rstd_ready, 1)

            root(0)
            pool.wait_ge(q.beta_ready, 1)
            for t in range(B):
                pool.tensor_tensor(x[:, t], x[:, t], beta, ALU.add).then_inc(q.x_based, 1)
            root(1)
            root(2)

            landed = (q.x0_landed, q.x1_landed)

            def token_column(j, par):
                pool.tensor_copy(idxb[:, par:par + 1], lidx[:, bass.ds(j, 1)]).then_inc(q.lidx_copied, 1)

            def gather(par, bufs, rows):
                pool.indirect_dma_start(out=bufs[par], out_offset=None, in_=rows,
                                        in_offset=bass.IndirectOffsetOnAxis(ap=idxb[:, par:par + 1], axis=0)
                                        ).then_inc(landed[par], 16)

            pool.wait_ge(q.list_ready, 1)
            pool.wait_ge(q.h_stored0, 16 * B)
            for par in range(2):
                token_column(par, par)
                pool.wait_ge(q.lidx_copied, par + 1)
                gather(par, xg, h0_dram)
            with pool.Fori(1, NB0 // 2) as i:
                for par in range(2):
                    pool.wait_ge(q.t_mm, i * 2 + (par - 1))
                    token_column(i * 2 + par, par)
                    pool.wait_ge(q.lidx_copied, i * 2 + (par + 1))
                    pool.sem_inc(q.idx_seen, 1)
                    gather(par, xg, h0_dram)

            gath = [q.gath0, q.gath1, q.gath2, q.gath3, q.gath4, q.gath5, q.gath6, q.gath7]
            pool.wait_ge(q.y0_stored, 16 * (NB0 // 2))
            pool.wait_ge(q.y1_stored, 16 * (NB0 // 2))
            for n in range(B * TOP):
                if n >= 8:
                    pool.wait_ge(q.comb_done, n - 7)
                pool.indirect_dma_start(out=g0[n % 8], out_offset=None, in_=y0_dram,
                                        in_offset=bass.IndirectOffsetOnAxis(ap=slot_u[:, n:n + 1], axis=0)
                                        ).then_inc(gath[n % 8], 16)
            root(3)
            pool.wait_ge(q.bv_ready, 1)
            for t in range(B):
                pool.tensor_tensor(x[:, t], x[:, t], bv, ALU.add).then_inc(q.x_based, 1)
            root(4)
            pool.wait_ge(q.list_ready, 2)
            pool.wait_ge(q.h_stored1, 16 * B)
            for j in range(NB1):
                par = j % 2
                if j >= 2:
                    pool.wait_ge(q.t1_mm, j - 1)
                token_column(j, par)
                pool.wait_ge(q.lidx_copied, NB0 + j + 1)
                gather(par, xg1, h1_dram)
            pool.wait_ge(q.y1_done, 16 * NB1)
            for t in range(B):
                pool.indirect_dma_start(out=g1[t], out_offset=None, in_=y1_dram,
                                        in_offset=bass.IndirectOffsetOnAxis(ap=slot_u[:, t:t + 1], axis=0)
                                        ).then_inc(gath[t], 16)

        @block.scalar
        def _(act):
            act.wait_ge(q.ld_kv, 80)
            act.activation(gates[:, 4:5], cols[:, C_DEC:C_DEC + 1], ACT.Sigmoid).then_inc(q.gates_ready, 1)
            act.activation(gates[:, 0:4], cols[:, C_GX:C_GX + 4], ACT.Tanh).then_inc(q.gates_ready, 1)

            def kv(b):
                bank = [0, 1, 2, 3, 4, 5, 0, 1, 2, 3, 4]
                for n in range(11):
                    act.wait_ge(q.kv_mm, b * 11 + (n + 1))
                    src = ps[:, bank[n], 0:T]
                    if n < KD:
                        ins = act.activation(sup[:, n], src, ACT.Relu, bias=cols[:, C_BFC + n:C_BFC + n + 1])
                    elif n < 2 * KD:
                        m = n - KD
                        if m == 0:
                            act.wait_ge(q.u_done, b * KD + KD)
                        ins = act.activation(ctxk[:, bass.ds(b, 1), m].rearrange("p b t -> p (b t)"), src,
                                             ACT.Identity, bias=cols[:, C_BK + m:C_BK + m + 1])
                    else:
                        c = n - 2 * KD
                        ins = act.activation(vals[:, bass.ds(b * 3 + c, 1)].rearrange("p b t -> p (b t)"),
                                             ps[0:TC, bank[n], :], ACT.Copy)
                    ins.then_inc(q.kv_ev, 1)

            for b in range(2):
                kv(b)
            with act.Fori(2, 5) as b:
                kv(b)
            act.wait_ge(q.ediff_ready, 1)
            d = disp0["m8"][:, :, 0:TOP]
            act.activation(wt[:].rearrange("p (b k) -> p b k", b=B), d, ACT.Exp).then_inc(q.eexp_ready, 1)
            with act.Fori(5, B) as b:
                kv(b)

            stored = (q.y0_stored, q.y1_stored)

            def silu(j, par):
                act.wait_ge(q.u_mm, j + 1)
                act.activation(sg[par], ps[:, 2 + par, 0:I0], ACT.Silu).then_inc(q.silu_done, 1)

            def y_out(j, par, i):
                act.wait_ge(q.d_mm, j + 2)
                if i is not None:
                    act.wait_ge(stored[par], i * 16)
                act.activation(yb[par], ps[:, 6 + par, :], ACT.Copy).then_inc(q.y_ev, 1)
                act.wait_ge(q.y_ev, j + 1)
                act.dma_start(y0_dram[bass.ds(j * P, P), :], yb[par]).then_inc(stored[par], 16)

            silu(0, 0)
            silu(1, 1)
            for par in range(2):
                silu(2 + par, par)
                y_out(par, par, None)
            with act.Fori(2, NB0 // 2) as i:
                for par in range(2):
                    silu(i * 2 + par, par)
                    y_out(i * 2 + (par - 2), par, i - 1)
            for par in range(2):
                y_out(NB0 - 2 + par, par, NB0 // 2 - 1)

            for n in range(16):
                act.wait_ge(q.ref_mm, n + 1)
                m, half = (n % 8) // 2, n % 2
                dst = (refT if n < 8 else qT)[:, m, half * 448:half * 448 + 448]
                bias = cols[:, (C_BFC if n < 8 else C_BQ) + m:(C_BFC if n < 8 else C_BQ) + m + 1]
                act.activation(dst, ps[:, n % 4, 0:448], ACT.Relu if n < 8 else ACT.Identity,
                               bias=bias).then_inc(q.ref_ev, 1)

            def exps(s, par):
                act.wait_ge(q.mx_ready, s + 1)
                for h in range(4):
                    ins = act.activation(prob[par][:, h], ps[0:S, h, 0:T], ACT.Exp, bias=nmx[:, par, h:h + 1],
                                         scale=SCALE, accum_out=psum_e[:, par, h:h + 1])
                ins.then_inc(q.e_done, 1)

            with act.Fori(0, 2 * B) as i:
                for par in range(2):
                    exps(i * 2 + par, par)

            act.wait_ge(q.ediff_ready, 2)
            act.activation(wt[:, 0:B], disp1["m8"][:, :, 0:1].rearrange("p b k -> p (b k)"), ACT.Exp
                           ).then_inc(q.eexp_ready, 1)

            def l1(c, j):
                s = c * NB1 + j
                act.wait_ge(q.u1_mm, s + 1)
                act.activation(hf[j % 2], ps[:, j % 2, :], ACT.Copy, scale=0.5).then_inc(q.half_done, 1)

            def l1_sq(s, par):
                act.wait_ge(q.h1_mm, s + 1)
                act.activation(aT[par].rearrange("p k n -> p (k n)"), ps[:, 2 + par, :], ACT.Square
                               ).then_inc(q.h1_ev, 1)

            l1(0, 0)
            for j in range(1, NB1):
                l1(0, j)
                l1_sq(j - 1, (j - 1) % 2)
            with act.Fori(1, NCH) as c:
                for j in range(NB1):
                    l1(c, j)
                    l1_sq(c * NB1 + (j - 1), (j - 1) % 2)
            l1_sq(NB1 * NCH - 1, 1)

        @block.tensor
        def _(pe):
            def kv(b):
                bank = [0, 1, 2, 3, 4, 5, 0, 1, 2, 3, 4]
                last = [7, 8, 9, 10, 11, 6]
                first = isinstance(b, int) and b == 0
                for n in range(11):
                    if n >= 6:
                        pe.wait_ge(q.kv_ev, b * 11 + (n - 5))
                    elif not first:
                        pe.wait_ge(q.kv_ev, b * 11 + (last[n] - 11))
                    for k in range(KD):
                        if n < KD:
                            o = ps[:, bank[n], 0:T]
                            w = wfc[:, k, n * P:(n + 1) * P]
                            r = ctxk[:, bass.ds(b, 1), k].rearrange("p b t -> p (b t)")
                        else:
                            if n == KD:
                                pe.wait_ge(q.kv_ev, b * 11 + (k + 1))
                            if n < 2 * KD:
                                m = n - KD
                                o, w, r = ps[:, bank[n], 0:T], wk[:, k, m * P:(m + 1) * P], sup[:, k]
                            else:
                                c = n - 2 * KD
                                o, w, r = ps[0:TC, bank[n], :], sup[:, k, c * TC:(c + 1) * TC], wv[:, k]
                        ins = pe.matmul(o, w, r, start=(k == 0), stop=(k == KD - 1))
                    ins.then_inc(q.kv_mm, 1)

            def summary():
                pe.wait_ge(q.ld_sum, 96)
                pe.wait_ge(q.u_done, KD * B)
                for m in range(KD):
                    for k in range(KD):
                        ins = pe.matmul(ps[:, 6, m * B:(m + 1) * B], w_in[:, k, m * P:(m + 1) * P], uT[:, k],
                                        start=(k == 0), stop=(k == KD - 1))
                ins.then_inc(q.s1_mm, 1)
                pe.wait_ge(q.s1_ready, 1)
                for k in range(KD):
                    ins = pe.matmul(ps[0:B, 7, :], s1T[:, k], w_out[:, k], start=(k == 0), stop=(k == KD - 1))
                ins.then_inc(q.sum_mm, 1)
                pe.wait_ge(q.sum_ready, 1)
                for t in range(B):
                    if t >= 2:
                        pe.wait_ge(q.y_added, t - 1)
                    pe.matmul(ps[0:S, 6 + t % 2, :], sel[:, t], summ, start=True, stop=True).then_inc(q.bc_mm, 1)

            def transposes(n, t):
                pe.wait_ge(q.h_ready, n * B + t + 1)
                for k in range(KD):
                    ins = pe.transpose(ps[:, 6 + t % 2, k * S:(k + 1) * S], z[:, t, k * P:(k + 1) * P], ident[0:S, 0:S])
                ins.then_inc(q.tr_mm, 1)

            def routed(n, m, rw, E):
                for t in range(B + 1):
                    if t < B:
                        if t >= 2:
                            pe.wait_ge(q.lg_ev, m * B + t - 1)
                        transposes(n, t)
                    if t >= 1:
                        u = t - 1
                        pe.wait_ge(q.tr_ev, n * B + u + 1)
                        for k in range(KD):
                            ins = pe.matmul(ps[0:S, 6 + u % 2, 448:448 + E], hT[:, k, u * S:(u + 1) * S],
                                            rw[:, k * E:(k + 1) * E], start=(k == 0), stop=(k == KD - 1))
                        ins.then_inc(q.lg_mm, 1)

            def ranks(n, v, E):
                pe.wait_ge(q.ready_m, n + 1)
                mm = v["m"].rearrange("p (b e) -> p b e", b=B)
                pe.matmul(ps[0:S, 6, 0:B * E], tri, v["m"], start=True, stop=False)
                for t in range(B - 1):
                    ins = pe.matmul(ps[0:S, 6, (t + 1) * E:B * E].rearrange("p (b e) -> p b e", e=E), ones_b[:, 0:S],
                                    mm[:, t:t + 1].to_broadcast([S, B - 1 - t, E]), start=False, stop=(t == B - 2))
                for t in range(B):
                    ins = pe.matmul(ps[:, 7, 0:E], ones_b, mm[:, t], start=(t == 0), stop=(t == B - 1))
                ins.then_inc(q.rank_mm, 1)

            def token_list(n, v, pairs, NB):
                pe.wait_ge(q.ready_r, n + 1)
                for c in range(pairs):
                    ins = pe.matmul(ps[:, 6, 0:2 * NB], v["rm"][:, c], v["q2"][:, c].rearrange("p a j -> p (a j)"),
                                    start=(c == 0), stop=(c == pairs - 1))
                ins.then_inc(q.list_mm, 1)

            pe.wait_ge(q.ld_kv, 80)
            kv(0)
            pe.wait_ge(q.ld_ctx1, 16)
            kv(1)
            pe.wait_ge(q.ld_ctx, 16 * (B - 2))
            summary()
            with pe.Fori(2, 4) as b:
                kv(b)
            pe.wait_ge(q.ld_small, 64)
            routed(0, 0, rw0, E0)
            with pe.Fori(4, 6) as b:
                kv(b)
            pe.wait_ge(q.ld_cst, 64)
            ranks(0, disp0, E0)
            kv(6)
            token_list(0, disp0, B * TOP, NB0)
            kv(7)

            landed = (q.x0_landed, q.x1_landed)

            def blk_t(j, par, i):
                pe.wait_ge(landed[par], i * 16 + 16)
                if not isinstance(j, int) or j >= 2:
                    pe.wait_ge(q.t_ev, j - 1)
                for k in range(KD):
                    ins = pe.transpose(ps[:, par, k * P:(k + 1) * P], xg[par][:, k * P:(k + 1) * P], ident[:])
                ins.then_inc(q.t_mm, 1)

            pe.sem_inc(q.d_mm, 1)

            def blk_up(j, par, off):
                pe.wait_ge(q.t_ev, j + 1)
                if not isinstance(j, int) or j >= 2:
                    pe.wait_ge(q.h_mul, j - 1)
                for k in range(KD):
                    ins = pe.matmul(ps[:, 2 + par, 0:2 * I0], xT[par][:, k], ring[:, bass.ds(off + k * 2 * I0, 2 * I0)],
                                    start=(k == 0), stop=(k == KD - 1))
                ins.then_inc(q.u_mm, 1)

            def blk_h(j, par):
                pe.wait_ge(q.h_mul, j + 1)
                if not isinstance(j, int) or j >= 2:
                    pe.wait_ge(q.h_ev, j - 1)
                for k in range(2):
                    ins = pe.transpose(ps[0:IH, 4 + par, k * P:(k + 1) * P], hm[par][:, k * IH:(k + 1) * IH], ident[:])
                ins.then_inc(q.h_mm, 1)

            def blk_d(j, par, off):
                pe.wait_ge(q.h_ev, j + 1)
                if not isinstance(j, int) or j >= 2:
                    pe.wait_ge(q.y_ev, j - 1)
                for k in range(2):
                    ins = pe.matmul(ps[:, 6 + par, :], hmT[par][:, k], ring[0:IH, bass.ds(off + GU + k * D, D)],
                                    start=(k == 0), stop=(k == 1))
                ins.then_inc(q.d_mm, 1)

            def place(j):
                return pe.value_load(table2[0:1, bass.ds(j, 1)], min_val=A_WK, max_val=A_FREE)

            def step(j, par, i, up=True, h=True, t=True, d=True):
                if up:
                    e = pe.value_load(table[0:1, bass.ds(j, 1)], min_val=0, max_val=E0 - 1)
                    off = place(j)
                    pe.wait_ge(q.w_ready, e + 1)
                    blk_up(j, par, off)
                if h:
                    blk_h(j - 1, 1 - par)
                if t:
                    blk_t(j + 1, 1 - par, i + par)
                if d:
                    blk_d(j - 2, par, place(j - 2))

            pe.wait_ge(q.list_ready, 1)
            pe.wait_ge(q.kv_ev, 11 * B)
            blk_t(0, 0, 0)
            step(0, 0, 0, h=False, d=False)
            step(1, 1, 0, d=False)
            step(2, 0, 1)
            step(3, 1, 1)
            with pe.Fori(2, NB0 // 2 - 1) as i:
                for par in range(2):
                    step(i * 2 + par, par, i)
            i = NB0 // 2 - 1
            step(NB0 - 2, 0, i)
            step(NB0 - 1, 1, i, t=False)
            step(NB0, 0, i, up=False, t=False)
            step(NB0 + 1, 1, i, up=False, h=False, t=False)

            for t in range(B):
                if t >= 2:
                    pe.wait_ge(q.tr_ev, B + t - 1)
                transposes(1, t)
            pe.wait_ge(q.tr_ev, 2 * B)
            for n in range(16):
                m, half = (n % 8) // 2, n % 2
                if n >= 4:
                    pe.wait_ge(q.ref_ev, n - 3)
                if n == 8:
                    pe.wait_ge(q.ref_ev, 8)
                w, r = (wfc, hT) if n < 8 else (wq, refT)
                for k in range(KD):
                    ins = pe.matmul(ps[:, n % 4, 0:448], w[:, k, m * P:(m + 1) * P], r[:, k, half * 448:half * 448 + 448],
                                    start=(k == 0), stop=(k == KD - 1))
                ins.then_inc(q.ref_mm, 1)
            for t in range(B):
                if t >= 2:
                    pe.wait_ge(q.rt_add, t - 1)
                for k in range(KD):
                    ins = pe.transpose(ps[0:S, 4 + t % 2, k * P:(k + 1) * P], refT[:, k, t * S:(t + 1) * S], ident[:])
                ins.then_inc(q.rt_mm, 1)

            landed_qk = (q.qk0_landed, q.qk1_landed)

            def scores(s, b2, par, g):
                if g == 0:
                    pe.wait_ge(landed_qk[par], b2 * 32 + 32)
                if not isinstance(s, int) or s >= 1:
                    pe.wait_ge(q.e_done, s)
                for h in range(4):
                    lo = h * DG
                    ins = pe.matmul(ps[0:S, h, 0:T], qb[par][lo:lo + DG, g], kb[par][lo:lo + DG, g],
                                    start=True, stop=True)
                ins.then_inc(q.s_mm, 1)

            def att(s, b, g):
                pe.wait_ge(q.e_done, s + 1)
                if not isinstance(s, int) or s >= 1:
                    pe.wait_ge(q.pt_ev, s)
                for c in range(3):
                    for h in range(4):
                        ins = pe.transpose(ps[0:TC, 4 + c, h * S:(h + 1) * S],
                                           prob[g % 2][:, h, c * TC:(c + 1) * TC], ident[0:S, 0:S])
                ins.then_inc(q.pt_mm, 1)
                pe.wait_ge(q.pt_ev, s + 1)
                if not isinstance(s, int) or s >= 1:
                    pe.wait_ge(q.o_done, s)
                for h in range(4):
                    for c in range(3):
                        v = vals[:, bass.ds(b * 3 + c, 1), (4 * g + h) * DG:(4 * g + h + 1) * DG]
                        ins = pe.matmul(ps[0:S, 7, h * DG:(h + 1) * DG], pT[:, c, h], v.rearrange("p b d -> p (b d)"),
                                        start=(c == 0), stop=(c == 2))
                ins.then_inc(q.pv_mm, 1)

            pe.wait_ge(q.rt_add, B)
            scores(0, 0, 0, 0)
            for g in range(3):
                scores(g + 1, 0, 0, g + 1)
                att(g, 0, g)
            scores(4, 0, 1, 0)
            att(3, 0, 3)

            def att_batch(b, b2, par, last=False):
                for g in range(4):
                    s = b * 4 + g
                    if g < 3:
                        scores(s + 1, b2, par, g + 1)
                    elif not last:
                        scores(s + 1, b2 + par, 1 - par, 0)
                    att(s, b, g)

            att_batch(1, 0, 1)
            with pe.Fori(1, B // 2 - 1) as i:
                for par in range(2):
                    att_batch(i * 2 + par, i, par)
            att_batch(B - 2, B // 2 - 1, 0)
            att_batch(B - 1, B // 2 - 1, 1, last=True)

            pe.wait_ge(q.o_done, 4 * B)
            routed(2, 1, rw1, E1)
            ranks(1, disp1, E1)
            token_list(1, disp1, B, NB1)
            for j in range(NB1):
                pe.wait_ge(landed[j % 2], 16 * (NB0 // 2 + j // 2 + 1))
                if j >= 2:
                    pe.wait_ge(q.t1_ev, j - 1)
                if j == 0:
                    pe.wait_ge(q.list_ready, 2)
                for k in range(KD):
                    ins = pe.transpose(ps[:, 6 + j % 2, k * P:(k + 1) * P], xg1[j % 2][:, k * P:(k + 1) * P], ident[:])
                ins.then_inc(q.t1_mm, 1)
            pe.wait_ge(q.t1_ev, NB1)
            places = [pe.value_load(table[0:1, j:j + 1], min_val=0, max_val=E1 - 1) for j in range(NB1)]

            def up1(s, c, j):
                if j == 0:
                    pe.wait_ge(q.ch_ready, c + 1)
                if not isinstance(s, int) or s >= 2:
                    pe.wait_ge(q.l_done, s - 1)
                off = places[j] * (RW1 // E1) + chunk_base(c)
                for k in range(KD):
                    ins = pe.matmul(ps[:, j % 2, :], xT1[:, j, k], ring[:, bass.ds(off + k * CH, CH)],
                                    start=(k == 0), stop=(k == KD - 1))
                ins.then_inc(q.u1_mm, 1)

            def turn1(s, j):
                pe.wait_ge(q.l_done, s + 1)
                if not isinstance(s, int) or s >= 2:
                    pe.wait_ge(q.h1_ev, s - 1)
                for k in range(KD):
                    ins = pe.transpose(ps[:, 2 + j % 2, k * P:(k + 1) * P], lk[j % 2][:, k * P:(k + 1) * P], ident[:])
                ins.then_inc(q.h1_mm, 1)

            def down1(s, c, j):
                pe.wait_ge(q.h1_ev, s + 1)
                if not isinstance(s, int) or s >= 2:
                    pe.wait_ge(q.y1_ev, s - 1)
                off = places[j] * (RW1 // E1) + chunk_base(c) + KD * CH
                for k in range(KD):
                    ins = pe.matmul(ps[:, 4 + j % 2, :], aT[j % 2][:, k], ring[:, bass.ds(off + k * D, D)],
                                    start=(k == 0), stop=(k == KD - 1))
                ins.then_inc(q.d1_mm, 1)

            def chunk_base(c):
                return (c % 2) * (A_CH[1] - A_CH[0]) + A_CH[0]

            def chunk_steps(c, first=False):
                for j in range(NB1):
                    s = c * NB1 + j
                    up1(s, c, j)
                    if not first or j >= 1:
                        turn1(s - 1, (j - 1) % NB1)
                    if not first or j >= 2:
                        down1(s - 2, c if j >= 2 else c - 1, (j - 2) % NB1)

            chunk_steps(0, first=True)
            with pe.Fori(1, NCH) as c:
                chunk_steps(c)
            s = NCH * NB1
            turn1(s - 1, NB1 - 1)
            down1(s - 2, NCH - 1, NB1 - 2)
            down1(s - 1, NCH - 1, NB1 - 1)

        @block.vector
        def _(dve):
            count = [0]

            def chain(ins):
                count[0] += 1
                ins.then_inc(q.dve_done, 1)
                dve.wait_ge(q.dve_done, count[0])

            def layer_stats(rows):
                for t in range(B):
                    ins = dve.bn_stats(stats[:, t], rows[:, t])
                chain(ins)
                for t in range(B):
                    ins = dve.bn_aggr(mv[:, t], stats[:, t])
                chain(ins)
                dve.tensor_scalar(veps[:], mv[:, :, 1], EPS, None, ALU.add).then_inc(q.veps_ready, 1)

            def normalize(n, rows, s):
                dve.wait_ge(q.rstd_ready, n + 1)
                for t in range(B):
                    dve.tensor_scalar(z[:, t], rows[:, t], mv[:, t, 0:1], rstd[:, t:t + 1], ALU.subtract, ALU.mult
                                      ).then_inc(s, 1)

            dve.wait_ge(q.ld_kv, 80)
            chain(dve.memset(ones_row, 1.0))
            dve.wait_ge(q.gates_ready, 2)
            chain(dve.tensor_scalar(k_row, ones_row, gates[:, 4:5], None, ALU.mult))
            chain(dve.tensor_tensor_scan(r_row, k_row, ones_row, 0.0, ALU.mult, ALU.add))
            chain(dve.tensor_reduce(gates[:, 5:6], r_row, AX.X, ALU.add))
            chain(dve.tensor_scalar(bC[:], cols[:, C_BIN:C_BIN + KD], gates[:, 5:6], None, ALU.mult))

            def decayed(b):
                for k in range(KD):
                    n = b * KD + k
                    if n >= 2:
                        dve.wait_ge(q.u_done, n - 1)
                    dve.tensor_tensor_reduce(prod_rows[n % 2], ctxk[:, b, k], r_row, 1.0, 0.0, ALU.mult, ALU.add,
                                             uT[:, k, b:b + 1]).then_inc(q.u_done, 1)
            decayed(0)
            dve.wait_ge(q.ld_ctx1, 16)
            decayed(1)
            dve.wait_ge(q.ld_ctx, 16 * (B - 2))
            for b in range(2, B):
                decayed(b)
            dve.wait_ge(q.ld_x, 16)
            layer_stats(x)
            normalize(0, x, q.z_ready)
            dve.wait_ge(q.ld_sum, 96)
            chain(dve.tensor_scalar(gamma, gamma, gx0, None, ALU.mult))
            dve.tensor_scalar(beta, beta, gx0, None, ALU.mult).then_inc(q.beta_ready, 1)
            dve.wait_ge(q.s1_mm, 1)
            dve.tensor_tensor(s1T[:], ps[:, 6, 0:KD * B].rearrange("p (k b) -> p k b", k=KD),
                              bC[:].rearrange("p (k o) -> p k o", o=1).to_broadcast([P, KD, B]), ALU.add
                              ).then_inc(q.s1_ready, 1)
            dve.wait_ge(q.sum_mm, 1)
            dve.scalar_tensor_tensor(out=summ, in0=ps[0:B, 7, :], scalar=1.0 / T, in1=bout, op0=ALU.mult, op1=ALU.add
                                     ).then_inc(q.sum_ready, 1)
            for t in range(B):
                dve.wait_ge(q.bc_mm, t + 1)
                dve.wait_ge(q.z_ready, t + 1)
                dve.tensor_tensor(z[:, t], z[:, t], ps[0:S, 6 + t % 2, :], ALU.add).then_inc(q.y_added, 1)
            dve.wait_ge(q.y_added, B)
            layer_stats(z)
            dve.wait_ge(q.rstd_ready, 2)
            dve.wait_ge(q.x_based, B)
            for t in range(B):
                ins = dve.scalar_tensor_tensor(out=z[:, t], in0=z[:, t], scalar=mv[:, t, 0:1], in1=gamma,
                                               op0=ALU.subtract, op1=ALU.mult)
            chain(ins)
            for t in range(B):
                ins = dve.scalar_tensor_tensor(out=x[:, t], in0=z[:, t], scalar=rstd[:, t:t + 1], in1=x[:, t],
                                               op0=ALU.mult, op1=ALU.add)
            chain(ins)
            layer_stats(x)
            normalize(2, x, q.h_ready)

            def turned(n, t):
                dve.wait_ge(q.tr_mm, n * B + t + 1)
                dve.tensor_copy(hT[:, :, t * S:(t + 1) * S],
                                ps[:, 6 + t % 2, 0:KD * S].rearrange("p (k s) -> p k s", k=KD)).then_inc(q.tr_ev, 1)

            def logits(n, m, E, lg):
                for t in range(B + 1):
                    if t < B:
                        turned(n, t)
                    if t >= 1:
                        u = t - 1
                        dve.wait_ge(q.lg_mm, m * B + u + 1)
                        dve.tensor_copy(lg[:, u], ps[0:S, 6 + u % 2, 448:448 + E]).then_inc(q.lg_ev, 1)
                dve.wait_ge(q.lg_ev, (m + 1) * B)

            def sort(n, v, E, C, NB):
                pairs = B * C
                oh = v["oh"].rearrange("p (c e) -> p c e", e=E)
                dve.wait_ge(q.rank_mm, n + 1)
                chain(dve.tensor_scalar(v["cnti"], ps[:, 7, 0:E], float(P - 1), None, ALU.add))
                chain(dve.memset(v["ones"], 1.0))
                chain(dve.tensor_scalar(v["cnti"], v["cnti"], 7, None, ALU.logical_shift_right))
                chain(dve.tensor_copy(v["nb"], v["cnti"]))
                if n == 0:
                    chain(dve.tensor_scalar(v["nb"], v["nb"], 1.0, None, ALU.max))
                chain(dve.tensor_tensor_scan(v["cum"], v["ones"], v["nb"], 0.0, ALU.mult, ALU.add))
                chain(dve.tensor_tensor(v["base"], v["cum"], v["nb"], ALU.subtract))
                chain(dve.tensor_scalar(v["base"], v["base"], float(P), None, ALU.mult))
                slot = v["slot"].rearrange("p (b e) -> p b e", b=B)
                chain(dve.tensor_tensor(slot, ps[0:S, 6, 0:B * E].rearrange("p (b e) -> p b e", b=B),
                                        v["base"][0:S].rearrange("p (o e) -> p o e", o=1).to_broadcast([S, B, E]),
                                        ALU.add))
                pick = v["pick"].rearrange("p (b k e) -> p b k e", b=B, k=C)
                chain(dve.tensor_tensor(pick, oh.rearrange("p (b k) e -> p b k e", b=B),
                                        slot.rearrange("p b (o e) -> p b o e", o=1).to_broadcast([S, B, C, E]),
                                        ALU.mult))
                chain(dve.tensor_reduce(v["sk"], v["pick"].rearrange("p (c e) -> p c e", e=E), AX.X, ALU.add))
                dve.tensor_copy(slot_u[:, 0:pairs], v["sk"])
                chain(dve.tensor_copy(v["ski"], v["sk"]))
                dve.tensor_scalar(v["qi"], v["ski"], 7, None, ALU.logical_shift_right)
                chain(dve.tensor_scalar(v["ri"], v["ski"], P - 1, None, ALU.bitwise_and))
                dve.tensor_copy(v["qf"], v["qi"])
                chain(dve.tensor_copy(v["rf"], v["ri"]))
                cum0 = v["cum"][0:1].rearrange("p (o e) -> p o e", o=1).to_broadcast([1, NB, E])
                j0 = iota[0:1, 0:NB].rearrange("p (j o) -> p j o", o=1).to_broadcast([1, NB, E])
                chain(dve.tensor_tensor(v["cmp"], cum0, j0, ALU.is_le))
                chain(dve.tensor_reduce(v["eb"][0:1], v["cmp"], AX.X, ALU.add))
                chain(dve.tensor_scalar(v["eb"][0:1], v["eb"][0:1], float(E - 1), None, ALU.min))
                dve.tensor_copy(table[0:1, 0:NB], v["eb"][0:1])
                if n == 0:
                    chain(dve.tensor_scalar(table[0:1, 64:64 + E], v["cum"][0:1], 1.0, None, ALU.add))
                    chain(dve.tensor_scalar(v["la"][0:1].bitcast(I32), table[0:1, 0:NB], NR0 - 1, None,
                                            ALU.bitwise_and))
                    chain(dve.tensor_copy(v["eb"][0:1], v["la"][0:1].bitcast(I32)))
                    t0 = v["la"][0:1]
                    chain(dve.tensor_scalar(t0, v["eb"][0:1], 0.0, float(A_RING[0]), ALU.is_equal, ALU.mult))
                    for r in range(1, NR0):
                        chain(dve.tensor_scalar(v["slot"][0:1, 0:NB], v["eb"][0:1], float(r), float(A_RING[r]),
                                                ALU.is_equal, ALU.mult))
                        chain(dve.tensor_tensor(t0, t0, v["slot"][0:1, 0:NB], ALU.add))
                    chain(dve.tensor_copy(table2[0:1, 0:NB], t0))
                rf = v["rf"].rearrange("p (c o) -> p c o", o=1)
                qf = v["qf"].rearrange("p (c o) -> p c o", o=1)
                io = iota[0:S].rearrange("p (o r) -> p o r", o=1)
                dve.tensor_tensor(v["rm"], io.to_broadcast([S, pairs, P]), rf.to_broadcast([S, pairs, P]), ALU.is_equal)
                chain(dve.tensor_tensor(v["qm"], io[:, :, 0:NB].to_broadcast([S, pairs, NB]),
                                        qf.to_broadcast([S, pairs, NB]), ALU.is_equal))
                tn = tile_no.rearrange("p (c o) -> p c o", o=1 if C == TOP else TOP)[:, :, 0:1]
                dve.tensor_tensor(v["q2"][:, :, 0], v["qm"], tn.to_broadcast([S, pairs, NB]), ALU.mult)
                dve.tensor_scalar(v["q2"][:, :, 1], v["qm"], cols[0:S, C_PID:C_PID + 1], None, ALU.mult
                                  ).then_inc(q.ready_r, 1)
                dve.wait_ge(q.list_mm, n + 1)
                chain(dve.tensor_scalar(v["la"], ps[:, 6, 0:NB], float(S), None, ALU.mult))
                dve.tensor_tensor(lidx[:, 0:NB], v["la"], ps[:, 6, NB:2 * NB], ALU.add).then_inc(q.list_ready, 1)

            v = disp0
            logits(0, 0, E0, lg0)
            dve.wait_ge(q.h_stored0, 16 * B)
            for t in range(B):
                ins = dve.max(v["m8"][:, t], lg0[:, t])
            chain(ins)
            for t in range(B):
                ins = dve.max_index(v["i8"][:, t], v["m8"][:, t], lg0[:, t])
            chain(ins)
            dve.tensor_copy(v["idf"].rearrange("p (b k) -> p b k", b=B), v["i8"][:, :, 0:TOP])
            chain(dve.tensor_copy(v["sk"][:, 0:B].rearrange("p (b o) -> p b o", o=1), v["m8"][:, :, 0:1]))
            dve.tensor_tensor(v["m8"][:, :, 0:TOP], v["m8"][:, :, 0:TOP],
                              v["sk"][:, 0:B].rearrange("p (b o) -> p b o", o=1).to_broadcast([S, B, TOP]),
                              ALU.subtract).then_inc(q.ediff_ready, 1)
            dve.wait_ge(q.ld_cst, 64)
            oh = v["oh"].rearrange("p (c e) -> p c e", e=E0)
            chain(dve.tensor_tensor(oh, iota[0:S, 0:E0].rearrange("p (o e) -> p o e", o=1).to_broadcast([S, B * TOP, E0]),
                                    v["idf"].rearrange("p (c o) -> p c o", o=1).to_broadcast([S, B * TOP, E0]),
                                    ALU.is_equal))
            chain(dve.tensor_reduce(v["slot"].rearrange("p (b e) -> p b e", b=B),
                                    v["oh"].rearrange("p (b k e) -> p b e k", b=B, k=TOP), AX.X, ALU.add))
            dve.tensor_copy(v["m"], v["slot"]).then_inc(q.ready_m, 1)
            dve.wait_ge(q.eexp_ready, 1)
            wt3 = wt[:].rearrange("p (b k) -> p b k", b=B)
            chain(dve.tensor_reduce(veps[:], wt3, AX.X, ALU.add))
            chain(dve.reciprocal(veps[:], veps[:]))
            chain(dve.tensor_scalar(veps[:], veps[:], gf0, None, ALU.mult))
            chain(dve.tensor_tensor(wt3, wt3, veps[:].rearrange("p (b o) -> p b o", o=1).to_broadcast([S, B, TOP]),
                                    ALU.mult))
            sort(0, v, E0, TOP, NB0)

            def t_ev(j, par):
                dve.wait_ge(q.t_mm, j + 1)
                dve.tensor_copy(xT[par].rearrange("p k n -> p (k n)"), ps[:, par, :]).then_inc(q.t_ev, 1)

            def mul(j, par):
                dve.wait_ge(q.silu_done, j + 1)
                dve.tensor_tensor(hm[par], sg[par], ps[:, 2 + par, I0:2 * I0], ALU.mult).then_inc(q.h_mul, 1)

            def h_ev(j, par):
                dve.wait_ge(q.h_mm, j + 1)
                dve.tensor_copy(hmT[par].rearrange("p k n -> p (k n)"), ps[0:IH, 4 + par, 0:2 * P]).then_inc(q.h_ev, 1)

            t_ev(0, 0)
            mul(0, 0)
            t_ev(1, 1)
            h_ev(0, 0)
            mul(1, 1)
            t_ev(2, 0)
            with dve.Fori(1, NB0 // 2 - 1) as i:
                for par in range(2):
                    j = i * 2 + par
                    h_ev(j - 1, 1 - par)
                    mul(j, par)
                    t_ev(j + 1, 1 - par)
            h_ev(NB0 - 3, 1)
            mul(NB0 - 2, 0)
            t_ev(NB0 - 1, 1)
            h_ev(NB0 - 2, 0)
            mul(NB0 - 1, 1)
            h_ev(NB0 - 1, 1)

            gath = [q.gath0, q.gath1, q.gath2, q.gath3, q.gath4, q.gath5, q.gath6, q.gath7]
            for k in range(B * TOP):
                t = k // TOP
                dve.wait_ge(gath[k % 8], 16 * (k // 8 + 1))
                if k % TOP:
                    dve.wait_ge(q.comb_done, k)
                dve.scalar_tensor_tensor(out=x[:, t], in0=g0[k % 8], scalar=wt[:, k:k + 1], in1=x[:, t],
                                         op0=ALU.mult, op1=ALU.add).then_inc(q.comb_done, 1)
            dve.wait_ge(q.comb_done, B * TOP)
            layer_stats(x)
            dve.wait_ge(q.rstd_ready, 4)
            for t in range(B):
                dve.tensor_scalar(z[:, t], x[:, t], mv[:, t, 0:1], rstd[:, t:t + 1], ALU.subtract, ALU.mult
                                  ).then_inc(q.h_ready, 1)
            dve.wait_ge(q.ld_bv, 16)
            dve.tensor_scalar(bv, bv, gx1, None, ALU.mult).then_inc(q.bv_ready, 1)
            for t in range(B):
                turned(1, t)
            dve.wait_ge(q.x_based, 2 * B)
            for t in range(B):
                dve.wait_ge(q.rt_mm, t + 1)
                dve.scalar_tensor_tensor(out=x[:, t], in0=ps[0:S, 4 + t % 2, :], scalar=gx1, in1=x[:, t],
                                         op0=ALU.mult, op1=ALU.add).then_inc(q.rt_add, 1)
            dve.wait_ge(q.rt_add, B)

            base = count[0]
            PER = 5

            def row_max(s, par):
                dve.wait_ge(q.s_mm, s + 1)
                dve.tensor_reduce(nmx[:, par], ps[0:S, 0:4, 0:T], AX.X, ALU.max).then_inc(q.dve_done, 1)

            def scaled_max(s, par, n):
                dve.wait_ge(q.dve_done, n)
                dve.tensor_scalar(nmx[:, par], nmx[:, par], -SCALE, None, ALU.mult).then_inc(q.mx_ready, 1)

            def p_ev(s):
                dve.wait_ge(q.pt_mm, s + 1)
                dve.tensor_copy(pT.rearrange("p c h s -> p c (h s)"), ps[0:TC, 4:7, 0:4 * S]).then_inc(q.pt_ev, 1)

            def out_add(s, b, g, par, n):
                dve.reciprocal(rinv[:, par], psum_e[:, par]).then_inc(q.dve_done, 1)
                dve.wait_ge(q.dve_done, n + 1)
                dve.tensor_scalar(rinv[:, par], rinv[:, par], gx1, None, ALU.mult).then_inc(q.dve_done, 1)
                dve.wait_ge(q.dve_done, n + 2)
                dve.wait_ge(q.pv_mm, s + 1)
                dve.tensor_tensor(o_t[:, par].rearrange("p (h d) -> p h d", h=4),
                                  ps[0:S, 7, 0:P].rearrange("p (h d) -> p h d", h=4),
                                  rinv[:, par].rearrange("p (h o) -> p h o", o=1).to_broadcast([S, 4, DG]), ALU.mult
                                  ).then_inc(q.dve_done, 1)
                dve.wait_ge(q.dve_done, n + 3)
                xs = x[:, bass.ds(b, 1), g * P:(g + 1) * P].rearrange("p b d -> p (b d)")
                dve.tensor_tensor(xs, xs, o_t[:, par], ALU.add).then_inc(q.o_done, 1)

            PER = 4

            def att_batch(b, last=False):
                for g in range(4):
                    s = b * 4 + g
                    n = s * PER + (base + 1)
                    if not (last and g == 3):
                        row_max(s + 1, (g + 1) % 2)
                        scaled_max(s + 1, (g + 1) % 2, n + 1)
                        n = n + 1
                    p_ev(s)
                    out_add(s, b, g, g % 2, n)

            row_max(0, 0)
            scaled_max(0, 0, base + 1)
            with dve.Fori(0, B - 1) as b:
                att_batch(b)
            att_batch(B - 1, last=True)
            count[0] = base + PER * 4 * B

            dve.wait_ge(q.o_done, 4 * B)
            layer_stats(x)
            normalize(4, x, q.h_ready)
            v = disp1
            logits(2, 1, E1, lg1)
            dve.wait_ge(q.h_stored1, 16 * B)
            diff = v["sk"].rearrange("p (b o) -> p b o", o=1)
            chain(dve.tensor_tensor(diff, lg1[:, :, 1:2], lg1[:, :, 0:1], ALU.subtract))
            oh = v["oh"].rearrange("p (b e) -> p b e", e=E1)
            dve.tensor_scalar(oh[:, :, 1:2], diff, 0.0, None, ALU.is_gt)
            dve.tensor_scalar(oh[:, :, 0:1], diff, 0.0, None, ALU.is_le)
            m1 = v["m"].rearrange("p (b e) -> p b e", e=E1)
            dve.tensor_scalar(m1[:, :, 1:2], diff, 0.0, None, ALU.is_gt)
            dve.tensor_scalar(m1[:, :, 0:1], diff, 0.0, None, ALU.is_le).then_inc(q.ready_m, 1)
            chain(dve.tensor_scalar(v["rf"], v["sk"], -1.0, None, ALU.mult))
            m8 = v["m8"][:, :, 0:1]
            dve.tensor_tensor(m8, diff, v["rf"].rearrange("p (b o) -> p b o", o=1), ALU.min).then_inc(q.ediff_ready, 1)
            dve.wait_ge(q.eexp_ready, 2)
            w1 = wt[:, 0:B]
            chain(dve.tensor_scalar(w1, w1, 1.0, None, ALU.add))
            chain(dve.reciprocal(w1, w1))
            chain(dve.tensor_scalar(w1, w1, gf1, None, ALU.mult))
            sort(1, v, E1, 1, NB1)
            for j in range(NB1):
                dve.wait_ge(q.t1_mm, j + 1)
                dve.tensor_copy(xT1[:, j].rearrange("p k n -> p (k n)"), ps[:, 6 + j % 2, :]).then_inc(q.t1_ev, 1)

            def leak(s, par):
                dve.wait_ge(q.half_done, s + 1)
                dve.tensor_tensor(lk[par], hf[par], ps[:, par, :], ALU.max).then_inc(q.l_done, 1)

            def y_acc(s, j, first):
                dve.wait_ge(q.d1_mm, s + 1)
                if first:
                    dve.tensor_copy(y1[:, j], ps[:, 4 + j % 2, :]).then_inc(q.y1_ev, 1)
                else:
                    dve.tensor_tensor(y1[:, j], y1[:, j], ps[:, 4 + j % 2, :], ALU.add).then_inc(q.y1_ev, 1)

            for j in range(NB1):
                leak(j, j % 2)
                if j >= 2:
                    y_acc(j - 2, j - 2, True)
            for j in range(NB1):
                leak(NB1 + j, j % 2)
                y_acc(NB1 + j - 2, (j - 2) % NB1, j < 2)
            with dve.Fori(2, NCH) as c:
                for j in range(NB1):
                    leak(c * NB1 + j, j % 2)
                    y_acc(c * NB1 + (j - 2), (j - 2) % NB1, False)
            y_acc(NCH * NB1 - 2, NB1 - 2, False)
            y_acc(NCH * NB1 - 1, NB1 - 1, False)
            for t in range(B):
                dve.wait_ge(gath[t], 16 * (B * TOP // 8 + 1))
                dve.scalar_tensor_tensor(out=x[:, t], in0=g1[t], scalar=wt[:, t:t + 1], in1=x[:, t],
                                         op0=ALU.mult, op1=ALU.add).then_inc(q.out_ready, 1)


def kernel(x, ctx_2048, g_xattn, g_ffn, L0_xattn_decay, L0_xattn_W_in, L0_xattn_b_in, L0_xattn_W_out,
           L0_xattn_b_out, L0_xattn_gamma, L0_xattn_beta, L0_ffn_router_w, L0_ffn_gate_w, L0_ffn_up_w,
           L0_ffn_down_w, L1_xattn_W_fc, L1_xattn_b_fc, L1_xattn_W_q, L1_xattn_b_q, L1_xattn_W_k, L1_xattn_b_k,
           L1_xattn_W_v, L1_xattn_b_v, L1_ffn_w_router, L1_ffn_w_fc, L1_ffn_w_proj):
    import ml_dtypes
    from concourse import bacc
    from concourse.bass_utils import run_bass_kernel_spmd

    def split_rows(a):
        k = a.shape[0] // P
        return a.reshape(k, P, -1).transpose(1, 0, 2).reshape(P, -1)

    def across(a, parts):
        return np.broadcast_to(np.asarray(a).reshape(1, -1), (parts, np.asarray(a).size))

    f = {n: np.asarray(a) for n, a in dict(
        x=x, ctx=ctx_2048, win=L0_xattn_W_in, wout=L0_xattn_W_out, wfc=L1_xattn_W_fc, wq=L1_xattn_W_q,
        wk=L1_xattn_W_k, wv=np.asarray(L1_xattn_W_v).reshape(D, D), r0=L0_ffn_router_w, r1=L1_ffn_w_router,
        gate=L0_ffn_gate_w, up=L0_ffn_up_w, down=L0_ffn_down_w, fc=L1_ffn_w_fc, proj=L1_ffn_w_proj).items()}
    cols = np.zeros((P, NCOL), np.float32)
    for at, b in ((C_BIN, L0_xattn_b_in), (C_BFC, L1_xattn_b_fc), (C_BQ, L1_xattn_b_q), (C_BK, L1_xattn_b_k)):
        cols[:, at:at + KD] = np.asarray(b).reshape(KD, P).T
    cols[:, C_GX:C_GX + 2] = across(g_xattn, P)
    cols[:, C_GF:C_GF + 2] = across(g_ffn, P)
    cols[:, C_DEC:C_DEC + 1] = across(L0_xattn_decay, P)
    cols[:, C_PID] = np.arange(P)
    gu = np.concatenate([f["gate"], f["up"]], axis=1)
    gu = gu.transpose(0, 2, 1).reshape(E0, KD, P, 2 * I0).transpose(0, 2, 1, 3).reshape(E0, P, GU)
    dn = f["down"].transpose(0, 2, 1).reshape(E0, 2, IH, D).transpose(0, 2, 1, 3).reshape(E0, IH, 2 * D)
    fc = f["fc"].reshape(E1, NCH, CH, KD, P).transpose(1, 4, 0, 3, 2).reshape(NCH, P, E1, KD * CH)
    pj = f["proj"].reshape(E1, D, NCH, CH // P, P).transpose(2, 4, 0, 3, 1).reshape(NCH, P, E1, KD * CH)
    ch = np.concatenate([fc, pj], axis=3).reshape(NCH, P, RW1)
    sel = np.zeros((B, B, S), np.float32)
    sel[np.arange(B), np.arange(B)] = 1
    iota = np.zeros((P, P + B * TOP), np.float32)
    iota[:, :P] = np.arange(P)
    iota[:, P:] = np.repeat(np.arange(B), TOP)
    arrays = dict(
        x=f["x"].transpose(1, 0, 2).reshape(S, B * D),
        ctx=f["ctx"][:, ::-1].transpose(0, 2, 1).reshape(B, KD, P, T).transpose(0, 2, 1, 3).reshape(B, P, KD * T),
        wfc=split_rows(f["wfc"].T), wq=split_rows(f["wq"].T), wk=split_rows(f["wk"].T), wv=split_rows(f["wv"].T),
        win=split_rows(f["win"].T), wout=split_rows(f["wout"].T), cols=cols,
        gamma=across(L0_xattn_gamma, S), beta=across(L0_xattn_beta, S), bout=across(L0_xattn_b_out, B),
        bv=across(L1_xattn_b_v, S), rw0=split_rows(f["r0"].T), rw1=split_rows(f["r1"].T), gu=gu, dn=dn, ch=ch,
        ident=np.eye(P, dtype=np.float32), sel=sel.reshape(B, B * S), iota=iota,
        tri=np.triu(np.ones((S, S)), 1).astype(ml_dtypes.bfloat16), ones=np.ones((S, P), ml_dtypes.bfloat16))
    nc = bacc.Bacc("TRN2", target_bir_lowering=False, num_devices=1)
    arrays = {"in_" + n: np.ascontiguousarray(a) for n, a in arrays.items()}
    args = [nc.dram_tensor(n, a.shape, mybir.dt.from_np(a.dtype), kind="ExternalInput").ap()
            for n, a in arrays.items()]
    out = nc.dram_tensor("out", (B, S, D), F32, kind="ExternalOutput").ap()
    build(nc, *args, out)
    r = run_bass_kernel_spmd(nc, [arrays], core_ids=[0])
    return r.results[0]["out"]
```

```python
from contextlib import ExitStack

import numpy as np

import concourse.bass as bass
from concourse import mybir

F32 = mybir.dt.float32
BF16 = mybir.dt.bfloat16
I32 = mybir.dt.int32
U32 = mybir.dt.uint32
ACT = mybir.ActivationFunctionType
ALU = mybir.AluOpType
AX = mybir.AxisListType

B, S, T, D = 8, 112, 375, 512
N = B * S
P = 128
KD = D // P
E0, TOP, I0 = 32, 4, 192
E1, HID = 2, 2048
H, DG = 16, 32
TC = T // 3
UB = H // 2
GB = H // 4
EPS = 1e-5
SCALE = 1.0 / float(np.sqrt(DG))
NB0 = (N * TOP + E0 * (P - 1)) // P
NB0 += NB0 % 2
NP0 = NB0 // 2
NPL = E0 // 2
NB1 = (N + E1 * (P - 1)) // P
IH = I0 // 2
CH = 512
NCH = HID // CH
GU = KD * 2 * I0
RW0 = GU + 2 * D
NR0 = 4
RW1 = E1 * 2 * KD * CH

C_BIN, C_BFC, C_BQ, C_BK, C_GX, C_GF, C_DEC, C_PID = 0, 4, 8, 12, 16, 18, 20, 21
NCOL = 24
FILLS = (NB0 - E0) // 4 * 16
T_LAST, T_DONE = 62, 64

A_X = 0
A_K = A_X + B * D
A_V = A_K + B * KD * T
A_W = A_V + 3 * B * D
A_WFC, A_WQ, A_WK, A_WV = (A_W + i * KD * D for i in range(4))
A_SUP = A_WV + KD * D
A_C = A_SUP + KD * T
A_Z = A_C + 2 * KD * D
A_HT = A_Z + B * D
A_FREE = A_HT + KD * N
A_END = A_FREE + RW0
A_RING = [A_FREE, A_C, A_Z + 4 * D + 4 * I0 + 4 * P + 2 * D, A_V + 3 * (B - 2) * D]
A_CST = A_C + 3600
A_G0 = [a + i * D for a in (A_FREE, A_C) for i in range(4)]
A_BV = A_FREE + 4 * D
A_REF = A_WK
A_QT = A_C
A_CH = [A_W, A_K]
A_XT1 = A_K + RW1
A_Y1 = A_XT1 + NB1 * D
A_L1 = A_Y1 + NB1 * D


def build(nc, x_in, ctx_in, wfc_in, wq_in, wk_in, wv_in, win_in, wout_in, cols_in, gamma_in, beta_in,
          bout_in, bv_in, rw0_in, rw1_in, gu_in, dn_in, ch_in, ident_in, sel_in, iota_in, tri_in, ones_in, out):
    h0_dram = nc.dram_tensor("h0_rows", [N, D], F32, kind="Internal").ap()
    y0_dram = nc.dram_tensor("y0_slots", [NB0 * P, D], F32, kind="Internal").ap()
    h1_dram = nc.dram_tensor("h1_rows", [N, D], F32, kind="Internal").ap()
    y1_dram = nc.dram_tensor("y1_slots", [NB1 * P, D], F32, kind="Internal").ap()
    out_rows = out.rearrange("b s d -> s b d")

    with ExitStack() as ctx:
        def sb(name, shape, dt=F32):
            return ctx.enter_context(nc.sbuf_tensor(name, shape, dt))

        def sem(name):
            return ctx.enter_context(nc.semaphore(name))

        arena = sb("arena", [P, A_END])

        def at(off, words, parts=P):
            return arena[0:parts, off:off + words]

        x = at(A_X, B * D, S).rearrange("p (b d) -> p b d", b=B)
        ctxk = at(A_K, B * KD * T).rearrange("p (b k t) -> p b k t", b=B, k=KD)
        vals = at(A_V, 3 * B * D, TC).rearrange("p (c d) -> p c d", d=D)
        wfc, wq, wk, wv = (at(a, KD * D).rearrange("p (k d) -> p k d", k=KD) for a in (A_WFC, A_WQ, A_WK, A_WV))
        sup = at(A_SUP, KD * T).rearrange("p (k t) -> p k t", k=KD)
        w_in = at(A_C, KD * D).rearrange("p (k d) -> p k d", k=KD)
        w_out = at(A_C + KD * D, KD * D).rearrange("p (k d) -> p k d", k=KD)
        z = at(A_Z, B * D, S).rearrange("p (b d) -> p b d", b=B)
        hT = at(A_HT, KD * N).rearrange("p (k n) -> p k n", k=KD)
        gamma = at(A_FREE, D, S)
        beta = at(A_FREE + D, D, S)
        bout = at(A_FREE + 2 * D, D, B)
        sel = at(A_FREE + 3 * D, B * S).rearrange("p (b s) -> p b s", b=B)
        bv = at(A_BV, D, S)
        ones_row = at(A_HT, T)
        k_row = at(A_HT + T, T)
        r_row = at(A_HT + 2 * T, T)
        prod_rows = [at(A_HT + (3 + i) * T, T) for i in range(2)]
        summ = at(A_HT + 5 * T, D)
        zero_rows = at(A_HT + 5 * T + D, D)
        lg0 = at(A_C + RW0, B * E0, S).rearrange("p (b e) -> p b e", b=B)
        z1 = at(A_SUP, D, S)
        hT1 = at(A_SUP + D, KD * S).rearrange("p (k s) -> p k s", k=KD)
        lg1 = at(A_SUP + D + KD * S, B * E1, S).rearrange("p (b e) -> p b e", b=B)
        iota = at(A_CST, P)
        tri = at(A_CST + P, S // 2, S).bitcast(BF16)
        ones_b = at(A_CST + P + S // 2, P // 2, S).bitcast(BF16)
        tile_no = at(A_CST + P + S // 2 + P // 2, B * TOP, S)

        ident = sb("ident", [P, P])
        cols = sb("cols", [P, NCOL])
        gates = sb("gates", [P, 8])
        rw0 = sb("rw0", [P, KD * E0])
        rw1 = sb("rw1", [P, KD * E1])
        stats = sb("stats", [S, B, 6])
        mv = sb("mv", [S, B, 2])
        veps = sb("veps", [S, B])
        mhalf = sb("mhalf", [S, B])
        rstd = sb("rstd", [S, B])
        uT = sb("uT", [P, KD, B])
        s1T = sb("s1T", [P, KD, B])
        bC = sb("bC", [P, KD])
        bq = sb("bq", [P, KD])
        lidx = sb("lidx", [P, NB0 + 2], U32)
        slot_u = sb("slot_u", [S, B * TOP], U32)
        wt = sb("wt", [S, B * TOP])
        table = sb("table", [1, 96], I32)
        table2 = sb("table2", [1, 64], I32)
        idxb = sb("idxb", [P, 2], U32)
        nmx = sb("nmx", [S, 2, 2])
        psum_e = sb("psum_e", [S, 2, 4])
        rinv = sb("rinv", [S, 2, 4])
        ps = ctx.enter_context(nc.psum_tensor("ps", [P, 8, 512], F32))

        names = """ld_kv ld_wk ld_wv ld_ctx1 ld_ctx ld_x ld_sum ld_cst ld_small ld_bv gates_ready u_done kv_mm kv_ev
            ch_ready s1_mm s1_ready sum_mm sum_ready bc_mm y_added beta_ready bv_ready z_ready x_based veps_ready rstd_ready h_ready h_stored
            tr_mm tr_ev lg_mm lg_ev ediff_ready eexp_ready ready_m rank_mm ready_r list_mm list_ready dve_done
            pool_done w_ready x0_landed x1_landed t_mm t_ev u_mm silu_done h_mul h_mm h_ev d_mm y_ev y0_stored y1_stored
            w0_landed w1_landed w2_landed w3_landed gath0 gath1 gath2 gath3 gath4 gath5 gath6 gath7 comb_done
            ref_mm ref_ev rt_mm rt_add qk0_landed qk1_landed s_mm mx_ready e_done pt_mm pt_ev pv_mm o_ev f_mm o_done
            c0_landed c1_landed ln_done dve_seen t1_mm t1_ev u1_mm half_done l_done h1_mm h1_ev d1_mm y1_ev y1_done out_ready out_stored
            lidx_copied idx_seen zeros_ready bq_ready pe_seen zero_ready filled summ_zeroed""".split()
        sems = {n: sem(n) for n in names}
        q = type("Sems", (), sems)

        block = ctx.enter_context(nc.Block())

        def dispatch_views(E, C, NB):
            pairs = B * C
            off = [A_Z]

            def take(words, parts=S):
                a = off[0]
                off[0] += words
                assert off[0] <= A_FREE
                return at(a, words, parts)
            v = {}
            v["m8"] = take(B * 8).rearrange("p (b k) -> p b k", k=8)
            v["i8"] = take(B * 8).bitcast(U32).rearrange("p (b k) -> p b k", k=8)
            v["idf"] = take(pairs)
            v["oh"] = take(pairs * E // 2).bitcast(BF16)
            v["m"] = take(B * E // 2).bitcast(BF16)
            v["slot"] = take(B * E)
            v["pick"] = take(pairs * E)
            v["sk"] = take(pairs)
            v["ski"] = take(pairs).bitcast(I32)
            v["qi"] = take(pairs).bitcast(I32)
            v["ri"] = take(pairs).bitcast(I32)
            v["qf"] = take(pairs)
            v["rf"] = take(pairs)
            v["cnti"] = take(E, P).bitcast(I32)
            v["nb"] = take(E, P)
            v["cum"] = take(E, P)
            v["ones"] = take(E, P)
            v["base"] = take(E, P)
            v["eb"] = take(NB, P)
            v["la"] = take(NB, P)
            v["rm"] = take(pairs * P // 2).bitcast(BF16).rearrange("p (c r) -> p c r", r=P)
            v["qm"] = take(pairs * NB // 2).bitcast(BF16).rearrange("p (c j) -> p c j", j=NB)
            v["q2"] = take(pairs * NB).bitcast(BF16).rearrange("p (c a j) -> p c a j", a=2, j=NB)
            v["cmp"] = v["rm"].rearrange("p c r -> p (c r)")[0:1, 0:NB * E].rearrange("p (j e) -> p j e", e=E)
            v["cmp_ok"] = NB * E <= pairs * P
            return v

        disp0 = dispatch_views(E0, TOP, NB0)
        disp1 = dispatch_views(E1, 1, NB1)
        assert disp0["cmp_ok"] and disp1["cmp_ok"]

        def pair(off, words, parts=P):
            return [at(off + i * words, words, parts) for i in range(2)]
        xg = pair(A_Z, D)
        xT = [a.rearrange("p (k n) -> p k n", k=KD) for a in pair(A_Z + 2 * D, D)]
        sg = pair(A_Z + 4 * D, I0)
        hm = pair(A_Z + 4 * D + 2 * I0, I0)
        hmT = [a.rearrange("p (k n) -> p k n", k=2) for a in pair(A_Z + 4 * D + 4 * I0, 2 * P, IH)]
        yb = pair(A_Z + 4 * D + 4 * I0 + 4 * P, D)
        g0 = [at(a, D, S) for a in A_G0]
        ring = arena[:, :]

        A_AT = A_Z
        prob = [at(A_AT + i * 2 * T, 2 * T, S).rearrange("p (h t) -> p h t", h=2) for i in range(2)]
        pT = at(A_AT + 4 * T, 6 * S, TC).rearrange("p (i s) -> p i s", i=6)
        oT = at(A_AT + 4 * T + 6 * S, S)
        A_VB = A_AT + 4 * T + 7 * S
        vb = [at(A_VB + i * 3 * D, 3 * D, TC).rearrange("p (c d) -> p c d", c=3) for i in range(2)]
        A_KB = A_VB + 6 * D
        kb = [at(A_KB + i * KD * T, KD * T).rearrange("p (k t) -> p k t", k=KD) for i in range(2)]
        A_QB = A_KB + 2 * KD * T
        qb = [at(A_QB + i * 2 * KD * S, 2 * KD * S).rearrange("p (k a s) -> p k a s", k=KD, a=2) for i in range(2)]
        assert A_QB + 4 * KD * S <= A_END
        refT = at(A_REF, KD * N).rearrange("p (k n) -> p k n", k=KD)
        qT = at(A_QT, KD * N).rearrange("p (k n) -> p k n", k=KD)

        xT1 = at(A_XT1, NB1 * D).rearrange("p (j k n) -> p j k n", j=NB1, k=KD)
        y1 = at(A_Y1, NB1 * D).rearrange("p (j d) -> p j d", j=NB1)
        hf = pair(A_L1, CH)
        lk = pair(A_L1 + 2 * CH, CH)
        aT = [a.rearrange("p (k n) -> p k n", k=KD) for a in pair(A_L1 + 4 * CH, CH)]
        xg1 = [y1[:, j] for j in range(NB1)]
        g1 = [at(A_RING[0] - 8 * D + i * D, D, S) for i in range(8)]
        assert A_L1 + 6 * CH <= A_W

        gx0, gx1, gf0, gf1 = (gates[0:S, i:i + 1] for i in range(4))

        def last_pair(eng):
            return eng.value_load(table[0:1, T_LAST:T_LAST + 1], min_val=NPL - 1, max_val=NP0 - 1)

        @block.sync
        def _(sp):
            def load(dst, src, s):
                sp.dma_start(dst, src).then_inc(s, 16)
            load(cols[:], cols_in, q.ld_kv)
            load(wfc, wfc_in.rearrange("p (k d) -> p k d", k=KD), q.ld_kv)
            load(ctxk[:, 0], ctx_in[0].rearrange("p (k t) -> p k t", k=KD), q.ld_kv)
            load(wk, wk_in.rearrange("p (k d) -> p k d", k=KD), q.ld_wk)
            load(wv, wv_in.rearrange("p (k d) -> p k d", k=KD), q.ld_wv)
            load(x, x_in.rearrange("p (b d) -> p b d", b=B), q.ld_x)
            load(ctxk[:, 1], ctx_in[1].rearrange("p (k t) -> p k t", k=KD), q.ld_ctx1)
            for b in range(2, B):
                load(ctxk[:, b], ctx_in[b].rearrange("p (k t) -> p k t", k=KD), q.ld_ctx)
            load(w_in, win_in.rearrange("p (k d) -> p k d", k=KD), q.ld_sum)
            load(w_out, wout_in.rearrange("p (k d) -> p k d", k=KD), q.ld_sum)
            load(gamma, gamma_in, q.ld_sum)
            load(beta, beta_in, q.ld_sum)
            load(bout, bout_in, q.ld_sum)
            load(sel, sel_in.rearrange("p (b s) -> p b s", b=B), q.ld_sum)
            load(ident[:], ident_in, q.ld_small)
            load(rw0[:], rw0_in, q.ld_small)
            load(rw1[:], rw1_in, q.ld_small)
            load(wq, wq_in.rearrange("p (k d) -> p k d", k=KD), q.ld_small)
            sp.wait_ge(q.zero_ready, 1)
            slots = y0_dram.rearrange("(j p) d -> p j d", p=P)
            zeros4 = zero_rows.rearrange("p (o d) -> p o d", o=1).to_broadcast([P, 4, D])
            for j in range(E0, NB0, 4):
                sp.dma_start(slots[:, j:j + 4], zeros4).then_inc(q.filled, 16)
            sp.wait_ge(q.sum_mm, 1)
            load(iota, iota_in[:, 0:P], q.ld_cst)
            load(tile_no, iota_in[0:S, P:P + B * TOP], q.ld_cst)
            load(tri, tri_in, q.ld_cst)
            load(ones_b, ones_in, q.ld_cst)
            for t in range(B):
                sp.wait_ge(q.h_ready, t + 1)
                sp.dma_start(h0_dram[t * S:(t + 1) * S, :], z[:, t]).then_inc(q.h_stored, 16)

            landed = [q.w0_landed, q.w1_landed, q.w2_landed, q.w3_landed]

            def load_expert(e, slot):
                dst = at(A_RING[slot], GU)
                sp.dma_start(dst, gu_in[bass.ds(e, 1)].rearrange("e p n -> (e p) n")).then_inc(landed[slot], 16)
                dst = at(A_RING[slot] + GU, 2 * D, IH)
                sp.dma_start(dst, dn_in[bass.ds(e, 1)].rearrange("e p n -> (e p) n")).then_inc(landed[slot], 16)

            load_expert(0, 0)
            load_expert(1, 1)
            load_expert(3, 3)
            sp.wait_ge(q.list_ready, 1)
            load_expert(2, 2)
            for e in range(NR0 - 1):
                sp.wait_ge(landed[e], 32)
                sp.sem_inc(q.w_ready, 1)

            def next_expert(e, slot, rounds):
                ahead = (slot + NR0 - 1) % NR0
                sp.wait_ge(landed[ahead], rounds)
                sp.sem_inc(q.w_ready, 1)
                done = sp.value_load(table[0:1, bass.ds(e + T_DONE, 1)], min_val=2, max_val=NB0 + 1)
                sp.wait_ge(q.d_mm, done)
                load_expert(e + NR0, slot)

            with sp.Fori(0, (E0 - NR0) // NR0) as i:
                for slot in range(NR0):
                    next_expert(i * NR0 + slot, slot, i * 32 + (32 if slot == 0 else 64))
            for e in range((E0 - NR0) // NR0 * NR0, E0 - NR0):
                next_expert(e, e % NR0, 32 * ((e + NR0 - 1) // NR0 + 1))
            sp.wait_ge(landed[(E0 - 1) % NR0], 32 * ((E0 - 1) // NR0 + 1))
            sp.sem_inc(q.w_ready, 1)

            sp.wait_ge(q.d_mm, last_pair(sp) * 2 + 3)
            load(bv, bv_in, q.ld_bv)

            def load_chunk(c, slot, s):
                for a in range(4):
                    w = RW1 // 4
                    sp.dma_start(at(A_CH[slot] + a * w, w), ch_in[c, :, a * w:(a + 1) * w]).then_inc(s, 16)

            staged = (q.qk0_landed, q.qk1_landed)

            def stage_kv(b, par):
                s = staged[par]
                sp.dma_start(kb[par], ctxk[:, bass.ds(b, 1)].rearrange("p b k t -> p (b k) t")).then_inc(s, 16)
                sp.dma_start(vb[par], vals[:, bass.ds(b * 3, 3)]).then_inc(s, 16)

            def stage_q(b, par):
                s = staged[par]
                for h in range(4):
                    rows = slice(h * DG, (h + 1) * DG)
                    sp.dma_start(qb[par][rows, :, h % 2], qT[rows, :, bass.ds(b * S, S)]).then_inc(s, 16)

            sp.wait_ge(q.ref_mm, 8)
            sp.wait_ge(q.kv_ev, 11 * B)
            stage_kv(0, 0)
            stage_kv(1, 1)
            sp.wait_ge(q.ref_ev, 12)
            sp.wait_ge(q.zeros_ready, 1)
            stage_q(0, 0)
            stage_q(1, 1)
            sp.wait_ge(q.ref_ev, 16)
            sp.wait_ge(q.rt_mm, B)
            load_chunk(0, 0, q.c0_landed)

            def store_normalized(b):
                sp.wait_ge(q.h_ready, b + (2 * B + 1))
                sp.dma_start(h1_dram[bass.ds(b * S, S), :], z1).then_inc(q.h_stored, 16)

            with sp.Fori(1, B // 2) as i:
                for par in range(2):
                    sp.wait_ge(q.pv_mm, i * (2 * UB) + (par - 1) * UB)
                    stage_kv(i * 2 + par, par)
                    stage_q(i * 2 + par, par)
                    store_normalized(i * 2 + (par - 2))
            for b in range(B - 2, B):
                store_normalized(b)
            sp.wait_ge(q.o_done, GB * B + 2)
            load_chunk(1, 1, q.c1_landed)
            chunk_landed = (q.c0_landed, q.c1_landed)
            for c in range(NCH):
                sp.wait_ge(chunk_landed[c % 2], 64 * (c // 2 + 1))
                sp.sem_inc(q.ch_ready, 1)
                if c >= 1 and c + 1 < NCH:
                    sp.wait_ge(q.d1_mm, NB1 * c)
                    load_chunk(c + 1, (c + 1) % 2, chunk_landed[(c + 1) % 2])
            for j in range(NB1):
                sp.wait_ge(q.y1_ev, NB1 * (NCH - 1) + j + 1)
                sp.dma_start(y1_dram[j * P:(j + 1) * P, :], y1[:, j]).then_inc(q.y1_done, 16)
            for t in range(B):
                sp.wait_ge(q.out_ready, t + 1)
                sp.dma_start(out_rows[:, t], x[:, t]).then_inc(q.out_stored, 16)
            sp.wait_ge(q.out_stored, 16 * B)

        @block.gpsimd
        def _(pool):
            pool.memset(zero_rows, 0.0).then_inc(q.zero_ready, 1)
            pool.memset(summ, 0.0).then_inc(q.summ_zeroed, 1)
            pool.memset(mhalf[:], -0.5).then_inc(q.pool_done, 1)
            pool.wait_ge(q.pool_done, 1)

            def root(n):
                pool.wait_ge(q.veps_ready, n + 1)
                pool.tensor_tensor(rstd[:], veps[:], mhalf[:], ALU.pow).then_inc(q.rstd_ready, 1)

            root(0)
            pool.wait_ge(q.beta_ready, 1)
            for t in range(B):
                pool.tensor_tensor(x[:, t], x[:, t], beta, ALU.add).then_inc(q.x_based, 1)
            root(1)
            root(2)

            landed = (q.x0_landed, q.x1_landed)

            def token_column(j, par):
                pool.tensor_copy(idxb[:, par:par + 1], lidx[:, bass.ds(j, 1)]).then_inc(q.lidx_copied, 1)

            def gather(par, bufs, rows):
                pool.indirect_dma_start(out=bufs[par], out_offset=None, in_=rows,
                                        in_offset=bass.IndirectOffsetOnAxis(ap=idxb[:, par:par + 1], axis=0)
                                        ).then_inc(landed[par], 16)

            pool.wait_ge(q.list_ready, 1)
            pool.wait_ge(q.h_stored, 16 * B)
            for par in range(2):
                token_column(par, par)
                pool.wait_ge(q.lidx_copied, par + 1)
                gather(par, xg, h0_dram)

            def gather_pair(i):
                for par in range(2):
                    pool.wait_ge(q.t_mm, i * 2 + (par - 1))
                    token_column(i * 2 + par, par)
                    pool.wait_ge(q.lidx_copied, i * 2 + (par + 1))
                    pool.sem_inc(q.idx_seen, 1)
                    gather(par, xg, h0_dram)

            last = last_pair(pool)
            with pool.Fori(1, NPL + 1) as i:
                gather_pair(i)
            with pool.Fori(NPL + 1, NP0 + 1) as i:
                with pool.If(last >= i - 1):
                    gather_pair(i)
            for par in range(2):
                pool.wait_ge(landed[par], last * 16 + 32)

            gath = [q.gath0, q.gath1, q.gath2, q.gath3, q.gath4, q.gath5, q.gath6, q.gath7]
            pool.wait_ge(q.y0_stored, last * 16 + 16)
            pool.wait_ge(q.y1_stored, last * 16 + 16)
            pool.sem_inc(q.idx_seen, 1)
            for n in range(B * TOP):
                if n >= 8:
                    pool.wait_ge(q.comb_done, n - 7)
                pool.indirect_dma_start(out=g0[n % 8], out_offset=None, in_=y0_dram,
                                        in_offset=bass.IndirectOffsetOnAxis(ap=slot_u[:, n:n + 1], axis=0)
                                        ).then_inc(gath[n % 8], 16)
            root(3)
            pool.wait_ge(q.bv_ready, 1)
            for t in range(B):
                pool.tensor_tensor(x[:, t], x[:, t], bv, ALU.add).then_inc(q.x_based, 1)
            pool.wait_ge(q.x_based, 2 * B)
            pool.memset(at(A_QB, 4 * KD * S), 0.0).then_inc(q.zeros_ready, 1)
            with pool.Fori(0, B) as b:
                pool.wait_ge(q.veps_ready, b + 5)
                pool.tensor_tensor(rstd[:, 0:1], veps[:, 0:1], mhalf[:, 0:1], ALU.pow).then_inc(q.rstd_ready, 1)
            pool.wait_ge(q.list_ready, 2)
            pool.wait_ge(q.h_stored, 16 * 2 * B)
            for j in range(NB1):
                pool.indirect_dma_start(out=xg1[j], out_offset=None, in_=h1_dram,
                                        in_offset=bass.IndirectOffsetOnAxis(ap=lidx[:, j:j + 1], axis=0)
                                        ).then_inc(gath[j], 16)
            pool.wait_ge(q.y1_done, 16 * NB1)
            for t in range(B):
                pool.indirect_dma_start(out=g1[t], out_offset=None, in_=y1_dram,
                                        in_offset=bass.IndirectOffsetOnAxis(ap=slot_u[:, t:t + 1], axis=0)
                                        ).then_inc(gath[t], 16)

        @block.scalar
        def _(act):
            act.wait_ge(q.ld_kv, 48)
            act.activation(gates[:, 4:5], cols[:, C_DEC:C_DEC + 1], ACT.Sigmoid).then_inc(q.gates_ready, 1)
            act.activation(gates[:, 0:4], cols[:, C_GX:C_GX + 4], ACT.Tanh).then_inc(q.gates_ready, 1)

            def kv(b):
                bank = [0, 1, 2, 3, 4, 5, 0, 1, 2, 3, 4]
                for n in range(11):
                    act.wait_ge(q.kv_mm, b * 11 + (n + 1))
                    src = ps[:, bank[n], 0:T]
                    if n < KD:
                        ins = act.activation(sup[:, n], src, ACT.Relu, bias=cols[:, C_BFC + n:C_BFC + n + 1])
                    elif n < 2 * KD:
                        m = n - KD
                        if m == 0:
                            act.wait_ge(q.u_done, b * KD + KD)
                        ins = act.activation(ctxk[:, bass.ds(b, 1), m].rearrange("p b t -> p (b t)"), src,
                                             ACT.Identity, bias=cols[:, C_BK + m:C_BK + m + 1])
                    else:
                        c = n - 2 * KD
                        ins = act.activation(vals[:, bass.ds(b * 3 + c, 1)].rearrange("p b t -> p (b t)"),
                                             ps[0:TC, bank[n], :], ACT.Copy, scale=gates[0:TC, 1:2])
                    ins.then_inc(q.kv_ev, 1)

            for b in range(2):
                kv(b)
            with act.Fori(2, 5) as b:
                kv(b)
            act.wait_ge(q.ediff_ready, 1)
            d = disp0["m8"][:, :, 0:TOP]
            act.activation(wt[:].rearrange("p (b k) -> p b k", b=B), d, ACT.Exp).then_inc(q.eexp_ready, 1)
            kv(5)

            stored = (q.y0_stored, q.y1_stored)

            def silu(j, par):
                act.wait_ge(q.u_mm, j + 1)
                act.activation(sg[par], ps[:, 2 + par, 0:I0], ACT.Silu).then_inc(q.silu_done, 1)

            def y_out(j, par, i):
                act.wait_ge(q.d_mm, j + 2)
                if i is not None:
                    act.wait_ge(stored[par], i * 16)
                act.activation(yb[par], ps[:, 6 + par, :], ACT.Copy).then_inc(q.y_ev, 1)
                act.wait_ge(q.y_ev, j + 1)
                act.dma_start(y0_dram[bass.ds(j * P, P), :], yb[par]).then_inc(stored[par], 16)

            act.wait_ge(q.filled, FILLS)
            silu(0, 0)
            silu(1, 1)
            for par in range(2):
                silu(2 + par, par)
                y_out(par, par, None)

            def act_pair(i):
                for par in range(2):
                    silu(i * 2 + par, par)
                    y_out(i * 2 + (par - 2), par, i - 1)

            last = last_pair(act)
            with act.Fori(2, NPL) as i:
                act_pair(i)
            with act.Fori(NPL, NP0) as i:
                with act.If(last >= i):
                    act_pair(i)
            for par in range(2):
                y_out(last * 2 + par, par, last)

            with act.Fori(6, B) as b:
                kv(b)
            act.wait_ge(q.bq_ready, 1)
            for n in range(16):
                act.wait_ge(q.ref_mm, n + 1)
                m, half = n % 4, n // 4 % 2
                dst = (refT if n < 8 else qT)[:, m, half * 448:half * 448 + 448]
                bias = cols[:, C_BFC + m:C_BFC + m + 1] if n < 8 else bq[:, m:m + 1]
                act.activation(dst, ps[:, n % 4, 0:448], ACT.Relu if n < 8 else ACT.Identity,
                               bias=bias, scale=1.0 if n < 8 else SCALE).then_inc(q.ref_ev, 1)

            def exps(u, par, place):
                act.wait_ge(q.mx_ready, u + 1)
                for h in range(2):
                    ins = act.activation(prob[par][:, h], ps[0:S, 2 * par + h, 0:T], ACT.Exp,
                                         bias=nmx[:, par, h:h + 1],
                                         accum_out=psum_e[:, place // 2, place % 2 + 2 * h:place % 2 + 2 * h + 1])
                ins.then_inc(q.e_done, 1)

            def out_rows(u, grp, bank):
                act.wait_ge(q.pv_mm, u + 1)
                act.activation(oT, ps[:, bank, 0:S], ACT.Copy).then_inc(q.o_ev, 1)

            def exp_unit(u, n, grp, b=None):
                exps(u, n % 2, n % 4)
                if n % 2 == 0 and grp is not None:
                    out_rows(u - 1, grp, 6 + (n // 2 - 1) % 2)
                if n == 6 and b is not None:
                    turned_rows(b - 1, 7)

            def turned_rows(b, bank):
                act.wait_ge(q.tr_mm, b + (2 * B + 1))
                act.activation(hT1.rearrange("p k s -> p (k s)"), ps[:, bank, 0:KD * S], ACT.Copy).then_inc(q.tr_ev, 1)

            for n in range(UB):
                exp_unit(n, n, n // 2 - 1 if n >= 2 else None)
            with act.Fori(1, B) as b:
                for n in range(UB):
                    exp_unit(b * UB + n, n, b * GB + (n // 2 - 1), b)
            out_rows(UB * B - 1, GB * B - 1, 7)
            turned_rows(B - 1, 7)

            act.wait_ge(q.ediff_ready, 2)
            act.activation(wt[:, 0:B], disp1["m8"][:, :, 0:1].rearrange("p b k -> p (b k)"), ACT.Exp
                           ).then_inc(q.eexp_ready, 1)

            def l1(c, j):
                s = c * NB1 + j
                act.wait_ge(q.u1_mm, s + 1)
                act.activation(hf[j % 2], ps[:, j % 2, :], ACT.Copy, scale=0.5).then_inc(q.half_done, 1)

            def l1_sq(s, par):
                act.wait_ge(q.h1_mm, s + 1)
                act.activation(aT[par].rearrange("p k n -> p (k n)"), ps[:, 2 + par, :], ACT.Square
                               ).then_inc(q.h1_ev, 1)

            l1(0, 0)
            for j in range(1, NB1):
                l1(0, j)
                l1_sq(j - 1, (j - 1) % 2)
            with act.Fori(1, NCH) as c:
                for j in range(NB1):
                    l1(c, j)
                    l1_sq(c * NB1 + (j - 1), (j - 1) % 2)
            l1_sq(NB1 * NCH - 1, 1)

        @block.tensor
        def _(pe):
            def kv(b, between=None):
                bank = [0, 1, 2, 3, 4, 5, 0, 1, 2, 3, 4]
                last = [7, 8, 9, 10, 11, 6]
                first = isinstance(b, int) and b == 0
                for n in range(11):
                    if n == 2 * KD and between:
                        between()
                    if n >= 6:
                        pe.wait_ge(q.kv_ev, b * 11 + (n - 5))
                    elif not first:
                        pe.wait_ge(q.kv_ev, b * 11 + (last[n] - 11))
                    for k in range(KD):
                        if n < KD:
                            o = ps[:, bank[n], 0:T]
                            w = wfc[:, k, n * P:(n + 1) * P]
                            r = ctxk[:, bass.ds(b, 1), k].rearrange("p b t -> p (b t)")
                        else:
                            if first and k == 0 and n in (KD, 2 * KD):
                                pe.wait_ge(q.ld_wk if n == KD else q.ld_wv, 16)
                            if n == KD:
                                pe.wait_ge(q.kv_ev, b * 11 + (k + 1))
                            if n < 2 * KD:
                                m = n - KD
                                o, w, r = ps[:, bank[n], 0:T], wk[:, k, m * P:(m + 1) * P], sup[:, k]
                            else:
                                c = n - 2 * KD
                                o, w, r = ps[0:TC, bank[n], :], sup[:, k, c * TC:(c + 1) * TC], wv[:, k]
                        ins = pe.matmul(o, w, r, start=(k == 0), stop=(k == KD - 1))
                    ins.then_inc(q.kv_mm, 1)

            def summary():
                pe.wait_ge(q.ld_sum, 96)
                pe.wait_ge(q.u_done, KD * B)
                for m in range(KD):
                    for k in range(KD):
                        ins = pe.matmul(ps[:, 6, m * B:(m + 1) * B], w_in[:, k, m * P:(m + 1) * P], uT[:, k],
                                        start=(k == 0), stop=(k == KD - 1))
                ins.then_inc(q.s1_mm, 1)
                pe.wait_ge(q.s1_ready, 1)
                for k in range(KD):
                    ins = pe.matmul(ps[0:B, 7, :], s1T[:, k], w_out[:, k], start=(k == 0), stop=(k == KD - 1))
                ins.then_inc(q.sum_mm, 1)
                pe.wait_ge(q.sum_ready, 1)
                for t in range(B):
                    if t >= 2:
                        pe.wait_ge(q.y_added, t - 1)
                    pe.matmul(ps[0:S, 6 + t % 2, :], sel[:, t], summ, start=True, stop=True).then_inc(q.bc_mm, 1)

            def transposes(n, t):
                pe.wait_ge(q.h_ready, n * B + t + 1)
                for k in range(KD):
                    ins = pe.transpose(ps[:, 6 + t % 2, k * S:(k + 1) * S], z[:, t, k * P:(k + 1) * P], ident[0:S, 0:S])
                ins.then_inc(q.tr_mm, 1)

            def routed(n, m, rw, E):
                for t in range(B + 1):
                    if t < B:
                        if t >= 2:
                            pe.wait_ge(q.lg_ev, m * B + t - 1)
                        transposes(n, t)
                    if t >= 1:
                        u = t - 1
                        pe.wait_ge(q.tr_ev, n * B + u + 1)
                        for k in range(KD):
                            ins = pe.matmul(ps[0:S, 6 + u % 2, 448:448 + E], hT[:, k, u * S:(u + 1) * S],
                                            rw[:, k * E:(k + 1) * E], start=(k == 0), stop=(k == KD - 1))
                        ins.then_inc(q.lg_mm, 1)

            def ranks(n, v, E):
                pe.wait_ge(q.ready_m, n + 1)
                mm = v["m"].rearrange("p (b e) -> p b e", b=B)
                pe.matmul(ps[0:S, 6, 0:B * E], tri, v["m"], start=True, stop=False)
                for t in range(B - 1):
                    ins = pe.matmul(ps[0:S, 6, (t + 1) * E:B * E].rearrange("p (b e) -> p b e", e=E), ones_b[:, 0:S],
                                    mm[:, t:t + 1].to_broadcast([S, B - 1 - t, E]), start=False, stop=(t == B - 2))
                for t in range(B):
                    ins = pe.matmul(ps[:, 7, 0:E], ones_b, mm[:, t], start=(t == 0), stop=(t == B - 1))
                ins.then_inc(q.rank_mm, 1)

            def token_list(n, v, pairs, NB):
                pe.wait_ge(q.ready_r, n + 1)
                for c in range(pairs):
                    ins = pe.matmul(ps[:, 6, 0:2 * NB], v["rm"][:, c], v["q2"][:, c].rearrange("p a j -> p (a j)"),
                                    start=(c == 0), stop=(c == pairs - 1))
                ins.then_inc(q.list_mm, 1)

            pe.wait_ge(q.ld_kv, 48)
            kv(0)
            pe.wait_ge(q.ld_ctx1, 16)
            kv(1)
            pe.wait_ge(q.ld_ctx, 16 * (B - 2))
            summary()
            with pe.Fori(2, 4) as b:
                kv(b)
            pe.wait_ge(q.ld_small, 64)
            routed(0, 0, rw0, E0)
            pe.wait_ge(q.ld_cst, 64)
            kv(4, between=lambda: ranks(0, disp0, E0))
            kv(5, between=lambda: token_list(0, disp0, B * TOP, NB0))

            landed = (q.x0_landed, q.x1_landed)

            def blk_t(j, par, i):
                pe.wait_ge(landed[par], i * 16 + 16)
                if not isinstance(j, int) or j >= 2:
                    pe.wait_ge(q.t_ev, j - 1)
                for k in range(KD):
                    ins = pe.transpose(ps[:, par, k * P:(k + 1) * P], xg[par][:, k * P:(k + 1) * P], ident[:])
                ins.then_inc(q.t_mm, 1)

            pe.sem_inc(q.d_mm, 1)

            def blk_up(j, par, off):
                pe.wait_ge(q.t_ev, j + 1)
                if not isinstance(j, int) or j >= 2:
                    pe.wait_ge(q.h_mul, j - 1)
                for k in range(KD):
                    ins = pe.matmul(ps[:, 2 + par, 0:2 * I0], xT[par][:, k], ring[:, bass.ds(off + k * 2 * I0, 2 * I0)],
                                    start=(k == 0), stop=(k == KD - 1))
                ins.then_inc(q.u_mm, 1)

            def blk_h(j, par):
                pe.wait_ge(q.h_mul, j + 1)
                if not isinstance(j, int) or j >= 2:
                    pe.wait_ge(q.h_ev, j - 1)
                for k in range(2):
                    ins = pe.transpose(ps[0:IH, 4 + par, k * P:(k + 1) * P], hm[par][:, k * IH:(k + 1) * IH], ident[:])
                ins.then_inc(q.h_mm, 1)

            def blk_d(j, par, off, free=None):
                pe.wait_ge(q.h_ev, j + 1)
                if free is not None:
                    pe.wait_ge(q.y_ev, free)
                elif not isinstance(j, int) or j >= 2:
                    pe.wait_ge(q.y_ev, j - 1)
                for k in range(2):
                    ins = pe.matmul(ps[:, 6 + par, :], hmT[par][:, k], ring[0:IH, bass.ds(off + GU + k * D, D)],
                                    start=(k == 0), stop=(k == 1))
                ins.then_inc(q.d_mm, 1)

            def place(j):
                return pe.value_load(table2[0:1, bass.ds(j, 1)], min_val=min(A_RING), max_val=max(A_RING))

            def step(j, par, i, h=True, d=True):
                e = pe.value_load(table[0:1, bass.ds(j, 1)], min_val=0, max_val=E0 - 1)
                off = place(j)
                pe.wait_ge(q.w_ready, e + 1)
                blk_up(j, par, off)
                if h:
                    blk_h(j - 1, 1 - par)
                blk_t(j + 1, 1 - par, i + par)
                if d:
                    blk_d(j - 2, par, place(j - 2))

            pe.wait_ge(q.list_ready, 1)
            pe.wait_ge(q.kv_ev, 11 * 6)
            blk_t(0, 0, 0)
            step(0, 0, 0, h=False, d=False)
            step(1, 1, 0, d=False)
            step(2, 0, 1)
            step(3, 1, 1)
            last = last_pair(pe)
            with pe.Fori(2, NPL) as i:
                for par in range(2):
                    step(i * 2 + par, par, i)
            with pe.Fori(NPL, NP0) as i:
                with pe.If(last >= i):
                    for par in range(2):
                        step(i * 2 + par, par, i)
            blk_h(last * 2 + 1, 1)
            for par in range(2):
                blk_d(last * 2 + par, par, place(last * 2 + par), free=last * 2 + par)

            pe.wait_ge(q.silu_done, last * 2 + 2)
            pe.wait_ge(q.h_mul, last * 2 + 2)
            pe.wait_ge(q.h_ev, last * 2 + 2)
            pe.wait_ge(q.t_ev, last * 2 + 3)
            pe.sem_inc(q.pe_seen, 1)
            with pe.Fori(6, B) as b:
                kv(b)
            pe.wait_ge(q.kv_ev, 11 * B)
            for t in range(B):
                if t >= 2:
                    pe.wait_ge(q.tr_ev, B + t - 1)
                transposes(1, t)
            pe.wait_ge(q.tr_ev, 2 * B)
            for n in range(16):
                m, half = n % 4, n // 4 % 2
                if n >= 4:
                    pe.wait_ge(q.ref_ev, n - 3)
                if n == 12:
                    pe.wait_ge(q.ref_ev, 8)
                w, r = (wfc, hT) if n < 8 else (wq, refT)
                for k in range(KD):
                    ins = pe.matmul(ps[:, n % 4, 0:448], w[:, k, m * P:(m + 1) * P], r[:, k, half * 448:half * 448 + 448],
                                    start=(k == 0), stop=(k == KD - 1))
                ins.then_inc(q.ref_mm, 1)
            for t in range(B):
                if t >= 2:
                    pe.wait_ge(q.rt_add, t - 1)
                for k in range(KD):
                    ins = pe.transpose(ps[0:S, 4 + t % 2, k * P:(k + 1) * P], refT[:, k, t * S:(t + 1) * S], ident[:])
                ins.then_inc(q.rt_mm, 1)

            landed_qk = (q.qk0_landed, q.qk1_landed)

            def scores(u, b2, par, n):
                if n == 0:
                    pe.wait_ge(landed_qk[par], b2 * 96 + 96)
                if not isinstance(u, int) or u >= 2:
                    pe.wait_ge(q.e_done, u - 1)
                for h in range(2):
                    g, rows = n // 2, slice(h * 2 * DG, (h + 1) * 2 * DG)
                    ins = pe.matmul(ps[0:S, 2 * (n % 2) + h, 0:T], qb[par][rows, g, n % 2], kb[par][rows, g],
                                    start=True, stop=True)
                ins.then_inc(q.s_mm, 1)

            def turn_probs(u, n):
                pe.wait_ge(q.e_done, u + 1)
                if not isinstance(u, int) or u >= 1:
                    pe.wait_ge(q.pt_ev, u)
                for i in range(6):
                    c, h = i // 2, i % 2
                    ins = pe.transpose(ps[0:TC, 4 + i // 3, (i % 3) * S:(i % 3 + 1) * S],
                                       prob[n % 2][:, h, c * TC:(c + 1) * TC], ident[0:S, 0:S])
                ins.then_inc(q.pt_mm, 1)

            def weigh(u, grp, par, n):
                pe.wait_ge(q.pt_ev, u + 1)
                if n % 2 == 0:
                    pe.wait_ge(q.o_done, grp + 1)
                bank = 6 + n // 2 % 2
                for h in range(2):
                    lo = (n % 2 + 2 * h) * DG
                    hd = n // 2 * 4 + n % 2 + 2 * h
                    for c in range(3):
                        ins = pe.matmul(ps[lo:lo + DG, bank, 0:S], vb[par][:, c, hd * DG:(hd + 1) * DG],
                                        pT[:, 2 * c + h], start=(c == 0), stop=(c == 2))
                ins.then_inc(q.pv_mm, 1)

            def turn_out(grp, n):
                pe.wait_ge(q.o_ev, grp + 1)
                pe.transpose(ps[0:S, 6 + n // 2 % 2, P:2 * P], oT, ident[:]).then_inc(q.f_mm, 1)

            def turn_rows(b):
                pe.wait_ge(q.h_ready, b + (2 * B + 1))
                for k in range(KD):
                    ins = pe.transpose(ps[:, 7, k * S:(k + 1) * S], z1[:, k * P:(k + 1) * P], ident[0:S, 0:S])
                ins.then_inc(q.tr_mm, 1)

            def router_rows(b):
                pe.wait_ge(q.tr_ev, b + (2 * B + 1))
                for k in range(KD):
                    ins = pe.matmul(ps[0:S, 6, 448:448 + E1], hT1[:, k], rw1[:, k * E1:(k + 1) * E1],
                                    start=(k == 0), stop=(k == KD - 1))
                ins.then_inc(q.lg_mm, 1)

            def att_pair(i, last=False):
                for par in range(2):
                    for n in range(UB):
                        u = i * (2 * UB) + (par * UB + n)
                        grp = i * (2 * GB) + (par * GB + n // 2)
                        over = last and par == 1
                        b = i * 2 + par
                        route = not (isinstance(i, int) and i == 0 and par == 0)
                        if n + 2 < UB:
                            scores(u + 2, i, par, n + 2)
                        elif not over:
                            scores(u + 2, i + par, 1 - par, n + 2 - UB)
                        if route and n == 0:
                            pe.wait_ge(q.lg_ev, b + (B - 1))
                        if route and n == 6:
                            pe.wait_ge(q.tr_ev, b + 2 * B)
                        weigh(u, grp, par, n)
                        if not (over and n == UB - 1):
                            turn_probs(u + 1, (n + 1) % UB)
                        if route and n in (4, 6):
                            pe.wait_ge(q.o_done, grp + 2)
                            (turn_rows if n == 4 else router_rows)(b - 1)
                        if n % 2:
                            turn_out(grp, n)

            pe.wait_ge(q.ref_ev, 16)
            pe.sem_inc(q.o_done, 2)
            scores(0, 0, 0, 0)
            scores(1, 0, 0, 1)
            pe.wait_ge(q.rt_add, B)
            turn_probs(0, 0)
            att_pair(0)
            with pe.Fori(1, B // 2 - 1) as i:
                att_pair(i)
            att_pair(B // 2 - 1, last=True)

            pe.wait_ge(q.o_done, GB * B + 2)
            turn_rows(B - 1)
            pe.wait_ge(q.lg_ev, 2 * B - 1)
            router_rows(B - 1)
            ranks(1, disp1, E1)
            token_list(1, disp1, B, NB1)
            pe.wait_ge(q.list_ready, 2)

            def block_rows(j):
                pe.wait_ge((q.gath0, q.gath1, q.gath2, q.gath3, q.gath4, q.gath5, q.gath6, q.gath7)[j],
                           16 * (B * TOP // 8 + 1))
                if j >= 2:
                    pe.wait_ge(q.t1_ev, j - 1)
                for k in range(KD):
                    ins = pe.transpose(ps[:, 6 + j % 2, k * P:(k + 1) * P], xg1[j][:, k * P:(k + 1) * P], ident[:])
                ins.then_inc(q.t1_mm, 1)

            places = []

            def up1(s, c, j):
                if j == 0:
                    pe.wait_ge(q.ch_ready, c + 1)
                if not isinstance(s, int) or s >= 2:
                    pe.wait_ge(q.l_done, s - 1)
                off = places[j] * (RW1 // E1) + chunk_base(c)
                for k in range(KD):
                    ins = pe.matmul(ps[:, j % 2, :], xT1[:, j, k], ring[:, bass.ds(off + k * CH, CH)],
                                    start=(k == 0), stop=(k == KD - 1))
                ins.then_inc(q.u1_mm, 1)

            def turn1(s, j):
                pe.wait_ge(q.l_done, s + 1)
                if not isinstance(s, int) or s >= 2:
                    pe.wait_ge(q.h1_ev, s - 1)
                for k in range(KD):
                    ins = pe.transpose(ps[:, 2 + j % 2, k * P:(k + 1) * P], lk[j % 2][:, k * P:(k + 1) * P], ident[:])
                ins.then_inc(q.h1_mm, 1)

            def down1(s, c, j):
                pe.wait_ge(q.h1_ev, s + 1)
                if not isinstance(s, int) or s >= 2:
                    pe.wait_ge(q.y1_ev, s - 1)
                off = places[j] * (RW1 // E1) + chunk_base(c) + KD * CH
                for k in range(KD):
                    ins = pe.matmul(ps[:, 4 + j % 2, :], aT[j % 2][:, k], ring[:, bass.ds(off + k * D, D)],
                                    start=(k == 0), stop=(k == KD - 1))
                ins.then_inc(q.d1_mm, 1)

            def chunk_base(c):
                return (c % 2) * (A_CH[1] - A_CH[0]) + A_CH[0]

            def chunk_steps(c, first=False):
                for j in range(NB1):
                    s = c * NB1 + j
                    if first:
                        pe.wait_ge(q.t1_ev, j + 1)
                        places.append(pe.value_load(table[0:1, j:j + 1], min_val=0, max_val=E1 - 1))
                    up1(s, c, j)
                    if first and j + 2 < NB1:
                        block_rows(j + 2)
                    if not first or j >= 1:
                        turn1(s - 1, (j - 1) % NB1)
                    if not first or j >= 2:
                        down1(s - 2, c if j >= 2 else c - 1, (j - 2) % NB1)

            block_rows(0)
            block_rows(1)
            chunk_steps(0, first=True)
            with pe.Fori(1, NCH) as c:
                chunk_steps(c)
            s = NCH * NB1
            turn1(s - 1, NB1 - 1)
            down1(s - 2, NCH - 1, NB1 - 2)
            down1(s - 1, NCH - 1, NB1 - 1)

        @block.vector
        def _(dve):
            count = [0]

            def chain(ins):
                count[0] += 1
                ins.then_inc(q.dve_done, 1)
                dve.wait_ge(q.dve_done, count[0])

            def layer_stats(rows):
                for t in range(B):
                    ins = dve.bn_stats(stats[:, t], rows[:, t])
                chain(ins)
                for t in range(B):
                    ins = dve.bn_aggr(mv[:, t], stats[:, t])
                chain(ins)
                dve.tensor_scalar(veps[:], mv[:, :, 1], EPS, None, ALU.add).then_inc(q.veps_ready, 1)

            def normalize(n, rows, s):
                dve.wait_ge(q.rstd_ready, n + 1)
                for t in range(B):
                    dve.tensor_scalar(z[:, t], rows[:, t], mv[:, t, 0:1], rstd[:, t:t + 1], ALU.subtract, ALU.mult
                                      ).then_inc(s, 1)

            dve.wait_ge(q.ld_kv, 48)
            chain(dve.memset(ones_row, 1.0))
            dve.wait_ge(q.gates_ready, 2)
            chain(dve.tensor_scalar(k_row, ones_row, gates[:, 4:5], None, ALU.mult))
            chain(dve.tensor_tensor_scan(r_row, k_row, ones_row, 0.0, ALU.mult, ALU.add))
            chain(dve.tensor_reduce(gates[:, 5:6], r_row, AX.X, ALU.add))
            dve.tensor_scalar(bq[:], cols[:, C_BQ:C_BQ + KD], SCALE, None, ALU.mult).then_inc(q.bq_ready, 1)
            chain(dve.tensor_scalar(bC[:], cols[:, C_BIN:C_BIN + KD], gates[:, 5:6], None, ALU.mult))

            def decayed(b):
                for k in range(KD):
                    n = b * KD + k
                    if n >= 2:
                        dve.wait_ge(q.u_done, n - 1)
                    dve.tensor_tensor_reduce(prod_rows[n % 2], ctxk[:, b, k], r_row, 1.0, 0.0, ALU.mult, ALU.add,
                                             uT[:, k, b:b + 1]).then_inc(q.u_done, 1)
            decayed(0)
            dve.wait_ge(q.ld_ctx1, 16)
            decayed(1)
            dve.wait_ge(q.ld_ctx, 16 * (B - 2))
            for b in range(2, B):
                decayed(b)
            dve.wait_ge(q.ld_x, 16)
            layer_stats(x)
            normalize(0, x, q.z_ready)
            dve.wait_ge(q.ld_sum, 96)
            chain(dve.tensor_scalar(gamma, gamma, gx0, None, ALU.mult))
            dve.tensor_scalar(beta, beta, gx0, None, ALU.mult).then_inc(q.beta_ready, 1)
            dve.wait_ge(q.s1_mm, 1)
            dve.tensor_tensor(s1T[:], ps[:, 6, 0:KD * B].rearrange("p (k b) -> p k b", k=KD),
                              bC[:].rearrange("p (k o) -> p k o", o=1).to_broadcast([P, KD, B]), ALU.add
                              ).then_inc(q.s1_ready, 1)
            dve.wait_ge(q.sum_mm, 1)
            dve.wait_ge(q.summ_zeroed, 1)
            dve.scalar_tensor_tensor(out=summ[0:B], in0=ps[0:B, 7, :], scalar=1.0 / T, in1=bout, op0=ALU.mult, op1=ALU.add
                                     ).then_inc(q.sum_ready, 1)
            for t in range(B):
                dve.wait_ge(q.bc_mm, t + 1)
                dve.wait_ge(q.z_ready, t + 1)
                dve.tensor_tensor(z[:, t], z[:, t], ps[0:S, 6 + t % 2, :], ALU.add).then_inc(q.y_added, 1)
            dve.wait_ge(q.y_added, B)
            layer_stats(z)
            dve.wait_ge(q.rstd_ready, 2)
            dve.wait_ge(q.x_based, B)
            for t in range(B):
                ins = dve.scalar_tensor_tensor(out=z[:, t], in0=z[:, t], scalar=mv[:, t, 0:1], in1=gamma,
                                               op0=ALU.subtract, op1=ALU.mult)
            chain(ins)
            for t in range(B):
                ins = dve.scalar_tensor_tensor(out=x[:, t], in0=z[:, t], scalar=rstd[:, t:t + 1], in1=x[:, t],
                                               op0=ALU.mult, op1=ALU.add)
            chain(ins)
            layer_stats(x)
            normalize(2, x, q.h_ready)

            def turned(n, t):
                dve.wait_ge(q.tr_mm, n * B + t + 1)
                dve.tensor_copy(hT[:, :, t * S:(t + 1) * S],
                                ps[:, 6 + t % 2, 0:KD * S].rearrange("p (k s) -> p k s", k=KD)).then_inc(q.tr_ev, 1)

            def logits(n, m, E, lg):
                for t in range(B + 1):
                    if t < B:
                        turned(n, t)
                    if t >= 1:
                        u = t - 1
                        dve.wait_ge(q.lg_mm, m * B + u + 1)
                        dve.tensor_copy(lg[:, u], ps[0:S, 6 + u % 2, 448:448 + E]).then_inc(q.lg_ev, 1)
                dve.wait_ge(q.lg_ev, (m + 1) * B)

            def sort(n, v, E, C, NB, meanwhile=None):
                pairs = B * C
                oh = v["oh"].rearrange("p (c e) -> p c e", e=E)
                dve.wait_ge(q.rank_mm, n + 1)
                chain(dve.tensor_scalar(v["cnti"], ps[:, 7, 0:E], float(P - 1), None, ALU.add))
                chain(dve.memset(v["ones"], 1.0))
                chain(dve.tensor_scalar(v["cnti"], v["cnti"], 7, None, ALU.logical_shift_right))
                chain(dve.tensor_copy(v["nb"], v["cnti"]))
                if n == 0:
                    chain(dve.tensor_scalar(v["nb"], v["nb"], 1.0, None, ALU.max))
                chain(dve.tensor_tensor_scan(v["cum"], v["ones"], v["nb"], 0.0, ALU.mult, ALU.add))
                chain(dve.tensor_tensor(v["base"], v["cum"], v["nb"], ALU.subtract))
                chain(dve.tensor_scalar(v["base"], v["base"], float(P), None, ALU.mult))
                slot = v["slot"].rearrange("p (b e) -> p b e", b=B)
                chain(dve.tensor_tensor(slot, ps[0:S, 6, 0:B * E].rearrange("p (b e) -> p b e", b=B),
                                        v["base"][0:S].rearrange("p (o e) -> p o e", o=1).to_broadcast([S, B, E]),
                                        ALU.add))
                pick = v["pick"].rearrange("p (b k e) -> p b k e", b=B, k=C)
                chain(dve.tensor_tensor(pick, oh.rearrange("p (b k) e -> p b k e", b=B),
                                        slot.rearrange("p b (o e) -> p b o e", o=1).to_broadcast([S, B, C, E]),
                                        ALU.mult))
                chain(dve.tensor_reduce(v["sk"], v["pick"].rearrange("p (c e) -> p c e", e=E), AX.X, ALU.add))
                dve.tensor_copy(slot_u[:, 0:pairs], v["sk"])
                chain(dve.tensor_copy(v["ski"], v["sk"]))
                dve.tensor_scalar(v["qi"], v["ski"], 7, None, ALU.logical_shift_right)
                chain(dve.tensor_scalar(v["ri"], v["ski"], P - 1, None, ALU.bitwise_and))
                dve.tensor_copy(v["qf"], v["qi"])
                chain(dve.tensor_copy(v["rf"], v["ri"]))
                cum0 = v["cum"][0:1].rearrange("p (o e) -> p o e", o=1).to_broadcast([1, NB, E])
                j0 = iota[0:1, 0:NB].rearrange("p (j o) -> p j o", o=1).to_broadcast([1, NB, E])
                chain(dve.tensor_tensor(v["cmp"], cum0, j0, ALU.is_le))
                chain(dve.tensor_reduce(v["eb"][0:1], v["cmp"], AX.X, ALU.add))
                chain(dve.tensor_scalar(v["eb"][0:1], v["eb"][0:1], float(E - 1), None, ALU.min))
                chain(dve.tensor_copy(table[0:1, 0:NB], v["eb"][0:1]))
                if n == 0:
                    chain(dve.tensor_scalar(table[0:1, T_DONE:T_DONE + E], v["cum"][0:1], 1.0, None, ALU.add))
                    last = table[0:1, T_LAST:T_LAST + 1]
                    chain(dve.tensor_scalar(last, table[0:1, T_DONE + E - 1:T_DONE + E], 1, None,
                                            ALU.logical_shift_right))
                    chain(dve.tensor_scalar(last, last, 1.0, None, ALU.subtract))
                    t0i = v["la"][0:1].bitcast(I32)
                    chain(dve.tensor_scalar(t0i, table[0:1, 0:NB], NR0 - 1, None, ALU.bitwise_and))
                    chain(dve.tensor_copy(v["eb"][0:1], t0i))
                    t0 = v["la"][0:1]
                    chain(dve.tensor_scalar(t0, v["eb"][0:1], 0.0, float(A_RING[0]), ALU.is_equal, ALU.mult))
                    for r in range(1, NR0):
                        chain(dve.tensor_scalar(v["slot"][0:1, 0:NB], v["eb"][0:1], float(r), float(A_RING[r]),
                                                ALU.is_equal, ALU.mult))
                        chain(dve.tensor_tensor(t0, t0, v["slot"][0:1, 0:NB], ALU.add))
                    chain(dve.tensor_copy(table2[0:1, 0:NB], t0))
                rf = v["rf"].rearrange("p (c o) -> p c o", o=1)
                qf = v["qf"].rearrange("p (c o) -> p c o", o=1)
                io = iota[0:S].rearrange("p (o r) -> p o r", o=1)
                dve.tensor_tensor(v["rm"], io.to_broadcast([S, pairs, P]), rf.to_broadcast([S, pairs, P]), ALU.is_equal)
                chain(dve.tensor_tensor(v["qm"], io[:, :, 0:NB].to_broadcast([S, pairs, NB]),
                                        qf.to_broadcast([S, pairs, NB]), ALU.is_equal))
                tn = tile_no.rearrange("p (c o) -> p c o", o=1 if C == TOP else TOP)[:, :, 0:1]
                dve.tensor_tensor(v["q2"][:, :, 0], v["qm"], tn.to_broadcast([S, pairs, NB]), ALU.mult)
                dve.tensor_scalar(v["q2"][:, :, 1], v["qm"], cols[0:S, C_PID:C_PID + 1], None, ALU.mult
                                  ).then_inc(q.ready_r, 1)
                if meanwhile:
                    meanwhile()
                dve.wait_ge(q.list_mm, n + 1)
                chain(dve.tensor_scalar(v["la"], ps[:, 6, 0:NB], float(S), None, ALU.mult))
                dve.tensor_tensor(lidx[:, 0:NB], v["la"], ps[:, 6, NB:2 * NB], ALU.add).then_inc(q.list_ready, 1)

            dve.memset(lidx[:, NB0:NB0 + 2], 0)
            v = disp0
            dve.wait_ge(q.filled, FILLS)
            logits(0, 0, E0, lg0)
            dve.wait_ge(q.h_stored, 16 * B)
            for t in range(B):
                ins = dve.max(v["m8"][:, t], lg0[:, t])
            chain(ins)
            for t in range(B):
                ins = dve.max_index(v["i8"][:, t], v["m8"][:, t], lg0[:, t])
            chain(ins)
            dve.tensor_copy(v["idf"].rearrange("p (b k) -> p b k", b=B), v["i8"][:, :, 0:TOP])
            chain(dve.tensor_copy(v["sk"][:, 0:B].rearrange("p (b o) -> p b o", o=1), v["m8"][:, :, 0:1]))
            dve.tensor_tensor(v["m8"][:, :, 0:TOP], v["m8"][:, :, 0:TOP],
                              v["sk"][:, 0:B].rearrange("p (b o) -> p b o", o=1).to_broadcast([S, B, TOP]),
                              ALU.subtract).then_inc(q.ediff_ready, 1)
            dve.wait_ge(q.ld_cst, 64)
            oh = v["oh"].rearrange("p (c e) -> p c e", e=E0)
            chain(dve.tensor_tensor(oh, iota[0:S, 0:E0].rearrange("p (o e) -> p o e", o=1).to_broadcast([S, B * TOP, E0]),
                                    v["idf"].rearrange("p (c o) -> p c o", o=1).to_broadcast([S, B * TOP, E0]),
                                    ALU.is_equal))
            chain(dve.tensor_reduce(v["slot"].rearrange("p (b e) -> p b e", b=B),
                                    v["oh"].rearrange("p (b k e) -> p b e k", b=B, k=TOP), AX.X, ALU.add))
            dve.tensor_copy(v["m"], v["slot"]).then_inc(q.ready_m, 1)

            def choice_weights():
                dve.wait_ge(q.eexp_ready, 1)
                wt3 = wt[:].rearrange("p (b k) -> p b k", b=B)
                chain(dve.tensor_reduce(veps[:], wt3, AX.X, ALU.add))
                chain(dve.reciprocal(veps[:], veps[:]))
                chain(dve.tensor_scalar(veps[:], veps[:], gf0, None, ALU.mult))
                chain(dve.tensor_tensor(wt3, wt3, veps[:].rearrange("p (b o) -> p b o", o=1).to_broadcast([S, B, TOP]),
                                        ALU.mult))

            sort(0, v, E0, TOP, NB0, meanwhile=choice_weights)

            def t_ev(j, par):
                dve.wait_ge(q.t_mm, j + 1)
                dve.tensor_copy(xT[par].rearrange("p k n -> p (k n)"), ps[:, par, :]).then_inc(q.t_ev, 1)

            def mul(j, par):
                dve.wait_ge(q.silu_done, j + 1)
                dve.tensor_tensor(hm[par], sg[par], ps[:, 2 + par, I0:2 * I0], ALU.mult).then_inc(q.h_mul, 1)

            def h_ev(j, par):
                dve.wait_ge(q.h_mm, j + 1)
                dve.tensor_copy(hmT[par].rearrange("p k n -> p (k n)"), ps[0:IH, 4 + par, 0:2 * P]).then_inc(q.h_ev, 1)

            t_ev(0, 0)
            mul(0, 0)
            t_ev(1, 1)
            h_ev(0, 0)
            mul(1, 1)
            t_ev(2, 0)

            def dve_pair(i):
                for par in range(2):
                    j = i * 2 + par
                    h_ev(j - 1, 1 - par)
                    mul(j, par)
                    t_ev(j + 1, 1 - par)

            last = last_pair(dve)
            with dve.Fori(1, NPL) as i:
                dve_pair(i)
            with dve.Fori(NPL, NP0) as i:
                with dve.If(last >= i):
                    dve_pair(i)
            h_ev(last * 2 + 1, 1)

            gath = [q.gath0, q.gath1, q.gath2, q.gath3, q.gath4, q.gath5, q.gath6, q.gath7]
            for k in range(B * TOP):
                t = k // TOP
                dve.wait_ge(gath[k % 8], 16 * (k // 8 + 1))
                if k % TOP:
                    dve.wait_ge(q.comb_done, k)
                dve.scalar_tensor_tensor(out=x[:, t], in0=g0[k % 8], scalar=wt[:, k:k + 1], in1=x[:, t],
                                         op0=ALU.mult, op1=ALU.add).then_inc(q.comb_done, 1)
            dve.wait_ge(q.comb_done, B * TOP)
            layer_stats(x)
            dve.wait_ge(q.rstd_ready, 4)
            for t in range(B):
                dve.tensor_scalar(z[:, t], x[:, t], mv[:, t, 0:1], rstd[:, t:t + 1], ALU.subtract, ALU.mult
                                  ).then_inc(q.h_ready, 1)
            dve.wait_ge(q.ld_bv, 16)
            dve.tensor_scalar(bv, bv, gx1, None, ALU.mult).then_inc(q.bv_ready, 1)
            for t in range(B):
                turned(1, t)
            dve.wait_ge(q.x_based, 2 * B)
            for t in range(B):
                dve.wait_ge(q.rt_mm, t + 1)
                dve.scalar_tensor_tensor(out=x[:, t], in0=ps[0:S, 4 + t % 2, :], scalar=gx1, in1=x[:, t],
                                         op0=ALU.mult, op1=ALU.add).then_inc(q.rt_add, 1)
            dve.wait_ge(q.rt_add, B)

            base = count[0]

            def row_max(u, par):
                dve.wait_ge(q.s_mm, u + 1)
                dve.tensor_reduce(nmx[:, par], ps[0:S, 2 * par:2 * par + 2, 0:T], AX.X, ALU.max, negate=True
                                  ).then_inc(q.mx_ready, 1)

            def probs_out(u):
                dve.wait_ge(q.pt_mm, u + 1)
                dve.tensor_copy(pT.rearrange("p (a i) s -> p a (i s)", a=2), ps[0:TC, 4:6, 0:3 * S]
                                ).then_inc(q.pt_ev, 1)

            def out_add(grp, b, m):
                par = m // 2 % 2
                dve.reciprocal(rinv[:, par], psum_e[:, par]).then_inc(q.dve_done, 1)
                dve.wait_ge(q.dve_done, grp + (base + 1))
                dve.wait_ge(q.f_mm, grp + 1)
                for h in range(4):
                    lo = (m // 2 * 4 + h) * DG
                    xs = x[:, bass.ds(b, 1), lo:lo + DG].rearrange("p b d -> p (b d)")
                    ins = dve.scalar_tensor_tensor(out=xs, in0=ps[0:S, 6 + par, P + h * DG:P + (h + 1) * DG],
                                                   scalar=rinv[:, par, h:h + 1], in1=xs, op0=ALU.mult, op1=ALU.add)
                ins.then_inc(q.o_done, 1)

            def row_stats(b):
                dve.wait_ge(q.o_done, b * GB + (GB + 2))
                xb = x[:, bass.ds(b, 1)].rearrange("p b d -> p (b d)")
                dve.bn_stats(stats[:, 0], xb).then_inc(q.ln_done, 1)

            def row_var(b):
                dve.wait_ge(q.ln_done, b * 2 + 1)
                dve.sem_inc(q.dve_seen, 1)
                dve.bn_aggr(mv[:, 0], stats[:, 0]).then_inc(q.ln_done, 1)
                dve.wait_ge(q.ln_done, b * 2 + 2)
                dve.tensor_scalar(veps[:, 0:1], mv[:, 0, 1:2], EPS, None, ALU.add).then_inc(q.veps_ready, 1)

            def row_norm(b):
                dve.wait_ge(q.rstd_ready, b + 5)
                dve.wait_ge(q.h_stored, b * 16 + 16 * B)
                dve.wait_ge(q.tr_mm, b + 2 * B)
                xb = x[:, bass.ds(b, 1)].rearrange("p b d -> p (b d)")
                dve.tensor_scalar(z1, xb, mv[:, 0, 0:1], rstd[:, 0:1], ALU.subtract, ALU.mult).then_inc(q.h_ready, 1)

            def row_logits(b):
                dve.wait_ge(q.lg_mm, b + (B + 1))
                dve.tensor_copy(lg1[:, bass.ds(b, 1)].rearrange("p b e -> p (b e)"), ps[0:S, 6, 448:448 + E1]
                                ).then_inc(q.lg_ev, 1)

            def att_batch(b, last=False, route=True):
                steps = {0: row_stats, 1: row_var, 3: row_norm, 7: row_logits} if route else {}
                for m in range(UB):
                    u = b * UB + m
                    if not (last and m >= UB - 2):
                        row_max(u + 2, m % 2)
                    if not (last and m == UB - 1):
                        probs_out(u + 1)
                    if m in steps:
                        steps[m](b - 1)
                    if m % 2:
                        out_add(b * GB + m // 2, b, m)

            row_max(0, 0)
            row_max(1, 1)
            probs_out(0)
            att_batch(0, route=False)
            with dve.Fori(1, B - 1) as b:
                att_batch(b)
            att_batch(B - 1, last=True)
            count[0] = base + GB * B

            for step in (row_stats, row_var, row_norm, row_logits):
                step(B - 1)
            dve.wait_ge(q.lg_ev, 2 * B)
            v = disp1
            diff = v["sk"].rearrange("p (b o) -> p b o", o=1)
            chain(dve.tensor_tensor(diff, lg1[:, :, 1:2], lg1[:, :, 0:1], ALU.subtract))
            oh = v["oh"].rearrange("p (b e) -> p b e", e=E1)
            dve.tensor_scalar(oh[:, :, 1:2], diff, 0.0, None, ALU.is_gt)
            dve.tensor_scalar(oh[:, :, 0:1], diff, 0.0, None, ALU.is_le)
            m1 = v["m"].rearrange("p (b e) -> p b e", e=E1)
            dve.tensor_scalar(m1[:, :, 1:2], diff, 0.0, None, ALU.is_gt)
            dve.tensor_scalar(m1[:, :, 0:1], diff, 0.0, None, ALU.is_le).then_inc(q.ready_m, 1)
            chain(dve.tensor_scalar(v["rf"], v["sk"], -1.0, None, ALU.mult))
            m8 = v["m8"][:, :, 0:1]
            dve.tensor_tensor(m8, diff, v["rf"].rearrange("p (b o) -> p b o", o=1), ALU.min).then_inc(q.ediff_ready, 1)
            dve.wait_ge(q.eexp_ready, 2)
            w1 = wt[:, 0:B]
            chain(dve.tensor_scalar(w1, w1, 1.0, None, ALU.add))
            chain(dve.reciprocal(w1, w1))
            chain(dve.tensor_scalar(w1, w1, gf1, None, ALU.mult))
            sort(1, v, E1, 1, NB1)

            def rows_out(j):
                dve.wait_ge(q.t1_mm, j + 1)
                dve.tensor_copy(xT1[:, j].rearrange("p k n -> p (k n)"), ps[:, 6 + j % 2, :]).then_inc(q.t1_ev, 1)

            def leak(s, par):
                dve.wait_ge(q.half_done, s + 1)
                dve.tensor_tensor(lk[par], hf[par], ps[:, par, :], ALU.max).then_inc(q.l_done, 1)

            def y_acc(s, j, first):
                dve.wait_ge(q.d1_mm, s + 1)
                if first:
                    dve.tensor_copy(y1[:, j], ps[:, 4 + j % 2, :]).then_inc(q.y1_ev, 1)
                else:
                    dve.tensor_tensor(y1[:, j], y1[:, j], ps[:, 4 + j % 2, :], ALU.add).then_inc(q.y1_ev, 1)

            rows_out(0)
            rows_out(1)
            for j in range(NB1):
                if j + 2 < NB1:
                    rows_out(j + 2)
                leak(j, j % 2)
                if j >= 2:
                    y_acc(j - 2, j - 2, True)
            for j in range(NB1):
                leak(NB1 + j, j % 2)
                y_acc(NB1 + j - 2, (j - 2) % NB1, j < 2)
            with dve.Fori(2, NCH) as c:
                for j in range(NB1):
                    leak(c * NB1 + j, j % 2)
                    y_acc(c * NB1 + (j - 2), (j - 2) % NB1, False)
            y_acc(NCH * NB1 - 2, NB1 - 2, False)
            y_acc(NCH * NB1 - 1, NB1 - 1, False)
            for t in range(B):
                dve.wait_ge(gath[t], 16 * (B * TOP // 8 + 2))
                dve.scalar_tensor_tensor(out=x[:, t], in0=g1[t], scalar=wt[:, t:t + 1], in1=x[:, t],
                                         op0=ALU.mult, op1=ALU.add).then_inc(q.out_ready, 1)


def kernel(x, ctx_2048, g_xattn, g_ffn, L0_xattn_decay, L0_xattn_W_in, L0_xattn_b_in, L0_xattn_W_out,
           L0_xattn_b_out, L0_xattn_gamma, L0_xattn_beta, L0_ffn_router_w, L0_ffn_gate_w, L0_ffn_up_w,
           L0_ffn_down_w, L1_xattn_W_fc, L1_xattn_b_fc, L1_xattn_W_q, L1_xattn_b_q, L1_xattn_W_k, L1_xattn_b_k,
           L1_xattn_W_v, L1_xattn_b_v, L1_ffn_w_router, L1_ffn_w_fc, L1_ffn_w_proj):
    import ml_dtypes
    from concourse import bacc
    from concourse.bass_utils import run_bass_kernel_spmd

    def split_rows(a):
        k = a.shape[0] // P
        return a.reshape(k, P, -1).transpose(1, 0, 2).reshape(P, -1)

    def across(a, parts):
        return np.broadcast_to(np.asarray(a).reshape(1, -1), (parts, np.asarray(a).size))

    f = {n: np.asarray(a) for n, a in dict(
        x=x, ctx=ctx_2048, win=L0_xattn_W_in, wout=L0_xattn_W_out, wfc=L1_xattn_W_fc, wq=L1_xattn_W_q,
        wk=L1_xattn_W_k, wv=np.asarray(L1_xattn_W_v).reshape(D, D), r0=L0_ffn_router_w, r1=L1_ffn_w_router,
        gate=L0_ffn_gate_w, up=L0_ffn_up_w, down=L0_ffn_down_w, fc=L1_ffn_w_fc, proj=L1_ffn_w_proj).items()}
    cols = np.zeros((P, NCOL), np.float32)
    for at, b in ((C_BIN, L0_xattn_b_in), (C_BFC, L1_xattn_b_fc), (C_BQ, L1_xattn_b_q), (C_BK, L1_xattn_b_k)):
        cols[:, at:at + KD] = np.asarray(b).reshape(KD, P).T
    cols[:, C_GX:C_GX + 2] = across(g_xattn, P)
    cols[:, C_GF:C_GF + 2] = across(g_ffn, P)
    cols[:, C_DEC:C_DEC + 1] = across(L0_xattn_decay, P)
    cols[:, C_PID] = np.arange(P)
    gu = np.concatenate([f["gate"], f["up"]], axis=1)
    gu = gu.transpose(0, 2, 1).reshape(E0, KD, P, 2 * I0).transpose(0, 2, 1, 3).reshape(E0, P, GU)
    dn = f["down"].transpose(0, 2, 1).reshape(E0, 2, IH, D).transpose(0, 2, 1, 3).reshape(E0, IH, 2 * D)
    fc = f["fc"].reshape(E1, NCH, CH, KD, P).transpose(1, 4, 0, 3, 2).reshape(NCH, P, E1, KD * CH)
    pj = f["proj"].reshape(E1, D, NCH, CH // P, P).transpose(2, 4, 0, 3, 1).reshape(NCH, P, E1, KD * CH)
    ch = np.concatenate([fc, pj], axis=3).reshape(NCH, P, RW1)
    sel = np.zeros((P, B, S), np.float32)
    sel[np.arange(B), np.arange(B)] = 1
    iota = np.zeros((P, P + B * TOP), np.float32)
    iota[:, :P] = np.arange(P)
    iota[:, P:] = np.repeat(np.arange(B), TOP)
    arrays = dict(
        x=f["x"].transpose(1, 0, 2).reshape(S, B * D),
        ctx=f["ctx"][:, ::-1].transpose(0, 2, 1).reshape(B, KD, P, T).transpose(0, 2, 1, 3).reshape(B, P, KD * T),
        wfc=split_rows(f["wfc"].T), wq=split_rows(f["wq"].T), wk=split_rows(f["wk"].T), wv=split_rows(f["wv"].T),
        win=split_rows(f["win"].T), wout=split_rows(f["wout"].T), cols=cols,
        gamma=across(L0_xattn_gamma, S), beta=across(L0_xattn_beta, S), bout=across(L0_xattn_b_out, B),
        bv=across(L1_xattn_b_v, S), rw0=split_rows(f["r0"].T), rw1=split_rows(f["r1"].T), gu=gu, dn=dn, ch=ch,
        ident=np.eye(P, dtype=np.float32), sel=sel.reshape(P, B * S), iota=iota,
        tri=np.triu(np.ones((S, S)), 1).astype(ml_dtypes.bfloat16), ones=np.ones((S, P), ml_dtypes.bfloat16))
    nc = bacc.Bacc("TRN2", target_bir_lowering=False, num_devices=1)
    arrays = {"in_" + n: np.ascontiguousarray(a) for n, a in arrays.items()}
    args = [nc.dram_tensor(n, a.shape, mybir.dt.from_np(a.dtype), kind="ExternalInput").ap()
            for n, a in arrays.items()]
    out = nc.dram_tensor("out", (B, S, D), F32, kind="ExternalOutput").ap()
    build(nc, *args, out)
    r = run_bass_kernel_spmd(nc, [arrays], core_ids=[0])
    return r.results[0]["out"]
```

```python
from contextlib import ExitStack

import numpy as np

import concourse.bass as bass
from concourse import mybir

F32 = mybir.dt.float32
F32R = mybir.dt.float32r
BF16 = mybir.dt.bfloat16
I32 = mybir.dt.int32
U32 = mybir.dt.uint32
ACT = mybir.ActivationFunctionType
ALU = mybir.AluOpType
AX = mybir.AxisListType

B, S, T, D = 8, 112, 375, 512
N = B * S
P = 128
KD = D // P
E0, TOP, I0 = 32, 4, 192
E1, HID = 2, 2048
H, DG = 16, 32
TC = T // 3
TE = T + 1
SPLIT = (2, 3, 4, 5)
UB = H // 2
GB = H // 4
EPS = 1e-5
SCALE = 1.0 / float(np.sqrt(DG))
NB0 = (N * TOP + E0 * (P - 1)) // P
NB0 += NB0 % 2
NP0 = NB0 // 2
NPL = E0 // 2
NB1 = (N + E1 * (P - 1)) // P
IH = I0 // 2
CH = 256
NCH = HID // CH
HK = CH // P
GU = KD * 2 * I0
RW0 = GU + 2 * D
NR0 = 4
RW1 = E1 * 2 * KD * CH
PIECES = 4
PW = RW1 // PIECES

C_BIN, C_BFC, C_BQ, C_BK, C_GX, C_GF, C_DEC, C_PID = 0, 4, 8, 12, 16, 18, 20, 21
NCOL = 24
FILLS = (NB0 - E0) // 4 * 16
T_LAST, T_DONE = 62, 64
assert NB0 <= T_LAST and (NB0 - E0) % 4 == 0

A_X = 0
A_K = A_X + B * D
A_V = A_K + B * KD * T
A_W = A_V + 3 * B * D
A_WFC, A_WQ, A_WK, A_WV = (A_W + i * KD * D for i in range(4))
A_SUP = A_WV + KD * D
A_C = A_SUP + KD * T + 4
A_Z = A_C + 2 * KD * D
A_HT = A_Z + B * D
A_FREE = A_HT + KD * N
A_END = A_FREE + RW0
A_RING = [A_FREE, A_Z + 4 * D + 4 * I0 + 4 * P + 2 * D, A_C, A_V + 3 * (B - 2) * D]
A_CST = A_C + 3648
A_G0 = [a + i * D for a in (A_FREE, A_C) for i in range(4)]
A_BV = A_FREE + 4 * D
A_REF = A_WK
A_QT = A_C
A_CH = A_W
A_WP = A_K
A_XH = A_WP + 4 * RW1
A_L1 = A_XH + NB1 * D
A_Y1 = A_Z + 4 * D
A_XL = A_Y1 + NB1 * D


def build(nc, x_in, ctx_in, wfc_in, wq_in, wk_in, wv_in, win_in, wout_in, cols_in, gamma_in, beta_in,
          bout_in, bv_in, rw0_in, rw1_in, gu_in, dn_in, ch_in, ident_in, sel_in, iota_in, tri_in, ones_in, out):
    h0_dram = nc.dram_tensor("h0_rows", [N, D], F32, kind="Internal").ap()
    y0_dram = nc.dram_tensor("y0_slots", [NB0 * P, D], F32, kind="Internal").ap()
    h1_dram = nc.dram_tensor("h1_rows", [N, D], F32, kind="Internal").ap()
    y1_dram = nc.dram_tensor("y1_slots", [NB1 * P, D], F32, kind="Internal").ap()
    out_rows = out.rearrange("b s d -> s b d")

    with ExitStack() as ctx:
        def sb(name, shape, dt=F32):
            return ctx.enter_context(nc.sbuf_tensor(name, shape, dt))

        def sem(name):
            return ctx.enter_context(nc.semaphore(name))

        arena_at = -(-nc.sbuf_base // 32) * 32
        arena = sb("arena", [P, A_END])
        assert nc.sbuf_base - arena_at == 4 * A_END, (nc.sbuf_base, arena_at, A_END)

        def at(off, words, parts=P):
            return arena[0:parts, off:off + words]

        def parts_at(name, off, words, dt=F32R):
            return nc.alloc_sbuf_tensor_at(name, [P, words], dt, offset=arena_at + 4 * off)

        w_at = (A_WFC, A_WK, A_WV)
        w_f32 = [parts_at(f"proj{i}", w_at[i], KD * D, F32)[:, :] for i in range(3)]
        w_lo = [parts_at(f"proj_lo{i}", w_at[i], KD * D)[:, :] for i in range(3)]
        w_hi = [parts_at(f"proj_hi{i}", a, KD * D)[:, :]
                for i, a in enumerate((A_V + 15 * D, A_WQ, A_V + 15 * D + KD * D))]
        c_f32 = parts_at("ctx_f32", A_K, B * KD * T, F32)
        c_lo = parts_at("ctx_lo", A_K, B * KD * T)
        c_hi = parts_at("ctx_hi", A_C, KD * TE)
        c_lo_end = parts_at("ctx_lo_end", A_C + 2 * KD * TE, TE)[:, :]
        s_f32 = parts_at("sup_f32", A_SUP, KD * TE, F32)
        s_lo = parts_at("sup_lo", A_SUP, KD * TE)
        s_hi = parts_at("sup_hi", A_C + KD * TE, KD * TE)

        wfc, wk, wv, wq = (a.rearrange("p (k d) -> p k d", k=KD)
                           for a in (*w_f32, parts_at("proj_q", A_WQ, KD * D, F32)[:, :]))
        sup = s_f32[:, 0:KD * T].rearrange("p (k t) -> p k t", k=KD)
        ctx_rows = c_f32[:, :].rearrange("p (b k t) -> p b k t", b=B, k=KD)
        hT = parts_at("turned", A_HT, KD * N, F32)[:, :].rearrange("p (k n) -> p k n", k=KD)
        refT = parts_at("ref", A_REF, KD * N, F32)[:, :].rearrange("p (k n) -> p k n", k=KD)
        decay = parts_at("decay_rows", A_HT, 5 * T, F32)
        ones_row, k_row, r_row, *prod_rows = (decay[:, i * T:(i + 1) * T] for i in range(5))
        x = at(A_X, B * D, S).rearrange("p (b d) -> p b d", b=B)
        ctxk = at(A_K, B * KD * T).rearrange("p (b k t) -> p b k t", b=B, k=KD)
        vals = at(A_V, 3 * B * D, TC).rearrange("p (c d) -> p c d", d=D)
        w_in = at(A_C, KD * D).rearrange("p (k d) -> p k d", k=KD)
        w_out = at(A_C + KD * D, KD * D).rearrange("p (k d) -> p k d", k=KD)
        z = at(A_Z, B * D, S).rearrange("p (b d) -> p b d", b=B)
        gamma = at(A_FREE, D, S)
        beta = at(A_FREE + D, D, S)
        bout = at(A_FREE + 2 * D, D, B)
        sel = at(A_FREE + 3 * D, B * S).rearrange("p (b s) -> p b s", b=B)
        bv = at(A_BV, D, S)
        summ = at(A_HT + 5 * T, D)
        zero_rows = at(A_HT + 5 * T + D, D)
        lg0 = at(A_C + (2 * KD + 1) * TE, B * E0, S).rearrange("p (b e) -> p b e", b=B)
        assert RW0 <= 2 * KD * TE and (2 * KD + 1) * TE + B * E0 <= A_CST - A_C
        z1 = at(A_SUP, D, S)
        hT1 = at(A_SUP + D, KD * S).rearrange("p (k s) -> p k s", k=KD)
        lg1 = at(A_SUP + D + KD * S, B * E1, S).rearrange("p (b e) -> p b e", b=B)
        iota = at(A_CST, P)
        tri = at(A_CST + P, S // 2, S).bitcast(BF16)
        ones_b = at(A_CST + P + S // 2, P // 2, S).bitcast(BF16)
        tile_no = at(A_CST + P + S // 2 + P // 2, B * TOP, S)

        ident = sb("ident", [P, P])
        cols = sb("cols", [P, NCOL])
        gates = sb("gates", [P, 8])
        rw0 = sb("rw0", [P, KD * E0])
        rw1 = sb("rw1", [P, KD * E1])
        stats = sb("stats", [S, B, 6])
        mv = sb("mv", [S, B, 2])
        veps = sb("veps", [S, B])
        mhalf = sb("mhalf", [S, B])
        rstd = sb("rstd", [S, B])
        table_warm = sb("table_warm", [P, 1])
        uT = sb("uT", [P, KD, B])
        s1T = sb("s1T", [P, KD, B])
        bC = sb("bC", [P, KD])
        bq = sb("bq", [P, KD])
        lidx = sb("lidx", [P, NB0 + 2], U32)
        slot_u = sb("slot_u", [S, B * TOP], U32)
        wt = sb("wt", [S, B * TOP])
        table = sb("table", [1, 96], I32)
        table2 = sb("table2", [1, 64], I32)
        idxb = sb("idxb", [P, 2], U32)
        nmx = sb("nmx", [S, 2, 2])
        psum_e = sb("psum_e", [S, 2, 4])
        rinv = sb("rinv", [S, 2, 4])
        ps = ctx.enter_context(nc.psum_tensor("ps", [P, 8, 512], F32))

        names = """ld_kv ld_wfc ld_wk ld_wv ld_ctx1 ld_ctx ld_x ld_sum ld_cst ld_small ld_bv gates_ready u_done
            kv_mm kv_ev ch_ready s1_mm s1_ready sum_mm sum_ready bc_mm y_added beta_ready bv_ready z_ready
            x_based veps_ready rstd_ready h_ready h_stored tr_mm tr_ev lg_mm lg_ev ediff_ready eexp_ready
            ready_m rank_mm ready_r list_mm list_ready dve_done pool_done w_ready x0_landed x1_landed t_mm t_ev
            u_mm silu_done h_mul h_mm h_ev d_mm y_ev y0_stored y1_stored w0_landed w1_landed w2_landed
            w3_landed gath0 gath1 gath2 gath3 gath4 gath5 gath6 gath7 comb_done ref_mm ref_ev rt_mm rt_add
            qk0_landed qk1_landed s_mm mx_ready e_done pt_mm pt_ev pv_mm o_ev f_mm o_done c0_landed c1_landed
            whi_ready wlo_ready ahi_ready alo_ready xhi_ready ln_done dve_seen t1_mm t1_ev u1_mm half_done
            l_done h1_mm h1_ev d1_mm y1_ev y1_done out_ready out_stored lidx_copied idx_seen zeros_ready
            bq_ready zero_ready filled summ_zeroed warm pt2_ev ld_wq whi_made wlo_made w_back chi_ready
            clo_ready sup_ev slo_ready""".split()
        sems = {n: sem(n) for n in names}
        q = type("Sems", (), sems)

        block = ctx.enter_context(nc.Block())

        def dispatch_views(E, C, NB):
            pairs = B * C
            off = [A_Z]

            def take(words, parts=S):
                a = off[0]
                off[0] += words
                assert off[0] <= A_FREE
                return at(a, words, parts)
            v = {}
            v["m8"] = take(B * 8).rearrange("p (b k) -> p b k", k=8)
            v["i8"] = take(B * 8).bitcast(U32).rearrange("p (b k) -> p b k", k=8)
            v["idf"] = take(pairs)
            v["oh"] = take(pairs * E // 2).bitcast(BF16)
            v["m"] = take(B * E // 2).bitcast(BF16)
            v["slot"] = take(B * E)
            v["pick"] = take(pairs * E)
            v["sk"] = take(pairs)
            v["ski"] = take(pairs).bitcast(I32)
            v["qi"] = take(pairs).bitcast(I32)
            v["ri"] = take(pairs).bitcast(I32)
            v["qf"] = take(pairs)
            v["rf"] = take(pairs)
            v["cnti"] = take(E, P).bitcast(I32)
            v["nb"] = take(E, P)
            v["cum"] = take(E, P)
            v["ones"] = take(E, P)
            v["base"] = take(E, P)
            v["eb"] = take(NB, P)
            v["la"] = take(NB, P)
            v["rm"] = take(pairs * P // 2).bitcast(BF16).rearrange("p (c r) -> p c r", r=P)
            v["qm"] = take(pairs * NB // 2).bitcast(BF16).rearrange("p (c j) -> p c j", j=NB)
            v["q2"] = take(pairs * NB).bitcast(BF16).rearrange("p (c a j) -> p c a j", a=2, j=NB)
            v["cmp"] = v["rm"].rearrange("p c r -> p (c r)")[0:1, 0:NB * E].rearrange("p (j e) -> p j e", e=E)
            v["cmp_ok"] = NB * E <= pairs * P
            return v

        disp0 = dispatch_views(E0, TOP, NB0)
        disp1 = dispatch_views(E1, 1, NB1)
        assert disp0["cmp_ok"] and disp1["cmp_ok"]

        def pair(off, words, parts=P):
            return [at(off + i * words, words, parts) for i in range(2)]
        xg = pair(A_Z, D)
        xT = [a.rearrange("p (k n) -> p k n", k=KD) for a in pair(A_Z + 2 * D, D)]
        sg = pair(A_Z + 4 * D, I0)
        hm = pair(A_Z + 4 * D + 2 * I0, I0)
        hmT = [a.rearrange("p (k n) -> p k n", k=2) for a in pair(A_Z + 4 * D + 4 * I0, 2 * P, IH)]
        yb = pair(A_Z + 4 * D + 4 * I0 + 4 * P, D)
        g0 = [at(a, D, S) for a in A_G0]
        ring = arena[:, :]

        A_AT = A_Z
        prob = [at(A_AT + i * 2 * T, 2 * T, S).rearrange("p (h t) -> p h t", h=2) for i in range(2)]
        pT = at(A_AT + 4 * T, 6 * S, TC).rearrange("p (i s) -> p i s", i=6)
        oT = at(A_AT + 4 * T + 6 * S, S)
        A_VB = A_AT + 4 * T + 7 * S
        vb = [at(A_VB + i * 3 * D, 3 * D, TC).rearrange("p (c d) -> p c d", c=3) for i in range(2)]
        A_KB = A_VB + 6 * D
        kb = [at(A_KB + i * KD * T, KD * T).rearrange("p (k t) -> p k t", k=KD) for i in range(2)]
        A_QB = A_KB + 2 * KD * T
        qb = [at(A_QB + i * 2 * KD * S, 2 * KD * S).rearrange("p (k a s) -> p k a s", k=KD, a=2) for i in range(2)]
        assert A_QB + 4 * KD * S <= A_END
        qT = at(A_QT, KD * N).rearrange("p (k n) -> p k n", k=KD)

        y1 = at(A_Y1, NB1 * D).rearrange("p (j d) -> p j d", j=NB1)
        xh1, xl1 = (parts_at(n, a, NB1 * D)[:, :].rearrange("p (j k n) -> p j k n", j=NB1, k=KD)
                    for n, a in (("rows_hi", A_XH), ("rows_lo", A_XL)))
        wp1 = parts_at("weights1", A_WP, 4 * RW1)
        hf = pair(A_L1, CH)
        lk = pair(A_L1 + 2 * CH, CH)
        w1 = parts_at("loaded1", A_CH, 2 * RW1, F32)
        act1 = [parts_at(f"act{i}", A_L1 + (4 + i) * CH, CH, F32)[:, :] for i in range(2)]
        ah1, al1 = ([parts_at(f"act_{n}{i}", a + i * CH, CH)[:, :] for i in range(2)]
                    for n, a in (("hi", A_L1 + 6 * CH), ("lo", A_L1 + 8 * CH)))
        xg1 = [y1[:, j] for j in range(NB1)]
        g1 = [at(A_WP + i * D, D, S) for i in range(8)]
        assert A_L1 + 10 * CH <= A_W and A_XL + NB1 * D <= A_END

        gx0, gx1, gf0, gf1 = (gates[0:S, i:i + 1] for i in range(4))

        def last_pair(eng):
            return eng.value_load(table[0:1, T_LAST:T_LAST + 1], min_val=NPL - 1, max_val=NP0 - 1)

        def further_pairs(eng, last, body, ahead=0):
            def loop(lo, hi):
                with eng.Fori(lo + ahead, hi + ahead) as i:
                    with eng.If(last >= i - ahead if ahead else last >= i):
                        body(i)
            half = (NPL + NP0) // 2
            loop(NPL, half)
            with eng.If(last >= half):
                loop(half, NP0)

        def piece(c, n):
            slot = c % 2
            return (w1[:, bass.ds(slot * RW1 + n * PW, PW)],
                    wp1[:, bass.ds(slot * (2 * RW1) + n * PW, PW)],
                    wp1[:, bass.ds(slot * (2 * RW1) + (RW1 + n * PW), PW)])

        @block.sync
        def _(sp):
            def load(dst, src, s):
                sp.dma_start(dst, src).then_inc(s, 16)
            load(cols[:], cols_in, q.ld_kv)
            wfc_rows = wfc_in.rearrange("p (k d) -> p k d", k=KD)
            load(wfc[:, :, 0:P], wfc_rows[:, :, 0:P], q.ld_kv)
            load(ctx_rows[:, 0], ctx_in[0].rearrange("p (k t) -> p k t", k=KD), q.ld_kv)
            load(wfc[:, :, P:D], wfc_rows[:, :, P:D], q.ld_wfc)
            load(wk, wk_in.rearrange("p (k d) -> p k d", k=KD), q.ld_wk)
            load(wv, wv_in.rearrange("p (k d) -> p k d", k=KD), q.ld_wv)
            load(x, x_in.rearrange("p (b d) -> p b d", b=B), q.ld_x)
            load(ctx_rows[:, 1], ctx_in[1].rearrange("p (k t) -> p k t", k=KD), q.ld_ctx1)
            for b in range(2, B):
                load(ctx_rows[:, b], ctx_in[b].rearrange("p (k t) -> p k t", k=KD), q.ld_ctx)
            load(w_in, win_in.rearrange("p (k d) -> p k d", k=KD), q.ld_sum)
            load(w_out, wout_in.rearrange("p (k d) -> p k d", k=KD), q.ld_sum)
            load(gamma, gamma_in, q.ld_sum)
            load(beta, beta_in, q.ld_sum)
            load(bout, bout_in, q.ld_sum)
            load(sel, sel_in.rearrange("p (b s) -> p b s", b=B), q.ld_sum)
            load(ident[:], ident_in, q.ld_small)
            load(rw0[:], rw0_in, q.ld_small)
            load(rw1[:], rw1_in, q.ld_small)
            sp.wait_ge(q.zero_ready, 1)
            slots = y0_dram.rearrange("(j p) d -> p j d", p=P)
            zeros4 = zero_rows.rearrange("p (o d) -> p o d", o=1).to_broadcast([P, 4, D])
            for j in range(E0, NB0, 4):
                sp.dma_start(slots[:, j:j + 4], zeros4).then_inc(q.filled, 16)
            sp.wait_ge(q.sum_mm, 1)
            load(iota, iota_in[:, 0:P], q.ld_cst)
            load(tile_no, iota_in[0:S, P:P + B * TOP], q.ld_cst)
            load(tri, tri_in, q.ld_cst)
            load(ones_b, ones_in, q.ld_cst)
            for t in range(B):
                sp.wait_ge(q.h_ready, t + 1)
                sp.dma_start(h0_dram[t * S:(t + 1) * S, :], z[:, t]).then_inc(q.h_stored, 16)

            landed = [q.w0_landed, q.w1_landed, q.w2_landed, q.w3_landed]

            def load_expert(e, slot):
                dst = at(A_RING[slot], GU)
                sp.dma_start(dst, gu_in[bass.ds(e, 1)].rearrange("e p n -> (e p) n")).then_inc(landed[slot], 16)
                dst = at(A_RING[slot] + GU, 2 * D, IH)
                sp.dma_start(dst, dn_in[bass.ds(e, 1)].rearrange("e p n -> (e p) n")).then_inc(landed[slot], 16)

            load_expert(0, 0)
            sp.wait_ge(q.list_ready, 1)
            load_expert(1, 1)
            sp.wait_ge(q.w_back, 2)
            load(wq, wq_in.rearrange("p (k d) -> p k d", k=KD), q.ld_wq)
            sp.wait_ge(q.kv_mm, max(SPLIT) * 11 + 11)
            load_expert(2, 2)

            def announce(e):
                sp.wait_ge(landed[e], 32)
                sp.sem_inc(q.w_ready, 1)

            announce(0)
            announce(1)
            sp.wait_ge(q.w_back, 3)
            load_expert(3, 3)
            announce(2)
            assert NR0 == 4

            def next_expert(e, slot, rounds):
                ahead = (slot + NR0 - 1) % NR0
                sp.wait_ge(landed[ahead], rounds)
                sp.sem_inc(q.w_ready, 1)
                done = sp.value_load(table[0:1, bass.ds(e + T_DONE, 1)], min_val=2, max_val=NB0 + 1)
                sp.wait_ge(q.d_mm, done)
                load_expert(e + NR0, slot)

            with sp.Fori(0, (E0 - NR0) // NR0) as i:
                for slot in range(NR0):
                    next_expert(i * NR0 + slot, slot, i * 32 + (32 if slot == 0 else 64))
            for e in range((E0 - NR0) // NR0 * NR0, E0 - NR0):
                next_expert(e, e % NR0, 32 * ((e + NR0 - 1) // NR0 + 1))
            sp.wait_ge(landed[(E0 - 1) % NR0], 32 * ((E0 - 1) // NR0 + 1))
            sp.sem_inc(q.w_ready, 1)

            sp.wait_ge(q.d_mm, last_pair(sp) * 2 + 3)
            load(bv, bv_in, q.ld_bv)

            def load_chunk(c):
                for a in range(2):
                    w = RW1 // 2
                    sp.dma_start(w1[:, c % 2 * RW1 + a * w:c % 2 * RW1 + (a + 1) * w], ch_in[c, :, a * w:(a + 1) * w]
                                 ).then_inc((q.c0_landed, q.c1_landed)[c % 2], 16)

            staged = (q.qk0_landed, q.qk1_landed)

            def stage_kv(b, par):
                s = staged[par]
                sp.dma_start(kb[par], ctxk[:, bass.ds(b, 1)].rearrange("p b k t -> p (b k) t")).then_inc(s, 16)
                sp.dma_start(vb[par], vals[:, bass.ds(b * 3, 3)]).then_inc(s, 16)

            def stage_q(b, par):
                s = staged[par]
                for h in range(4):
                    rows = slice(h * DG, (h + 1) * DG)
                    sp.dma_start(qb[par][rows, :, h % 2], qT[rows, :, bass.ds(b * S, S)]).then_inc(s, 16)

            sp.wait_ge(q.ref_mm, 8)
            sp.wait_ge(q.kv_ev, 11 * B)
            stage_kv(0, 0)
            stage_kv(1, 1)
            sp.wait_ge(q.ref_ev, 12)
            sp.wait_ge(q.zeros_ready, 1)
            stage_q(0, 0)
            stage_q(1, 1)
            sp.wait_ge(q.ref_ev, 16)
            sp.wait_ge(q.rt_mm, B)
            load_chunk(0)
            load_chunk(1)

            def store_normalized(b):
                sp.wait_ge(q.h_ready, b + (2 * B + 1))
                sp.dma_start(h1_dram[bass.ds(b * S, S), :], z1).then_inc(q.h_stored, 16)

            with sp.Fori(1, B // 2) as i:
                for par in range(2):
                    sp.wait_ge(q.pv_mm, i * (2 * UB) + (par - 1) * UB)
                    stage_kv(i * 2 + par, par)
                    stage_q(i * 2 + par, par)
                    store_normalized(i * 2 + (par - 2))
            for b in range(B - 2, B):
                store_normalized(b)
            for c in range(NCH):
                sp.wait_ge((q.c0_landed, q.c1_landed)[c % 2], 32 * (c // 2 + 1))
                sp.sem_inc(q.ch_ready, 1)
                if c + 2 < NCH:
                    sp.wait_ge(q.wlo_ready, PIECES * (c + 1))
                    load_chunk(c + 2)
            for j in range(NB1):
                sp.wait_ge(q.y1_ev, NB1 * (NCH - 1) + j + 1)
                sp.dma_start(y1_dram[j * P:(j + 1) * P, :], y1[:, j]).then_inc(q.y1_done, 16)
            for t in range(B):
                sp.wait_ge(q.out_ready, t + 1)
                sp.dma_start(out_rows[:, t], x[:, t]).then_inc(q.out_stored, 16)
            sp.wait_ge(q.out_stored, 16 * B)

        @block.gpsimd
        def _(pool):
            pool.memset(zero_rows, 0.0).then_inc(q.zero_ready, 1)
            pool.memset(summ, 0.0).then_inc(q.summ_zeroed, 1)
            pool.memset(mhalf[:], -0.5).then_inc(q.pool_done, 1)
            pool.wait_ge(q.pool_done, 1)

            def root(n):
                pool.wait_ge(q.veps_ready, n + 1)
                pool.tensor_tensor(rstd[:], veps[:], mhalf[:], ALU.pow).then_inc(q.rstd_ready, 1)

            root(0)

            def weight_rest(i):
                pool.wait_ge(q.whi_made, i + 1)
                pool.tensor_tensor(w_lo[i], w_f32[i], w_hi[i], ALU.subtract).then_inc(q.wlo_made, 1)

            def ctx_rest(b):
                pool.wait_ge(q.chi_ready, SPLIT.index(b) + 1)
                lo, mid = b * KD * T, b * KD * T + (KD - 1) * T
                n = (KD - 1) * T
                pool.tensor_tensor(c_lo_end, c_f32[:, mid:mid + TE], c_hi[:, n:n + TE], ALU.subtract
                                   ).then_inc(q.clo_ready, 1)
                pool.wait_ge(q.clo_ready, SPLIT.index(b) * 2 + 1)
                pool.tensor_tensor(c_lo[:, lo:lo + n + 1], c_f32[:, lo:lo + n + 1], c_hi[:, 0:n + 1], ALU.subtract
                                   ).then_inc(q.clo_ready, 1)

            def sup_rests(b):
                for n in range(KD):
                    pool.wait_ge(q.sup_ev, SPLIT.index(b) * KD + n + 1)
                    pool.wait_ge(q.kv_ev, b * 11 + n + 1)
                    e = slice(n * TE, (n + 1) * TE)
                    pool.tensor_tensor(s_lo[:, e], s_f32[:, e], s_hi[:, e], ALU.subtract).then_inc(q.slo_ready, 1)

            weight_rest(0)
            pool.wait_ge(q.beta_ready, 1)
            for t in range(B):
                pool.tensor_tensor(x[:, t], x[:, t], beta, ALU.add).then_inc(q.x_based, 1)
            weight_rest(1)
            ctx_rest(2)
            root(1)
            sup_rests(2)
            weight_rest(2)
            ctx_rest(3)
            root(2)
            sup_rests(3)
            ctx_rest(4)
            sup_rests(4)
            ctx_rest(5)
            sup_rests(5)

            landed = (q.x0_landed, q.x1_landed)

            def token_column(j, par):
                pool.tensor_copy(idxb[:, par:par + 1], lidx[:, bass.ds(j, 1)]).then_inc(q.lidx_copied, 1)

            def gather(par, bufs, rows):
                pool.indirect_dma_start(out=bufs[par], out_offset=None, in_=rows,
                                        in_offset=bass.IndirectOffsetOnAxis(ap=idxb[:, par:par + 1], axis=0)
                                        ).then_inc(landed[par], 16)

            pool.wait_ge(q.list_ready, 1)
            pool.wait_ge(q.h_stored, 16 * B)
            for par in range(2):
                token_column(par, par)
                pool.wait_ge(q.lidx_copied, par + 1)
                gather(par, xg, h0_dram)

            def gather_pair(i):
                for par in range(2):
                    pool.wait_ge(q.t_mm, i * 2 + (par - 1))
                    token_column(i * 2 + par, par)
                    pool.wait_ge(q.lidx_copied, i * 2 + (par + 1))
                    pool.sem_inc(q.idx_seen, 1)
                    gather(par, xg, h0_dram)

            last = last_pair(pool)
            with pool.Fori(1, NPL + 1) as i:
                gather_pair(i)
            further_pairs(pool, last, gather_pair, ahead=1)
            for par in range(2):
                pool.wait_ge(landed[par], last * 16 + 32)

            gath = [q.gath0, q.gath1, q.gath2, q.gath3, q.gath4, q.gath5, q.gath6, q.gath7]
            pool.wait_ge(q.y0_stored, last * 16 + 16)
            pool.wait_ge(q.y1_stored, last * 16 + 16)
            pool.sem_inc(q.idx_seen, 1)
            for n in range(B * TOP):
                if n >= 8:
                    pool.wait_ge(q.comb_done, n - 7)
                pool.indirect_dma_start(out=g0[n % 8], out_offset=None, in_=y0_dram,
                                        in_offset=bass.IndirectOffsetOnAxis(ap=slot_u[:, n:n + 1], axis=0)
                                        ).then_inc(gath[n % 8], 16)
            root(3)
            pool.wait_ge(q.bv_ready, 1)
            for t in range(B):
                pool.tensor_tensor(x[:, t], x[:, t], bv, ALU.add).then_inc(q.x_based, 1)
            pool.wait_ge(q.x_based, 2 * B)
            pool.memset(at(A_QB, 4 * KD * S), 0.0).then_inc(q.zeros_ready, 1)
            def root1(b):
                pool.wait_ge(q.veps_ready, b + 5)
                pool.tensor_tensor(rstd[:, 0:1], veps[:, 0:1], mhalf[:, 0:1], ALU.pow).then_inc(q.rstd_ready, 1)

            def first_weights(n):
                w, hi, lo = piece(0, n)
                pool.tensor_copy(hi, w).then_inc(q.whi_ready, 1)
                pool.wait_ge(q.whi_ready, n + 1)
                pool.tensor_tensor(lo, w, hi, ALU.subtract).then_inc(q.wlo_ready, 1)

            with pool.Fori(0, B - 2) as b:
                root1(b)
            assert A_WP + 2 * RW1 <= A_K + (B - 2) * KD * T
            pool.wait_ge(q.c0_landed, 32)
            pool.wait_ge(q.pv_mm, UB * (B - 2))
            first_weights(0)
            first_weights(1)
            root1(B - 2)
            first_weights(2)
            first_weights(3)
            root1(B - 1)

            def weight_rests(c):
                for n in range(PIECES):
                    pool.wait_ge(q.whi_ready, c * PIECES + (n + 1))
                    w, hi, lo = piece(c, n)
                    pool.tensor_tensor(lo, w, hi, ALU.subtract).then_inc(q.wlo_ready, 1)

            pool.wait_ge(q.list_ready, 2)
            pool.wait_ge(q.h_stored, 16 * 2 * B)
            for j in range(NB1):
                pool.indirect_dma_start(out=xg1[j], out_offset=None, in_=h1_dram,
                                        in_offset=bass.IndirectOffsetOnAxis(ap=lidx[:, j:j + 1], axis=0)
                                        ).then_inc(gath[j], 16)
            with pool.Fori(1, NCH) as c:
                weight_rests(c)
            pool.wait_ge(q.y1_done, 16 * NB1)
            for t in range(B):
                pool.indirect_dma_start(out=g1[t], out_offset=None, in_=y1_dram,
                                        in_offset=bass.IndirectOffsetOnAxis(ap=slot_u[:, t:t + 1], axis=0)
                                        ).then_inc(gath[t], 16)

        @block.scalar
        def _(act):
            act.wait_ge(q.ld_kv, 48)
            act.activation(gates[:, 4:5], cols[:, C_DEC:C_DEC + 1], ACT.Sigmoid).then_inc(q.gates_ready, 1)
            act.activation(gates[:, 0:4], cols[:, C_GX:C_GX + 4], ACT.Tanh).then_inc(q.gates_ready, 1)

            def kv(b, behind={}, split=False):
                bank = [0, 1, 2, 3, 4, 5, 0, 1, 2, 3, 4]
                for n in range(11):
                    act.wait_ge(q.kv_mm, b * 11 + (n + 1))
                    src = ps[:, bank[n], 0:T]
                    if n < KD and split:
                        src, bias = ps[:, bank[n], 0:TE], cols[:, C_BFC + n:C_BFC + n + 1]
                        act.activation(s_f32[:, n * TE:(n + 1) * TE], src, ACT.Relu, bias=bias).then_inc(q.sup_ev, 1)
                        ins = act.activation(s_hi[:, n * TE:(n + 1) * TE], src, ACT.Relu, bias=bias)
                    elif n < KD:
                        ins = act.activation(sup[:, n], src, ACT.Relu, bias=cols[:, C_BFC + n:C_BFC + n + 1])
                    elif n < 2 * KD:
                        m = n - KD
                        if m == 0:
                            act.wait_ge(q.u_done, b * KD + KD)
                        ins = act.activation(ctxk[:, bass.ds(b, 1), m].rearrange("p b t -> p (b t)"), src,
                                             ACT.Identity, bias=cols[:, C_BK + m:C_BK + m + 1])
                    else:
                        c = n - 2 * KD
                        if split and b == max(SPLIT) and c == 0:
                            act.wait_ge(q.w_back, 1)
                        ins = act.activation(vals[:, bass.ds(b * 3 + c, 1)].rearrange("p b t -> p (b t)"),
                                             ps[0:TC, bank[n], :], ACT.Copy, scale=gates[0:TC, 1:2])
                    ins.then_inc(q.kv_ev, 1)
                    if n in behind:
                        behind[n]()

            def weight_round(i):
                act.activation(w_hi[i], w_f32[i], ACT.Copy).then_inc(q.whi_made, 1)

            def ctx_round(b):
                act.activation(c_hi[:, 0:KD * T + 1], c_f32[:, b * KD * T:(b + 1) * KD * T + 1], ACT.Copy
                               ).then_inc(q.chi_ready, 1)

            def first_ctx_round():
                act.wait_ge(q.sum_mm, 1)
                act.wait_ge(q.ld_ctx, 16 * (B - 2))
                ctx_round(SPLIT[0])

            kv(0)
            kv(1, {3: lambda: weight_round(0), 7: lambda: weight_round(1), 9: first_ctx_round,
                   10: lambda: weight_round(2)})
            for b in SPLIT[:-1]:
                kv(b, {5: lambda: ctx_round(b + 1)}, split=True)
            act.wait_ge(q.ediff_ready, 1)
            d = disp0["m8"][:, :, 0:TOP]
            act.activation(wt[:].rearrange("p (b k) -> p b k", b=B), d, ACT.Exp).then_inc(q.eexp_ready, 1)
            kv(SPLIT[-1], split=True)

            stored = (q.y0_stored, q.y1_stored)

            def silu(j, par):
                act.wait_ge(q.u_mm, j + 1)
                act.activation(sg[par], ps[:, 2 + par, 0:I0], ACT.Silu).then_inc(q.silu_done, 1)

            def y_out(j, par, i):
                act.wait_ge(q.d_mm, j + 2)
                if i is not None:
                    act.wait_ge(stored[par], i * 16)
                act.activation(yb[par], ps[:, 6 + par, :], ACT.Copy).then_inc(q.y_ev, 1)
                act.wait_ge(q.y_ev, j + 1)
                act.dma_start(y0_dram[bass.ds(j * P, P), :], yb[par]).then_inc(stored[par], 16)

            act.activation(table_warm[:], gates[:, 0:1], ACT.Silu).then_inc(q.warm, 1)
            act.wait_ge(q.filled, FILLS)
            silu(0, 0)
            silu(1, 1)
            for par in range(2):
                silu(2 + par, par)
                y_out(par, par, None)

            def act_pair(i):
                for par in range(2):
                    silu(i * 2 + par, par)
                    y_out(i * 2 + (par - 2), par, i - 1)

            last = last_pair(act)
            with act.Fori(2, NPL) as i:
                act_pair(i)
            further_pairs(act, last, act_pair)
            for par in range(2):
                y_out(last * 2 + par, par, last)

            with act.Fori(6, B) as b:
                kv(b)
            act.wait_ge(q.bq_ready, 1)
            for n in range(16):
                act.wait_ge(q.ref_mm, n + 1)
                m, half = n % 4, n // 4 % 2
                dst = (refT if n < 8 else qT)[:, m, half * 448:half * 448 + 448]
                bias = cols[:, C_BFC + m:C_BFC + m + 1] if n < 8 else bq[:, m:m + 1]
                act.activation(dst, ps[:, n % 4, 0:448], ACT.Relu if n < 8 else ACT.Identity,
                               bias=bias, scale=1.0 if n < 8 else SCALE).then_inc(q.ref_ev, 1)

            def exps(u, par, place):
                act.wait_ge(q.mx_ready, u + 1)
                for h in range(2):
                    ins = act.activation(prob[par][:, h], ps[0:S, 2 * par + h, 0:T], ACT.Exp,
                                         bias=nmx[:, par, h:h + 1],
                                         accum_out=psum_e[:, place // 2, place % 2 + 2 * h:place % 2 + 2 * h + 1])
                ins.then_inc(q.e_done, 1)

            def out_rows(u, grp, bank):
                act.wait_ge(q.pv_mm, u + 1)
                act.activation(oT, ps[:, bank, 0:S], ACT.Copy).then_inc(q.o_ev, 1)

            def probs_out(u):
                act.wait_ge(q.pt_mm, u + 1)
                act.activation(pT[:, 3:6].rearrange("p i s -> p (i s)"), ps[0:TC, 5, 0:3 * S], ACT.Copy
                               ).then_inc(q.pt2_ev, 1)

            def exp_unit(u, n, grp, b=None):
                if n >= 1 or grp is not None:
                    probs_out(u - 1)
                exps(u, n % 2, n % 4)
                if n % 2 == 0 and grp is not None:
                    out_rows(u - 1, grp, 6 + (n // 2 - 1) % 2)
                if n == 6 and b is not None:
                    turned_rows(b - 1, 7)

            def turned_rows(b, bank):
                act.wait_ge(q.tr_mm, b + (2 * B + 1))
                act.activation(hT1.rearrange("p k s -> p (k s)"), ps[:, bank, 0:KD * S], ACT.Copy).then_inc(q.tr_ev, 1)

            for n in range(UB):
                exp_unit(n, n, n // 2 - 1 if n >= 2 else None)
            with act.Fori(1, B) as b:
                for n in range(UB):
                    exp_unit(b * UB + n, n, b * GB + (n // 2 - 1), b)
            probs_out(UB * B - 1)
            out_rows(UB * B - 1, GB * B - 1, 7)
            turned_rows(B - 1, 7)

            def weight_rounds(c, n, first=False):
                if n == 0:
                    act.wait_ge(q.ch_ready, c + 1)
                    if first:
                        act.wait_ge(q.pv_mm, UB * B)
                    if not first:
                        act.wait_ge(q.d1_mm, c * NB1 - NB1)
                w, hi, lo = piece(c, n)
                act.activation(hi, w, ACT.Copy).then_inc(q.whi_ready, 1)

            act.wait_ge(q.ediff_ready, 2)
            act.activation(wt[:, 0:B], disp1["m8"][:, :, 0:1].rearrange("p b k -> p (b k)"), ACT.Exp
                           ).then_inc(q.eexp_ready, 1)

            def l1(c, j):
                act.wait_ge(q.u1_mm, c * NB1 + (j + 1))
                act.activation(hf[j % 2], ps[:, j % 2, 0:CH], ACT.Copy, scale=0.5).then_inc(q.half_done, 1)

            def l1_sq(s, par):
                act.wait_ge(q.h1_mm, s + 1)
                act.activation(act1[par], ps[:, 2 + par, 0:CH], ACT.Square).then_inc(q.h1_ev, 1)
                act.activation(ah1[par], ps[:, 2 + par, 0:CH], ACT.Square).then_inc(q.ahi_ready, 1)

            def rows_round(j):
                act.wait_ge(q.t1_mm, j + 1)
                act.activation(xh1[:, j].rearrange("p k n -> p (k n)"), ps[:, 6 + j % 2, :], ACT.Copy
                               ).then_inc(q.xhi_ready, 1)

            def act_chunk(c, first=False, last=False):
                for j in range(NB1):
                    if first and j + 2 < NB1:
                        rows_round(j + 2)
                    l1(c, j)
                    if not first or j >= 1:
                        l1_sq(c * NB1 + (j - 1), (j - 1) % 2)
                    if 2 <= j < 2 + PIECES and not last:
                        weight_rounds(c + 1, j - 2, first=first)

            rows_round(0)
            rows_round(1)
            act_chunk(0, first=True)
            with act.Fori(1, NCH - 1) as c:
                act_chunk(c)
            act_chunk(NCH - 1, last=True)
            l1_sq(NB1 * NCH - 1, 1)

        @block.tensor
        def _(pe):
            def kv(b, ahead={}):
                bank = [0, 1, 2, 3, 4, 5, 0, 1, 2, 3, 4]
                last = [7, 8, 9, 10, 11, 6]
                first = isinstance(b, int) and b == 0
                for n in range(11):
                    if n in ahead:
                        ahead[n]()
                    if n >= 6:
                        pe.wait_ge(q.kv_ev, b * 11 + (n - 5))
                    elif not first:
                        pe.wait_ge(q.kv_ev, b * 11 + (last[n] - 11))
                    for k in range(KD):
                        if n < KD:
                            o = ps[:, bank[n], 0:T]
                            w = wfc[:, k, n * P:(n + 1) * P]
                            r = ctx_rows[:, b, k]
                        else:
                            if first and k == 0 and n in (KD, 2 * KD):
                                pe.wait_ge(q.ld_wk if n == KD else q.ld_wv, 16)
                            if n == KD:
                                pe.wait_ge(q.kv_ev, b * 11 + (k + 1))
                            if n < 2 * KD:
                                m = n - KD
                                o, w, r = ps[:, bank[n], 0:T], wk[:, k, m * P:(m + 1) * P], sup[:, k]
                            else:
                                c = n - 2 * KD
                                o, w, r = ps[0:TC, bank[n], :], sup[:, k, c * TC:(c + 1) * TC], wv[:, k]
                        ins = pe.matmul(o, w, r, start=(k == 0), stop=(k == KD - 1))
                    ins.then_inc(q.kv_mm, 1)

            def kv_split(b, ahead={}):
                bank = [0, 1, 2, 3, 4, 5, 0, 1, 2, 3, 4]
                at_split = SPLIT.index(b)

                def free(n):
                    last = [7, 8, 9, 10, 11, 6]
                    pe.wait_ge(q.kv_ev, b * 11 + (n - 5 if n >= 6 else last[n] - 11))

                def step_ahead(n):
                    if n in ahead:
                        ahead[n]()

                def w(part, k, m):
                    return part[:, k * D + m * P:k * D + (m + 1) * P]

                pe.wait_ge(q.wlo_made, 1)
                pe.wait_ge(q.clo_ready, at_split * 2 + 2)
                for n in range(KD):
                    step_ahead(n)
                    free(n)
                    for k in range(KD):
                        o = ps[:, bank[n], 0:TE]
                        hi = c_hi[:, k * T:k * T + TE]
                        lo = c_lo[:, (b * KD + k) * T:(b * KD + k) * T + TE] if k < KD - 1 else c_lo_end
                        pe.matmul(o, w(w_hi[0], k, n), hi, start=(k == 0), stop=False)
                        pe.matmul(o, w(w_lo[0], k, n), hi, start=False, stop=False)
                        ins = pe.matmul(o, w(w_hi[0], k, n), lo, start=False, stop=(k == KD - 1))
                    ins.then_inc(q.kv_mm, 1)

                def keys_hi(n):
                    step_ahead(n)
                    free(n)
                    for k in range(KD):
                        if n == KD:
                            pe.wait_ge(q.kv_ev, b * 11 + (k + 1))
                        hi = s_hi[:, k * TE:(k + 1) * TE]
                        pe.matmul(ps[:, bank[n], 0:TE], w(w_hi[1], k, n - KD), hi, start=(k == 0), stop=False)
                        pe.matmul(ps[:, bank[n], 0:TE], w(w_lo[1], k, n - KD), hi, start=False, stop=False)

                def keys_lo(n):
                    for k in range(KD):
                        pe.wait_ge(q.slo_ready, at_split * KD + k + 1)
                        ins = pe.matmul(ps[:, bank[n], 0:TE], w(w_hi[1], k, n - KD), s_lo[:, k * TE:(k + 1) * TE],
                                        start=False, stop=(k == KD - 1))
                    ins.then_inc(q.kv_mm, 1)

                pe.wait_ge(q.wlo_made, 2)
                keys_hi(KD)
                for n in range(KD + 1, 2 * KD):
                    keys_hi(n)
                    keys_lo(n - 1)
                keys_lo(2 * KD - 1)

                pe.wait_ge(q.wlo_made, 3)
                for n in range(2 * KD, 11):
                    step_ahead(n)
                    free(n)
                    c = n - 2 * KD
                    for k in range(KD):
                        o = ps[0:TC, bank[n], :]
                        rows = slice(k * TE + c * TC, k * TE + (c + 1) * TC)
                        pe.matmul(o, s_hi[:, rows], w_hi[2][:, k * D:(k + 1) * D], start=(k == 0), stop=False)
                        pe.matmul(o, s_lo[:, rows], w_hi[2][:, k * D:(k + 1) * D], start=False, stop=False)
                        ins = pe.matmul(o, s_hi[:, rows], w_lo[2][:, k * D:(k + 1) * D], start=False,
                                        stop=(k == KD - 1))
                    ins.then_inc(q.kv_mm, 1)

            def summary_in():
                pe.wait_ge(q.ld_sum, 96)
                pe.wait_ge(q.u_done, KD * B)
                for m in range(KD):
                    for k in range(KD):
                        ins = pe.matmul(ps[:, 6, m * B:(m + 1) * B], w_in[:, k, m * P:(m + 1) * P], uT[:, k],
                                        start=(k == 0), stop=(k == KD - 1))
                ins.then_inc(q.s1_mm, 1)

            def summary_out():
                pe.wait_ge(q.s1_ready, 1)
                for k in range(KD):
                    ins = pe.matmul(ps[0:B, 7, :], s1T[:, k], w_out[:, k], start=(k == 0), stop=(k == KD - 1))
                ins.then_inc(q.sum_mm, 1)

            def spread(t):
                if t == 0:
                    pe.wait_ge(q.sum_ready, 1)
                if t >= 2:
                    pe.wait_ge(q.y_added, t - 1)
                pe.matmul(ps[0:S, 6 + t % 2, :], sel[:, t], summ, start=True, stop=True).then_inc(q.bc_mm, 1)

            def transposes(n, t):
                pe.wait_ge(q.h_ready, n * B + t + 1)
                for k in range(KD):
                    ins = pe.transpose(ps[:, 6 + t % 2, k * S:(k + 1) * S], z[:, t, k * P:(k + 1) * P], ident[0:S, 0:S])
                ins.then_inc(q.tr_mm, 1)

            def routed(t):
                if t < B:
                    if t >= 2:
                        pe.wait_ge(q.lg_ev, t - 1)
                    transposes(0, t)
                if t >= 1:
                    u = t - 1
                    pe.wait_ge(q.tr_ev, u + 1)
                    for k in range(KD):
                        ins = pe.matmul(ps[0:S, 6 + u % 2, 448:448 + E0], hT[:, k, u * S:(u + 1) * S],
                                        rw0[:, k * E0:(k + 1) * E0], start=(k == 0), stop=(k == KD - 1))
                    ins.then_inc(q.lg_mm, 1)

            def ranks(n, v, E):
                pe.wait_ge(q.ready_m, n + 1)
                mm = v["m"].rearrange("p (b e) -> p b e", b=B)
                pe.matmul(ps[0:S, 6, 0:B * E], tri, v["m"], start=True, stop=False)
                for t in range(B - 1):
                    ins = pe.matmul(ps[0:S, 6, (t + 1) * E:B * E].rearrange("p (b e) -> p b e", e=E), ones_b[:, 0:S],
                                    mm[:, t:t + 1].to_broadcast([S, B - 1 - t, E]), start=False, stop=(t == B - 2))
                for t in range(B):
                    ins = pe.matmul(ps[:, 7, 0:E], ones_b, mm[:, t], start=(t == 0), stop=(t == B - 1))
                ins.then_inc(q.rank_mm, 1)

            def token_list(n, v, pairs, NB):
                pe.wait_ge(q.ready_r, n + 1)
                for c in range(pairs):
                    ins = pe.matmul(ps[:, 6, 0:2 * NB], v["rm"][:, c], v["q2"][:, c].rearrange("p a j -> p (a j)"),
                                    start=(c == 0), stop=(c == pairs - 1))
                ins.then_inc(q.list_mm, 1)

            pe.wait_ge(q.ld_kv, 48)
            kv(0, {1: lambda: pe.wait_ge(q.ld_wfc, 16)})
            pe.wait_ge(q.ld_ctx1, 16)
            kv(1, {3: summary_in, 6: summary_out,
                   **{7 + i: lambda i=i: [spread(t) for t in (2 * i, 2 * i + 1)] for i in range(B // 2)}})
            pe.wait_ge(q.ld_ctx, 16 * (B - 2))
            kv_split(2)
            kv_split(3, {t: lambda t=t: (t == 0 and pe.wait_ge(q.ld_small, 48), routed(t)) for t in range(B + 1)})
            kv_split(4, {4: lambda: (pe.wait_ge(q.ld_cst, 64), ranks(0, disp0, E0))})
            landed = (q.x0_landed, q.x1_landed)

            def blk_t(j, par, i):
                pe.wait_ge(landed[par], i * 16 + 16)
                if not isinstance(j, int) or j >= 2:
                    pe.wait_ge(q.t_ev, j - 1)
                for k in range(KD):
                    ins = pe.transpose(ps[:, par, k * P:(k + 1) * P], xg[par][:, k * P:(k + 1) * P], ident[:])
                ins.then_inc(q.t_mm, 1)

            def first_rows():
                pe.wait_ge(q.kv_ev, 5 * 11 + 7)
                blk_t(0, 0, 0)

            kv_split(5, {8: lambda: token_list(0, disp0, B * TOP, NB0), 10: first_rows})

            pe.sem_inc(q.d_mm, 1)

            def blk_up(j, par, off):
                pe.wait_ge(q.t_ev, j + 1)
                if not isinstance(j, int) or j >= 2:
                    pe.wait_ge(q.h_mul, j - 1)
                for k in range(KD):
                    ins = pe.matmul(ps[:, 2 + par, 0:2 * I0], xT[par][:, k], ring[:, bass.ds(off + k * 2 * I0, 2 * I0)],
                                    start=(k == 0), stop=(k == KD - 1))
                ins.then_inc(q.u_mm, 1)

            def blk_h(j, par):
                pe.wait_ge(q.h_mul, j + 1)
                if not isinstance(j, int) or j >= 2:
                    pe.wait_ge(q.h_ev, j - 1)
                for k in range(2):
                    ins = pe.transpose(ps[0:IH, 4 + par, k * P:(k + 1) * P], hm[par][:, k * IH:(k + 1) * IH], ident[:])
                ins.then_inc(q.h_mm, 1)

            def blk_d(j, par, off, free=None):
                pe.wait_ge(q.h_ev, j + 1)
                if free is not None:
                    pe.wait_ge(q.y_ev, free)
                elif not isinstance(j, int) or j >= 2:
                    pe.wait_ge(q.y_ev, j - 1)
                for k in range(2):
                    ins = pe.matmul(ps[:, 6 + par, :], hmT[par][:, k], ring[0:IH, bass.ds(off + GU + k * D, D)],
                                    start=(k == 0), stop=(k == 1))
                ins.then_inc(q.d_mm, 1)

            def place(j):
                return pe.value_load(table2[0:1, bass.ds(j, 1)], min_val=min(A_RING), max_val=max(A_RING))

            def step(j, par, i, h=True, d=True):
                e = pe.value_load(table[0:1, bass.ds(j, 1)], min_val=0, max_val=E0 - 1)
                off = place(j)
                pe.wait_ge(q.w_ready, e + 1)
                blk_up(j, par, off)
                if h:
                    blk_h(j - 1, 1 - par)
                blk_t(j + 1, 1 - par, i + par)
                if d:
                    blk_d(j - 2, par, place(j - 2))

            pe.wait_ge(q.list_ready, 1)
            pe.wait_ge(q.kv_ev, 11 * 6)
            step(0, 0, 0, h=False, d=False)
            step(1, 1, 0, d=False)
            step(2, 0, 1)
            step(3, 1, 1)
            last = last_pair(pe)

            def pe_pair(i):
                for par in range(2):
                    step(i * 2 + par, par, i)

            with pe.Fori(2, NPL) as i:
                pe_pair(i)
            further_pairs(pe, last, pe_pair)

            def end_t():
                pe.wait_ge(q.t_ev, last * 2 + 3)

            def end_h():
                blk_h(last * 2 + 1, 1)

            def end_d(par):
                pe.wait_ge(q.silu_done, last * 2 + 2)
                pe.wait_ge(q.h_mul, last * 2 + 2)
                blk_d(last * 2 + par, par, place(last * 2 + par), free=last * 2 + par)

            def end_e():
                pe.wait_ge(q.h_ev, last * 2 + 2)

            pe.wait_ge(q.w_back, 3)
            kv(6, {0: end_t, 1: end_h, 2: lambda: end_d(0), 3: lambda: end_d(1), 4: end_e})
            kv(7)
            pe.wait_ge(q.kv_ev, 11 * B)
            for t in range(B):
                if t >= 2:
                    pe.wait_ge(q.tr_ev, B + t - 1)
                transposes(1, t)
            pe.wait_ge(q.tr_ev, 2 * B)
            def ref_rows(t):
                pe.wait_ge(q.ref_ev, 4 if t < B // 2 else 8)
                if t >= 2:
                    pe.wait_ge(q.rt_add, t - 1)
                for k in range(KD):
                    ins = pe.transpose(ps[0:S, 4 + t % 2, k * P:(k + 1) * P], refT[:, k, t * S:(t + 1) * S], ident[:])
                ins.then_inc(q.rt_mm, 1)

            for n in range(16):
                if n >= 8:
                    ref_rows(n - 8)
                m, half = n % 4, n // 4 % 2
                if n >= 4:
                    pe.wait_ge(q.ref_ev, n - 3)
                if n == 8:
                    pe.wait_ge(q.ld_wq, 16)
                if n == 12:
                    pe.wait_ge(q.ref_ev, 8)
                w, r = (wfc, hT) if n < 8 else (wq, refT)
                for k in range(KD):
                    ins = pe.matmul(ps[:, n % 4, 0:448], w[:, k, m * P:(m + 1) * P], r[:, k, half * 448:half * 448 + 448],
                                    start=(k == 0), stop=(k == KD - 1))
                ins.then_inc(q.ref_mm, 1)

            landed_qk = (q.qk0_landed, q.qk1_landed)

            def scores(u, b2, par, n):
                if n == 0:
                    pe.wait_ge(landed_qk[par], b2 * 96 + 96)
                if not isinstance(u, int) or u >= 2:
                    pe.wait_ge(q.e_done, u - 1)
                for h in range(2):
                    g, rows = n // 2, slice(h * 2 * DG, (h + 1) * 2 * DG)
                    ins = pe.matmul(ps[0:S, 2 * (n % 2) + h, 0:T], qb[par][rows, g, n % 2], kb[par][rows, g],
                                    start=True, stop=True)
                ins.then_inc(q.s_mm, 1)

            def turn_probs(u, n):
                pe.wait_ge(q.e_done, u + 1)
                if not isinstance(u, int) or u >= 1:
                    pe.wait_ge(q.pt_ev, u)
                    pe.wait_ge(q.pt2_ev, u)
                for i in range(6):
                    c, h = i // 2, i % 2
                    ins = pe.transpose(ps[0:TC, 4 + i // 3, (i % 3) * S:(i % 3 + 1) * S],
                                       prob[n % 2][:, h, c * TC:(c + 1) * TC], ident[0:S, 0:S])
                ins.then_inc(q.pt_mm, 1)

            def weigh(u, grp, par, n):
                pe.wait_ge(q.pt_ev, u + 1)
                pe.wait_ge(q.pt2_ev, u + 1)
                if n % 2 == 0:
                    pe.wait_ge(q.o_done, grp + 1)
                bank = 6 + n // 2 % 2
                for h in range(2):
                    lo = (n % 2 + 2 * h) * DG
                    hd = n // 2 * 4 + n % 2 + 2 * h
                    for c in range(3):
                        ins = pe.matmul(ps[lo:lo + DG, bank, 0:S], vb[par][:, c, hd * DG:(hd + 1) * DG],
                                        pT[:, 2 * c + h], start=(c == 0), stop=(c == 2))
                ins.then_inc(q.pv_mm, 1)

            def turn_out(grp, n):
                pe.wait_ge(q.o_ev, grp + 1)
                pe.transpose(ps[0:S, 6 + n // 2 % 2, P:2 * P], oT, ident[:]).then_inc(q.f_mm, 1)

            def turn_rows(b):
                pe.wait_ge(q.h_ready, b + (2 * B + 1))
                for k in range(KD):
                    ins = pe.transpose(ps[:, 7, k * S:(k + 1) * S], z1[:, k * P:(k + 1) * P], ident[0:S, 0:S])
                ins.then_inc(q.tr_mm, 1)

            def router_rows(b):
                pe.wait_ge(q.tr_ev, b + (2 * B + 1))
                for k in range(KD):
                    ins = pe.matmul(ps[0:S, 6, 448:448 + E1], hT1[:, k], rw1[:, k * E1:(k + 1) * E1],
                                    start=(k == 0), stop=(k == KD - 1))
                ins.then_inc(q.lg_mm, 1)

            def att_pair(i, last=False):
                for par in range(2):
                    for n in range(UB):
                        u = i * (2 * UB) + (par * UB + n)
                        grp = i * (2 * GB) + (par * GB + n // 2)
                        over = last and par == 1
                        b = i * 2 + par
                        route = not (isinstance(i, int) and i == 0 and par == 0)
                        if n + 2 < UB:
                            scores(u + 2, i, par, n + 2)
                        elif not over:
                            scores(u + 2, i + par, 1 - par, n + 2 - UB)
                        if route and n == 0:
                            pe.wait_ge(q.lg_ev, b + (B - 1))
                        if route and n == 6:
                            pe.wait_ge(q.tr_ev, b + 2 * B)
                        weigh(u, grp, par, n)
                        if not (over and n == UB - 1):
                            turn_probs(u + 1, (n + 1) % UB)
                        if route and n in (4, 6):
                            pe.wait_ge(q.o_done, grp + 2)
                            (turn_rows if n == 4 else router_rows)(b - 1)
                        if n % 2:
                            turn_out(grp, n)

            pe.wait_ge(q.ref_ev, 16)
            pe.sem_inc(q.o_done, 2)
            scores(0, 0, 0, 0)
            scores(1, 0, 0, 1)
            pe.wait_ge(q.rt_add, B)
            turn_probs(0, 0)
            att_pair(0)
            with pe.Fori(1, B // 2 - 1) as i:
                att_pair(i)
            att_pair(B // 2 - 1, last=True)

            pe.wait_ge(q.o_done, GB * B + 2)
            turn_rows(B - 1)
            pe.wait_ge(q.lg_ev, 2 * B - 1)
            router_rows(B - 1)
            ranks(1, disp1, E1)
            token_list(1, disp1, B, NB1)
            pe.wait_ge(q.list_ready, 2)

            def block_rows(j):
                pe.wait_ge((q.gath0, q.gath1, q.gath2, q.gath3, q.gath4, q.gath5, q.gath6, q.gath7)[j],
                           16 * (B * TOP // 8 + 1))
                if j >= 2:
                    pe.wait_ge(q.t1_ev, j - 1)
                for k in range(KD):
                    ins = pe.transpose(ps[:, 6 + j % 2, k * P:(k + 1) * P], xg1[j][:, k * P:(k + 1) * P], ident[:])
                ins.then_inc(q.t1_mm, 1)

            places = []

            def products(out, steps, rows, off, width, done):
                for k in range(steps):
                    hi, lo = rows(k)
                    whi = wp1[:, bass.ds(off + k * width, width)]
                    wlo = wp1[:, bass.ds(off + (RW1 + k * width), width)]
                    pe.matmul(out, hi, whi, start=(k == 0), stop=False)
                    pe.matmul(out, hi, wlo, start=False, stop=False)
                    ins = pe.matmul(out, lo, whi, start=False, stop=(k == steps - 1))
                ins.then_inc(done, 1)

            def up1(s, c, j):
                if j == 0:
                    pe.wait_ge(q.wlo_ready, c * PIECES + PIECES)
                if not isinstance(s, int) or s >= 2:
                    pe.wait_ge(q.l_done, s - 1)
                off = places[j] * (RW1 // E1) + c % 2 * (2 * RW1)
                products(ps[:, j % 2, 0:CH], KD, lambda k: (xh1[:, j, k], xl1[:, j, k]), off, CH, q.u1_mm)

            def turn1(s, j):
                pe.wait_ge(q.l_done, s + 1)
                if not isinstance(s, int) or s >= 2:
                    pe.wait_ge(q.h1_ev, s - 1)
                for k in range(HK):
                    ins = pe.transpose(ps[:, 2 + j % 2, k * P:(k + 1) * P], lk[j % 2][:, k * P:(k + 1) * P], ident[:])
                ins.then_inc(q.h1_mm, 1)

            def down1(s, c, j):
                pe.wait_ge(q.alo_ready, s + 1)
                if not isinstance(s, int) or s >= 2:
                    pe.wait_ge(q.y1_ev, s - 1)
                off = places[j] * (RW1 // E1) + (c % 2 * (2 * RW1) + KD * CH)
                products(ps[:, 4 + j % 2, :], HK, lambda k: (ah1[j % 2][:, k * P:(k + 1) * P],
                                                             al1[j % 2][:, k * P:(k + 1) * P]), off, D, q.d1_mm)

            def chunk_steps(c, first=False):
                for j in range(NB1):
                    s = c * NB1 + j
                    if first:
                        pe.wait_ge(q.t1_ev, j + 1)
                        places.append(pe.value_load(table[0:1, j:j + 1], min_val=0, max_val=E1 - 1))
                    up1(s, c, j)
                    if first and j + 2 < NB1:
                        block_rows(j + 2)
                    if not first or j >= 1:
                        turn1(s - 1, (j - 1) % NB1)
                    if not first or j >= 2:
                        down1(s - 2, c if j >= 2 else c - 1, (j - 2) % NB1)

            block_rows(0)
            block_rows(1)
            chunk_steps(0, first=True)
            with pe.Fori(1, NCH) as c:
                chunk_steps(c)
            s = NCH * NB1
            turn1(s - 1, NB1 - 1)
            down1(s - 2, NCH - 1, NB1 - 2)
            down1(s - 1, NCH - 1, NB1 - 1)

        @block.vector
        def _(dve):
            count = [0]

            def chain(ins):
                count[0] += 1
                ins.then_inc(q.dve_done, 1)
                dve.wait_ge(q.dve_done, count[0])

            def layer_stats(rows):
                for t in range(B):
                    ins = dve.bn_stats(stats[:, t], rows[:, t])
                chain(ins)
                for t in range(B):
                    ins = dve.bn_aggr(mv[:, t], stats[:, t])
                chain(ins)
                dve.tensor_scalar(veps[:], mv[:, :, 1], EPS, None, ALU.add).then_inc(q.veps_ready, 1)

            def normalize(n, rows, s):
                dve.wait_ge(q.rstd_ready, n + 1)
                for t in range(B):
                    dve.tensor_scalar(z[:, t], rows[:, t], mv[:, t, 0:1], rstd[:, t:t + 1], ALU.subtract, ALU.mult
                                      ).then_inc(s, 1)

            dve.wait_ge(q.ld_kv, 48)
            chain(dve.memset(ones_row, 1.0))
            dve.wait_ge(q.gates_ready, 2)
            chain(dve.tensor_scalar(k_row, ones_row, gates[:, 4:5], None, ALU.mult))
            chain(dve.tensor_tensor_scan(r_row, k_row, ones_row, 0.0, ALU.mult, ALU.add))
            chain(dve.tensor_reduce(gates[:, 5:6], r_row, AX.X, ALU.add))
            dve.tensor_scalar(bq[:], cols[:, C_BQ:C_BQ + KD], SCALE, None, ALU.mult).then_inc(q.bq_ready, 1)
            chain(dve.tensor_scalar(bC[:], cols[:, C_BIN:C_BIN + KD], gates[:, 5:6], None, ALU.mult))

            def decayed(b):
                for k in range(KD):
                    n = b * KD + k
                    if n >= 2:
                        dve.wait_ge(q.u_done, n - 1)
                    dve.tensor_tensor_reduce(prod_rows[n % 2], ctx_rows[:, b, k], r_row, 1.0, 0.0, ALU.mult, ALU.add,
                                             uT[:, k, b:b + 1]).then_inc(q.u_done, 1)
            decayed(0)
            dve.wait_ge(q.ld_ctx1, 16)
            decayed(1)
            dve.wait_ge(q.ld_ctx, 16 * (B - 2))
            for b in range(2, B):
                decayed(b)
            dve.wait_ge(q.ld_x, 16)
            layer_stats(x)
            normalize(0, x, q.z_ready)
            dve.wait_ge(q.ld_sum, 96)
            chain(dve.tensor_scalar(gamma, gamma, gx0, None, ALU.mult))
            dve.tensor_scalar(beta, beta, gx0, None, ALU.mult).then_inc(q.beta_ready, 1)
            dve.wait_ge(q.s1_mm, 1)
            dve.tensor_tensor(s1T[:], ps[:, 6, 0:KD * B].rearrange("p (k b) -> p k b", k=KD),
                              bC[:].rearrange("p (k o) -> p k o", o=1).to_broadcast([P, KD, B]), ALU.add
                              ).then_inc(q.s1_ready, 1)
            dve.wait_ge(q.sum_mm, 1)
            dve.wait_ge(q.summ_zeroed, 1)
            dve.scalar_tensor_tensor(out=summ[0:B], in0=ps[0:B, 7, :], scalar=1.0 / T, in1=bout, op0=ALU.mult, op1=ALU.add
                                     ).then_inc(q.sum_ready, 1)
            for t in range(B):
                dve.wait_ge(q.bc_mm, t + 1)
                dve.wait_ge(q.z_ready, t + 1)
                dve.tensor_tensor(z[:, t], z[:, t], ps[0:S, 6 + t % 2, :], ALU.add).then_inc(q.y_added, 1)
            dve.wait_ge(q.y_added, B)
            layer_stats(z)
            dve.wait_ge(q.rstd_ready, 2)
            dve.wait_ge(q.x_based, B)
            for t in range(B):
                ins = dve.scalar_tensor_tensor(out=z[:, t], in0=z[:, t], scalar=mv[:, t, 0:1], in1=gamma,
                                               op0=ALU.subtract, op1=ALU.mult)
            chain(ins)
            for t in range(B):
                ins = dve.scalar_tensor_tensor(out=x[:, t], in0=z[:, t], scalar=rstd[:, t:t + 1], in1=x[:, t],
                                               op0=ALU.mult, op1=ALU.add)
            chain(ins)
            layer_stats(x)
            normalize(2, x, q.h_ready)

            def turned(n, t):
                dve.wait_ge(q.tr_mm, n * B + t + 1)
                dve.tensor_copy(hT[:, :, t * S:(t + 1) * S],
                                ps[:, 6 + t % 2, 0:KD * S].rearrange("p (k s) -> p k s", k=KD)).then_inc(q.tr_ev, 1)

            def logits(n, m, E, lg):
                for t in range(B + 1):
                    if t < B:
                        turned(n, t)
                    if t >= 1:
                        u = t - 1
                        dve.wait_ge(q.lg_mm, m * B + u + 1)
                        dve.tensor_copy(lg[:, u], ps[0:S, 6 + u % 2, 448:448 + E]).then_inc(q.lg_ev, 1)
                dve.wait_ge(q.lg_ev, (m + 1) * B)

            def sort(n, v, E, C, NB, meanwhile=None):
                pairs = B * C
                oh = v["oh"].rearrange("p (c e) -> p c e", e=E)
                dve.wait_ge(q.rank_mm, n + 1)
                chain(dve.tensor_scalar(v["cnti"], ps[:, 7, 0:E], float(P - 1), None, ALU.add))
                chain(dve.memset(v["ones"], 1.0))
                chain(dve.tensor_scalar(v["cnti"], v["cnti"], 7, None, ALU.logical_shift_right))
                chain(dve.tensor_copy(v["nb"], v["cnti"]))
                if n == 0:
                    chain(dve.tensor_scalar(v["nb"], v["nb"], 1.0, None, ALU.max))
                chain(dve.tensor_tensor_scan(v["cum"], v["ones"], v["nb"], 0.0, ALU.mult, ALU.add))
                chain(dve.tensor_tensor(v["base"], v["cum"], v["nb"], ALU.subtract))
                chain(dve.tensor_scalar(v["base"], v["base"], float(P), None, ALU.mult))
                slot = v["slot"].rearrange("p (b e) -> p b e", b=B)
                chain(dve.tensor_tensor(slot, ps[0:S, 6, 0:B * E].rearrange("p (b e) -> p b e", b=B),
                                        v["base"][0:S].rearrange("p (o e) -> p o e", o=1).to_broadcast([S, B, E]),
                                        ALU.add))
                pick = v["pick"].rearrange("p (b k e) -> p b k e", b=B, k=C)
                chain(dve.tensor_tensor(pick, oh.rearrange("p (b k) e -> p b k e", b=B),
                                        slot.rearrange("p b (o e) -> p b o e", o=1).to_broadcast([S, B, C, E]),
                                        ALU.mult))
                chain(dve.tensor_reduce(v["sk"], v["pick"].rearrange("p (c e) -> p c e", e=E), AX.X, ALU.add))
                dve.tensor_copy(slot_u[:, 0:pairs], v["sk"])
                chain(dve.tensor_copy(v["ski"], v["sk"]))
                dve.tensor_scalar(v["qi"], v["ski"], 7, None, ALU.logical_shift_right)
                chain(dve.tensor_scalar(v["ri"], v["ski"], P - 1, None, ALU.bitwise_and))
                dve.tensor_copy(v["qf"], v["qi"])
                chain(dve.tensor_copy(v["rf"], v["ri"]))
                cum0 = v["cum"][0:1].rearrange("p (o e) -> p o e", o=1).to_broadcast([1, NB, E])
                j0 = iota[0:1, 0:NB].rearrange("p (j o) -> p j o", o=1).to_broadcast([1, NB, E])
                chain(dve.tensor_tensor(v["cmp"], cum0, j0, ALU.is_le))
                chain(dve.tensor_reduce(v["eb"][0:1], v["cmp"], AX.X, ALU.add))
                chain(dve.tensor_scalar(v["eb"][0:1], v["eb"][0:1], float(E - 1), None, ALU.min))
                chain(dve.tensor_copy(table[0:1, 0:NB], v["eb"][0:1]))
                if n == 0:
                    chain(dve.tensor_scalar(table[0:1, T_DONE:T_DONE + E], v["cum"][0:1], 1.0, None, ALU.add))
                    last = table[0:1, T_LAST:T_LAST + 1]
                    chain(dve.tensor_scalar(last, table[0:1, T_DONE + E - 1:T_DONE + E], 1, None,
                                            ALU.logical_shift_right))
                    chain(dve.tensor_scalar(last, last, 1.0, None, ALU.subtract))
                    t0i = v["la"][0:1].bitcast(I32)
                    chain(dve.tensor_scalar(t0i, table[0:1, 0:NB], NR0 - 1, None, ALU.bitwise_and))
                    chain(dve.tensor_copy(v["eb"][0:1], t0i))
                    t0 = v["la"][0:1]
                    chain(dve.tensor_scalar(t0, v["eb"][0:1], 0.0, float(A_RING[0]), ALU.is_equal, ALU.mult))
                    for r in range(1, NR0):
                        chain(dve.tensor_scalar(v["slot"][0:1, 0:NB], v["eb"][0:1], float(r), float(A_RING[r]),
                                                ALU.is_equal, ALU.mult))
                        chain(dve.tensor_tensor(t0, t0, v["slot"][0:1, 0:NB], ALU.add))
                    chain(dve.tensor_copy(table2[0:1, 0:NB], t0))
                rf = v["rf"].rearrange("p (c o) -> p c o", o=1)
                qf = v["qf"].rearrange("p (c o) -> p c o", o=1)
                io = iota[0:S].rearrange("p (o r) -> p o r", o=1)
                dve.tensor_tensor(v["rm"], io.to_broadcast([S, pairs, P]), rf.to_broadcast([S, pairs, P]), ALU.is_equal)
                chain(dve.tensor_tensor(v["qm"], io[:, :, 0:NB].to_broadcast([S, pairs, NB]),
                                        qf.to_broadcast([S, pairs, NB]), ALU.is_equal))
                tn = tile_no.rearrange("p (c o) -> p c o", o=1 if C == TOP else TOP)[:, :, 0:1]
                dve.tensor_tensor(v["q2"][:, :, 0], v["qm"], tn.to_broadcast([S, pairs, NB]), ALU.mult)
                dve.tensor_scalar(v["q2"][:, :, 1], v["qm"], cols[0:S, C_PID:C_PID + 1], None, ALU.mult
                                  ).then_inc(q.ready_r, 1)
                if meanwhile:
                    meanwhile()
                dve.wait_ge(q.list_mm, n + 1)
                chain(dve.tensor_scalar(v["la"], ps[:, 6, 0:NB], float(S), None, ALU.mult))
                dve.tensor_tensor(lidx[:, 0:NB], v["la"], ps[:, 6, NB:2 * NB], ALU.add).then_inc(q.list_ready, 1)

            dve.memset(lidx[:, NB0:NB0 + 2], 0)
            v = disp0
            dve.wait_ge(q.filled, FILLS)
            logits(0, 0, E0, lg0)
            dve.wait_ge(q.h_stored, 16 * B)
            for t in range(B):
                ins = dve.max(v["m8"][:, t], lg0[:, t])
            chain(ins)
            for t in range(B):
                ins = dve.max_index(v["i8"][:, t], v["m8"][:, t], lg0[:, t])
            chain(ins)
            dve.tensor_copy(v["idf"].rearrange("p (b k) -> p b k", b=B), v["i8"][:, :, 0:TOP])
            chain(dve.tensor_copy(v["sk"][:, 0:B].rearrange("p (b o) -> p b o", o=1), v["m8"][:, :, 0:1]))
            dve.tensor_tensor(v["m8"][:, :, 0:TOP], v["m8"][:, :, 0:TOP],
                              v["sk"][:, 0:B].rearrange("p (b o) -> p b o", o=1).to_broadcast([S, B, TOP]),
                              ALU.subtract).then_inc(q.ediff_ready, 1)
            dve.wait_ge(q.ld_cst, 64)
            oh = v["oh"].rearrange("p (c e) -> p c e", e=E0)
            chain(dve.tensor_tensor(oh, iota[0:S, 0:E0].rearrange("p (o e) -> p o e", o=1).to_broadcast([S, B * TOP, E0]),
                                    v["idf"].rearrange("p (c o) -> p c o", o=1).to_broadcast([S, B * TOP, E0]),
                                    ALU.is_equal))
            chain(dve.tensor_reduce(v["slot"].rearrange("p (b e) -> p b e", b=B),
                                    v["oh"].rearrange("p (b k e) -> p b e k", b=B, k=TOP), AX.X, ALU.add))
            dve.tensor_copy(v["m"], v["slot"]).then_inc(q.ready_m, 1)

            def weight_back(i, done):
                dve.wait_ge(q.kv_mm, max(SPLIT) * 11 + done)
                dve.tensor_tensor(w_f32[i], w_lo[i], w_hi[i], ALU.add).then_inc(q.w_back, 1)

            def choice_weights():
                weight_back(0, KD)
                dve.wait_ge(q.eexp_ready, 1)
                wt3 = wt[:].rearrange("p (b k) -> p b k", b=B)
                chain(dve.tensor_reduce(veps[:], wt3, AX.X, ALU.add))
                chain(dve.reciprocal(veps[:], veps[:]))
                chain(dve.tensor_scalar(veps[:], veps[:], gf0, None, ALU.mult))
                chain(dve.tensor_tensor(wt3, wt3, veps[:].rearrange("p (b o) -> p b o", o=1).to_broadcast([S, B, TOP]),
                                        ALU.mult))

            sort(0, v, E0, TOP, NB0, meanwhile=choice_weights)

            def t_ev(j, par):
                dve.wait_ge(q.t_mm, j + 1)
                dve.tensor_copy(xT[par].rearrange("p k n -> p (k n)"), ps[:, par, :]).then_inc(q.t_ev, 1)

            def mul(j, par):
                dve.wait_ge(q.silu_done, j + 1)
                dve.tensor_tensor(hm[par], sg[par], ps[:, 2 + par, I0:2 * I0], ALU.mult).then_inc(q.h_mul, 1)

            def h_ev(j, par):
                dve.wait_ge(q.h_mm, j + 1)
                dve.tensor_copy(hmT[par].rearrange("p k n -> p (k n)"), ps[0:IH, 4 + par, 0:2 * P]).then_inc(q.h_ev, 1)

            weight_back(1, 2 * KD)
            t_ev(0, 0)
            t_ev(1, 1)
            mul(0, 0)
            weight_back(2, 11)
            h_ev(0, 0)
            mul(1, 1)
            t_ev(2, 0)

            def dve_pair(i):
                for par in range(2):
                    j = i * 2 + par
                    h_ev(j - 1, 1 - par)
                    mul(j, par)
                    t_ev(j + 1, 1 - par)

            last = last_pair(dve)
            with dve.Fori(1, NPL) as i:
                dve_pair(i)
            further_pairs(dve, last, dve_pair)
            h_ev(last * 2 + 1, 1)

            gath = [q.gath0, q.gath1, q.gath2, q.gath3, q.gath4, q.gath5, q.gath6, q.gath7]
            for k in range(B * TOP):
                t = k // TOP
                dve.wait_ge(gath[k % 8], 16 * (k // 8 + 1))
                if k % TOP:
                    dve.wait_ge(q.comb_done, k)
                dve.scalar_tensor_tensor(out=x[:, t], in0=g0[k % 8], scalar=wt[:, k:k + 1], in1=x[:, t],
                                         op0=ALU.mult, op1=ALU.add).then_inc(q.comb_done, 1)
            dve.wait_ge(q.comb_done, B * TOP)
            layer_stats(x)
            dve.wait_ge(q.rstd_ready, 4)
            for t in range(B):
                dve.tensor_scalar(z[:, t], x[:, t], mv[:, t, 0:1], rstd[:, t:t + 1], ALU.subtract, ALU.mult
                                  ).then_inc(q.h_ready, 1)
            dve.wait_ge(q.ld_bv, 16)
            dve.tensor_scalar(bv, bv, gx1, None, ALU.mult).then_inc(q.bv_ready, 1)
            for t in range(B):
                turned(1, t)
            dve.wait_ge(q.x_based, 2 * B)
            for t in range(B):
                dve.wait_ge(q.rt_mm, t + 1)
                dve.scalar_tensor_tensor(out=x[:, t], in0=ps[0:S, 4 + t % 2, :], scalar=gx1, in1=x[:, t],
                                         op0=ALU.mult, op1=ALU.add).then_inc(q.rt_add, 1)
            dve.wait_ge(q.rt_add, B)

            base = count[0]

            def row_max(u, par):
                dve.wait_ge(q.s_mm, u + 1)
                dve.tensor_reduce(nmx[:, par], ps[0:S, 2 * par:2 * par + 2, 0:T], AX.X, ALU.max, negate=True
                                  ).then_inc(q.mx_ready, 1)

            def probs_out(u):
                dve.wait_ge(q.pt_mm, u + 1)
                dve.tensor_copy(pT[:, 0:3].rearrange("p i s -> p (i s)"), ps[0:TC, 4, 0:3 * S]).then_inc(q.pt_ev, 1)

            def out_add(grp, b, m):
                par = m // 2 % 2
                dve.reciprocal(rinv[:, par], psum_e[:, par]).then_inc(q.dve_done, 1)
                dve.wait_ge(q.dve_done, grp + (base + 1))
                dve.wait_ge(q.f_mm, grp + 1)
                for h in range(4):
                    lo = (m // 2 * 4 + h) * DG
                    xs = x[:, bass.ds(b, 1), lo:lo + DG].rearrange("p b d -> p (b d)")
                    ins = dve.scalar_tensor_tensor(out=xs, in0=ps[0:S, 6 + par, P + h * DG:P + (h + 1) * DG],
                                                   scalar=rinv[:, par, h:h + 1], in1=xs, op0=ALU.mult, op1=ALU.add)
                ins.then_inc(q.o_done, 1)

            def row_stats(b):
                dve.wait_ge(q.o_done, b * GB + (GB + 2))
                xb = x[:, bass.ds(b, 1)].rearrange("p b d -> p (b d)")
                dve.bn_stats(stats[:, 0], xb).then_inc(q.ln_done, 1)

            def row_var(b):
                dve.wait_ge(q.ln_done, b * 2 + 1)
                dve.sem_inc(q.dve_seen, 1)
                dve.bn_aggr(mv[:, 0], stats[:, 0]).then_inc(q.ln_done, 1)
                dve.wait_ge(q.ln_done, b * 2 + 2)
                dve.tensor_scalar(veps[:, 0:1], mv[:, 0, 1:2], EPS, None, ALU.add).then_inc(q.veps_ready, 1)

            def row_norm(b):
                dve.wait_ge(q.rstd_ready, b + 5)
                dve.wait_ge(q.h_stored, b * 16 + 16 * B)
                dve.wait_ge(q.tr_mm, b + 2 * B)
                xb = x[:, bass.ds(b, 1)].rearrange("p b d -> p (b d)")
                dve.tensor_scalar(z1, xb, mv[:, 0, 0:1], rstd[:, 0:1], ALU.subtract, ALU.mult).then_inc(q.h_ready, 1)

            def row_logits(b):
                dve.wait_ge(q.lg_mm, b + (B + 1))
                dve.tensor_copy(lg1[:, bass.ds(b, 1)].rearrange("p b e -> p (b e)"), ps[0:S, 6, 448:448 + E1]
                                ).then_inc(q.lg_ev, 1)

            def att_batch(b, last=False, route=True):
                steps = {0: row_stats, 1: row_var, 3: row_norm, 7: row_logits} if route else {}
                for m in range(UB):
                    u = b * UB + m
                    if not (last and m >= UB - 2):
                        row_max(u + 2, m % 2)
                    if not (last and m == UB - 1):
                        probs_out(u + 1)
                    if m in steps:
                        steps[m](b - 1)
                    if m % 2:
                        out_add(b * GB + m // 2, b, m)

            row_max(0, 0)
            row_max(1, 1)
            probs_out(0)
            att_batch(0, route=False)
            with dve.Fori(1, B - 1) as b:
                att_batch(b)
            att_batch(B - 1, last=True)
            count[0] = base + GB * B

            for step in (row_stats, row_var, row_norm, row_logits):
                step(B - 1)
            dve.wait_ge(q.lg_ev, 2 * B)
            v = disp1
            diff = v["sk"].rearrange("p (b o) -> p b o", o=1)
            chain(dve.tensor_tensor(diff, lg1[:, :, 1:2], lg1[:, :, 0:1], ALU.subtract))
            oh = v["oh"].rearrange("p (b e) -> p b e", e=E1)
            dve.tensor_scalar(oh[:, :, 1:2], diff, 0.0, None, ALU.is_gt)
            dve.tensor_scalar(oh[:, :, 0:1], diff, 0.0, None, ALU.is_le)
            m1 = v["m"].rearrange("p (b e) -> p b e", e=E1)
            dve.tensor_scalar(m1[:, :, 1:2], diff, 0.0, None, ALU.is_gt)
            dve.tensor_scalar(m1[:, :, 0:1], diff, 0.0, None, ALU.is_le).then_inc(q.ready_m, 1)
            chain(dve.tensor_scalar(v["rf"], v["sk"], -1.0, None, ALU.mult))
            m8 = v["m8"][:, :, 0:1]
            dve.tensor_tensor(m8, diff, v["rf"].rearrange("p (b o) -> p b o", o=1), ALU.min).then_inc(q.ediff_ready, 1)
            dve.wait_ge(q.eexp_ready, 2)
            w1 = wt[:, 0:B]
            chain(dve.tensor_scalar(w1, w1, 1.0, None, ALU.add))
            chain(dve.reciprocal(w1, w1))
            chain(dve.tensor_scalar(w1, w1, gf1, None, ALU.mult))
            sort(1, v, E1, 1, NB1)

            def rows_out(j):
                dve.wait_ge(q.t1_mm, j + 1)
                dve.wait_ge(q.xhi_ready, j + 1)
                dve.tensor_tensor(xl1[:, j].rearrange("p k n -> p (k n)"), ps[:, 6 + j % 2, :],
                                  xh1[:, j].rearrange("p k n -> p (k n)"), ALU.subtract).then_inc(q.t1_ev, 1)

            def leak(s, par):
                dve.wait_ge(q.half_done, s + 1)
                dve.tensor_tensor(lk[par], hf[par], ps[:, par, 0:CH], ALU.max).then_inc(q.l_done, 1)

            def act_rest(s, par):
                dve.wait_ge(q.ahi_ready, s + 1)
                dve.tensor_tensor(al1[par], act1[par], ah1[par], ALU.subtract).then_inc(q.alo_ready, 1)

            def y_acc(s, j, first):
                dve.wait_ge(q.d1_mm, s + 1)
                if first:
                    dve.tensor_copy(y1[:, j], ps[:, 4 + j % 2, :]).then_inc(q.y1_ev, 1)
                else:
                    dve.tensor_tensor(y1[:, j], y1[:, j], ps[:, 4 + j % 2, :], ALU.add).then_inc(q.y1_ev, 1)

            rows_out(0)
            rows_out(1)
            for j in range(NB1):
                if j + 2 < NB1:
                    rows_out(j + 2)
                leak(j, j % 2)
                if j >= 1:
                    act_rest(j - 1, (j - 1) % 2)
                if j >= 2:
                    y_acc(j - 2, j - 2, True)

            def dve_chunk(c, second=False):
                for j in range(NB1):
                    leak(c * NB1 + j, j % 2)
                    act_rest(c * NB1 + (j - 1), (j - 1) % 2)
                    y_acc(c * NB1 + (j - 2), (j - 2) % NB1, second and j < 2)

            dve_chunk(1, second=True)
            with dve.Fori(2, NCH) as c:
                dve_chunk(c)
            act_rest(NCH * NB1 - 1, 1)
            y_acc(NCH * NB1 - 2, NB1 - 2, False)
            y_acc(NCH * NB1 - 1, NB1 - 1, False)
            for t in range(B):
                dve.wait_ge(gath[t], 16 * (B * TOP // 8 + 2))
                dve.scalar_tensor_tensor(out=x[:, t], in0=g1[t], scalar=wt[:, t:t + 1], in1=x[:, t],
                                         op0=ALU.mult, op1=ALU.add).then_inc(q.out_ready, 1)


def kernel(x, ctx_2048, g_xattn, g_ffn, L0_xattn_decay, L0_xattn_W_in, L0_xattn_b_in, L0_xattn_W_out,
           L0_xattn_b_out, L0_xattn_gamma, L0_xattn_beta, L0_ffn_router_w, L0_ffn_gate_w, L0_ffn_up_w,
           L0_ffn_down_w, L1_xattn_W_fc, L1_xattn_b_fc, L1_xattn_W_q, L1_xattn_b_q, L1_xattn_W_k, L1_xattn_b_k,
           L1_xattn_W_v, L1_xattn_b_v, L1_ffn_w_router, L1_ffn_w_fc, L1_ffn_w_proj):
    import ml_dtypes
    from concourse import bacc
    from concourse.bass_utils import run_bass_kernel_spmd

    def split_rows(a):
        k = a.shape[0] // P
        return a.reshape(k, P, -1).transpose(1, 0, 2).reshape(P, -1)

    def across(a, parts):
        return np.broadcast_to(np.asarray(a).reshape(1, -1), (parts, np.asarray(a).size))

    f = {n: np.asarray(a) for n, a in dict(
        x=x, ctx=ctx_2048, win=L0_xattn_W_in, wout=L0_xattn_W_out, wfc=L1_xattn_W_fc, wq=L1_xattn_W_q,
        wk=L1_xattn_W_k, wv=np.asarray(L1_xattn_W_v).reshape(D, D), r0=L0_ffn_router_w, r1=L1_ffn_w_router,
        gate=L0_ffn_gate_w, up=L0_ffn_up_w, down=L0_ffn_down_w, fc=L1_ffn_w_fc, proj=L1_ffn_w_proj).items()}
    cols = np.zeros((P, NCOL), np.float32)
    for at, b in ((C_BIN, L0_xattn_b_in), (C_BFC, L1_xattn_b_fc), (C_BQ, L1_xattn_b_q), (C_BK, L1_xattn_b_k)):
        cols[:, at:at + KD] = np.asarray(b).reshape(KD, P).T
    cols[:, C_GX:C_GX + 2] = across(g_xattn, P)
    cols[:, C_GF:C_GF + 2] = across(g_ffn, P)
    cols[:, C_DEC:C_DEC + 1] = across(L0_xattn_decay, P)
    cols[:, C_PID] = np.arange(P)
    gu = np.concatenate([f["gate"], f["up"]], axis=1)
    gu = gu.transpose(0, 2, 1).reshape(E0, KD, P, 2 * I0).transpose(0, 2, 1, 3).reshape(E0, P, GU)
    dn = f["down"].transpose(0, 2, 1).reshape(E0, 2, IH, D).transpose(0, 2, 1, 3).reshape(E0, IH, 2 * D)
    fc = f["fc"].reshape(E1, NCH, CH, KD, P).transpose(1, 4, 0, 3, 2).reshape(NCH, P, E1, KD * CH)
    pj = f["proj"].reshape(E1, D, NCH, CH // P, P).transpose(2, 4, 0, 3, 1).reshape(NCH, P, E1, KD * CH)
    ch = np.concatenate([fc, pj], axis=3).reshape(NCH, P, RW1)
    sel = np.zeros((P, B, S), np.float32)
    sel[np.arange(B), np.arange(B)] = 1
    iota = np.zeros((P, P + B * TOP), np.float32)
    iota[:, :P] = np.arange(P)
    iota[:, P:] = np.repeat(np.arange(B), TOP)
    arrays = dict(
        x=f["x"].transpose(1, 0, 2).reshape(S, B * D),
        ctx=f["ctx"][:, ::-1].transpose(0, 2, 1).reshape(B, KD, P, T).transpose(0, 2, 1, 3).reshape(B, P, KD * T),
        wfc=split_rows(f["wfc"].T), wq=split_rows(f["wq"].T), wk=split_rows(f["wk"].T), wv=split_rows(f["wv"].T),
        win=split_rows(f["win"].T), wout=split_rows(f["wout"].T), cols=cols,
        gamma=across(L0_xattn_gamma, S), beta=across(L0_xattn_beta, S), bout=across(L0_xattn_b_out, B),
        bv=across(L1_xattn_b_v, S), rw0=split_rows(f["r0"].T), rw1=split_rows(f["r1"].T), gu=gu, dn=dn, ch=ch,
        ident=np.eye(P, dtype=np.float32), sel=sel.reshape(P, B * S), iota=iota,
        tri=np.triu(np.ones((S, S)), 1).astype(ml_dtypes.bfloat16), ones=np.ones((S, P), ml_dtypes.bfloat16))
    nc = bacc.Bacc("TRN2", target_bir_lowering=False, num_devices=1)
    arrays = {"in_" + n: np.ascontiguousarray(a) for n, a in arrays.items()}
    args = [nc.dram_tensor(n, a.shape, mybir.dt.from_np(a.dtype), kind="ExternalInput").ap()
            for n, a in arrays.items()]
    out = nc.dram_tensor("out", (B, S, D), F32, kind="ExternalOutput").ap()
    build(nc, *args, out)
    r = run_bass_kernel_spmd(nc, [arrays], core_ids=[0])
    return r.results[0]["out"]
```
